# Optimizing a Trainium2 kernel written in Bass

```python
import numpy as np
import jax
import jax.numpy as jnp

def _softmax(x, axis=-1):
    return jax.nn.softmax(x, axis=axis)

def _gelu(x):
    return jax.nn.gelu(x, approximate=True)

def _silu(x):
    return jax.nn.silu(x)

def _sigmoid(x):
    return jax.nn.sigmoid(x)

def _layernorm(x, axis=-1, eps=1e-05):
    m = jnp.mean(x, axis=axis, keepdims=True)
    v = jnp.var(x, axis=axis, keepdims=True)
    return (x - m) / jnp.sqrt(v + eps)

def _scatter_add(tgt, idx, src, axis=0):
    return tgt.at[idx].add(src)

def _segment_sum(src, seg, n):
    return jax.ops.segment_sum(src, seg, n)
kernel_name = 'mk_vit_tower_d1_tok_img768_r4_5d4c5c'

def setup_inputs(seed: int=0):
    np.random.seed(seed)
    _w = jnp.asarray

    def _rec_inputs():
        import jax
        import jax.numpy as jnp
        _rk = jax.random.key(seed)
        x = -0.000505798 + 1.00042 * jax.random.normal(jax.random.fold_in(_rk, 1), (16, 3, 112, 112), jnp.float32)
        return x
    x = _rec_inputs()

    def _L0_tok_setup():
        import jax, jax.numpy as jnp
        from jax import lax
        import numpy as np
        import math
        B, C, H, W = (8, 3, 96, 96)
        P = 16
        E = 192
        VOCAB = 256

        def _conv2d(x, w, b, stride=1, pad=1):
            y = lax.conv_general_dilated(x, w, (stride, stride), [(pad, pad), (pad, pad)], dimension_numbers=('NCHW', 'OIHW', 'NCHW'))
            return y + b[None, :, None, None]

        def _group_norm(x, g, b, groups=32, eps=1e-05):
            N, Ch, Hh, Ww = x.shape
            xr = x.reshape(N, groups, Ch // groups, Hh, Ww)
            m = xr.mean(axis=(2, 3, 4), keepdims=True)
            v = xr.var(axis=(2, 3, 4), keepdims=True)
            xn = ((xr - m) / jnp.sqrt(v + eps)).reshape(N, Ch, Hh, Ww)
            return xn * g[None, :, None, None] + b[None, :, None, None]
        key = jax.random.key(seed)
        ks = jax.random.split(key, 8)
        f32 = jnp.float32
        return {'pixel_values': jax.random.normal(ks[0], (B, C, H, W), f32), 'conv1_w': jax.random.normal(ks[1], (64, C, 3, 3), f32) * 0.05, 'conv1_b': jnp.zeros((64,), f32), 'gn1_g': jnp.ones((64,), f32), 'gn1_b': jnp.zeros((64,), f32), 'rconv1_w': jax.random.normal(ks[2], (64, 64, 3, 3), f32) * 0.05, 'rconv1_b': jnp.zeros((64,), f32), 'gn2_g': jnp.ones((64,), f32), 'gn2_b': jnp.zeros((64,), f32), 'rconv2_w': jax.random.normal(ks[3], (64, 64, 3, 3), f32) * 0.05, 'rconv2_b': jnp.zeros((64,), f32), 'proj_w': jax.random.normal(ks[4], (E, 64, P, P), f32) * 0.02, 'proj_b': jnp.zeros((E,), f32), 'row_emb': jax.random.normal(ks[5], (VOCAB, E), f32) * 0.02, 'col_emb': jax.random.normal(ks[6], (VOCAB, E), f32) * 0.02}
    _L0_tok_all = _L0_tok_setup()
    _L0_tok_in = {k: v for k, v in _L0_tok_all.items() if k in ('conv1_w', 'conv1_b', 'gn1_g', 'gn1_b', 'rconv1_w', 'rconv1_b', 'gn2_g', 'gn2_b', 'rconv2_w', 'rconv2_b', 'proj_w', 'proj_b', 'row_emb', 'col_emb')}
    del _L0_tok_all

    def _L0_attn_setup():
        import jax, jax.numpy as jnp
        import numpy as np
        B, T, C, NH = (8, 256, 192, 12)
        key = jax.random.key(seed)
        k1, k2, k3 = jax.random.split(key, 3)
        x = jax.random.normal(k1, (B, T, C), dtype=jnp.float32)
        Wqkv = jax.random.normal(k2, (C, 3 * C), dtype=jnp.float32) * 0.02
        bqkv = jnp.zeros((3 * C,), dtype=jnp.float32)
        Wproj = jax.random.normal(k3, (C, C), dtype=jnp.float32) * 0.02
        bproj = jnp.zeros((C,), dtype=jnp.float32)
        return {'x': x, 'Wqkv': Wqkv, 'bqkv': bqkv, 'Wproj': Wproj, 'bproj': bproj}
    _L0_attn_all = _L0_attn_setup()
    _L0_attn_in = {k: v for k, v in _L0_attn_all.items() if k in ('Wqkv', 'bqkv', 'Wproj', 'bproj')}
    del _L0_attn_all

    def _L0_ffn_setup():
        import jax, jax.numpy as jnp
        import numpy as np
        H = 12
        ALPHA = (1, 2, 3)
        DEPTH = 5
        BLOCK_DEPTH = 3
        TOTAL_DEPTH_M1 = 14 - 1
        SMALL_ACTIVE = BLOCK_DEPTH <= DEPTH <= TOTAL_DEPTH_M1 - BLOCK_DEPTH

        def _ln(x, g, b, eps=1e-05):
            m = jnp.mean(x, axis=-1, keepdims=True)
            v = jnp.mean((x - m) ** 2, axis=-1, keepdims=True)
            return (x - m) * jax.lax.rsqrt(v + eps) * g + b

        def _attn_branch(xp, w_qkv, w_proj, b_proj, keep_heads, keep_ch):
            B2, N, C = xp.shape
            hd = C // H
            scale = hd ** (-0.5)
            qkv = (xp @ w_qkv).reshape(B2, N, 3, H, hd).transpose(2, 0, 3, 1, 4)
            hmask = (jnp.arange(H) < keep_heads).astype(xp.dtype)[None, :, None, None]
            q, k, v = (qkv[0] * hmask, qkv[1] * hmask, qkv[2] * hmask)
            a = jax.nn.softmax(jnp.einsum('bhnd,bhmd->bhnm', q, k) * scale, axis=-1)
            o = jnp.einsum('bhnm,bhmd->bhnd', a, v).transpose(0, 2, 1, 3).reshape(B2, N, C)
            o = o @ w_proj + b_proj
            cmask = (jnp.arange(C) < keep_ch).astype(xp.dtype)
            return o * cmask

        def _mlp_branch(xp, w1, b1, w2, b2, keep_ch):
            C = xp.shape[-1]
            cmask = (jnp.arange(C) < keep_ch).astype(xp.dtype)
            h = jax.nn.gelu(xp * cmask @ w1 + b1, approximate=False)
            return (h @ w2 + b2) * cmask
        key = jax.random.key(seed)
        ks = jax.random.split(key, 8)
        B, N, C = (64, 257, 192)
        HID = 4 * C

        def w(k, shape):
            return jax.random.normal(k, shape, jnp.float32) * 0.02
        return {'x': jax.random.normal(ks[0], (B, N, C), jnp.float32), 'gumbel_weights': jax.random.uniform(ks[1], (3,), jnp.float32), 'n1l_g': jnp.ones((C,), jnp.float32), 'n1l_b': jnp.zeros((C,), jnp.float32), 'n1s_g': jnp.ones((C,), jnp.float32), 'n1s_b': jnp.zeros((C,), jnp.float32), 'w_qkv': w(ks[2], (C, 3 * C)), 'w_proj': w(ks[3], (C, C)), 'b_proj': jnp.zeros((C,), jnp.float32), 'n2l_g': jnp.ones((C,), jnp.float32), 'n2l_b': jnp.zeros((C,), jnp.float32), 'n2s_g': jnp.ones((C,), jnp.float32), 'n2s_b': jnp.zeros((C,), jnp.float32), 'w_fc1': w(ks[4], (C, HID)), 'b_fc1': jnp.zeros((HID,), jnp.float32), 'w_fc2': w(ks[5], (HID, C)), 'b_fc2': jnp.zeros((C,), jnp.float32)}
    _L0_ffn_all = _L0_ffn_setup()
    _L0_ffn_in = {k: v for k, v in _L0_ffn_all.items() if k in ('gumbel_weights', 'n1l_g', 'n1l_b', 'n1s_g', 'n1s_b', 'w_qkv', 'w_proj', 'b_proj', 'n2l_g', 'n2l_b', 'n2s_g', 'n2s_b', 'w_fc1', 'b_fc1', 'w_fc2', 'b_fc2')}
    del _L0_ffn_all
    return {'x': x, 'L0_tok_conv1_w': _L0_tok_in['conv1_w'], 'L0_tok_conv1_b': _L0_tok_in['conv1_b'], 'L0_tok_gn1_g': _L0_tok_in['gn1_g'], 'L0_tok_gn1_b': _L0_tok_in['gn1_b'], 'L0_tok_rconv1_w': _L0_tok_in['rconv1_w'], 'L0_tok_rconv1_b': _L0_tok_in['rconv1_b'], 'L0_tok_gn2_g': _L0_tok_in['gn2_g'], 'L0_tok_gn2_b': _L0_tok_in['gn2_b'], 'L0_tok_rconv2_w': _L0_tok_in['rconv2_w'], 'L0_tok_rconv2_b': _L0_tok_in['rconv2_b'], 'L0_tok_proj_w': _L0_tok_in['proj_w'], 'L0_tok_proj_b': _L0_tok_in['proj_b'], 'L0_tok_row_emb': _L0_tok_in['row_emb'], 'L0_tok_col_emb': _L0_tok_in['col_emb'], 'L0_attn_Wqkv': _L0_attn_in['Wqkv'], 'L0_attn_bqkv': _L0_attn_in['bqkv'], 'L0_attn_Wproj': _L0_attn_in['Wproj'], 'L0_attn_bproj': _L0_attn_in['bproj'], 'L0_ffn_gumbel_weights': _L0_ffn_in['gumbel_weights'], 'L0_ffn_n1l_g': _L0_ffn_in['n1l_g'], 'L0_ffn_n1l_b': _L0_ffn_in['n1l_b'], 'L0_ffn_n1s_g': _L0_ffn_in['n1s_g'], 'L0_ffn_n1s_b': _L0_ffn_in['n1s_b'], 'L0_ffn_w_qkv': _L0_ffn_in['w_qkv'], 'L0_ffn_w_proj': _L0_ffn_in['w_proj'], 'L0_ffn_b_proj': _L0_ffn_in['b_proj'], 'L0_ffn_n2l_g': _L0_ffn_in['n2l_g'], 'L0_ffn_n2l_b': _L0_ffn_in['n2l_b'], 'L0_ffn_n2s_g': _L0_ffn_in['n2s_g'], 'L0_ffn_n2s_b': _L0_ffn_in['n2s_b'], 'L0_ffn_w_fc1': _L0_ffn_in['w_fc1'], 'L0_ffn_b_fc1': _L0_ffn_in['b_fc1'], 'L0_ffn_w_fc2': _L0_ffn_in['w_fc2'], 'L0_ffn_b_fc2': _L0_ffn_in['b_fc2']}

def reference(x, L0_tok_conv1_w, L0_tok_conv1_b, L0_tok_gn1_g, L0_tok_gn1_b, L0_tok_rconv1_w, L0_tok_rconv1_b, L0_tok_gn2_g, L0_tok_gn2_b, L0_tok_rconv2_w, L0_tok_rconv2_b, L0_tok_proj_w, L0_tok_proj_b, L0_tok_row_emb, L0_tok_col_emb, L0_attn_Wqkv, L0_attn_bqkv, L0_attn_Wproj, L0_attn_bproj, L0_ffn_gumbel_weights, L0_ffn_n1l_g, L0_ffn_n1l_b, L0_ffn_n1s_g, L0_ffn_n1s_b, L0_ffn_w_qkv, L0_ffn_w_proj, L0_ffn_b_proj, L0_ffn_n2l_g, L0_ffn_n2l_b, L0_ffn_n2s_g, L0_ffn_n2s_b, L0_ffn_w_fc1, L0_ffn_b_fc1, L0_ffn_w_fc2, L0_ffn_b_fc2):
    import jax
    import jax.numpy as jnp

    def _L0_tok_ref(pixel_values, conv1_w, conv1_b, gn1_g, gn1_b, rconv1_w, rconv1_b, gn2_g, gn2_b, rconv2_w, rconv2_b, proj_w, proj_b, row_emb, col_emb):
        import jax, jax.numpy as jnp
        from jax import lax
        import numpy as np
        import math
        B, C, H, W = (8, 3, 96, 96)
        P = 16
        E = 192
        VOCAB = 256

        def _conv2d(x, w, b, stride=1, pad=1):
            y = lax.conv_general_dilated(x, w, (stride, stride), [(pad, pad), (pad, pad)], dimension_numbers=('NCHW', 'OIHW', 'NCHW'))
            return y + b[None, :, None, None]

        def _group_norm(x, g, b, groups=32, eps=1e-05):
            N, Ch, Hh, Ww = x.shape
            xr = x.reshape(N, groups, Ch // groups, Hh, Ww)
            m = xr.mean(axis=(2, 3, 4), keepdims=True)
            v = xr.var(axis=(2, 3, 4), keepdims=True)
            xn = ((xr - m) / jnp.sqrt(v + eps)).reshape(N, Ch, Hh, Ww)
            return xn * g[None, :, None, None] + b[None, :, None, None]
        bsz, c, h, w = pixel_values.shape
        h0, w0 = (h // P, w // P)
        seq_len = h0 * w0
        x = pixel_values.reshape(bsz, c, h0, P, w0, P)
        x = x.transpose(0, 2, 4, 1, 3, 5).reshape(bsz * h0 * w0, c, P, P)
        mean = x.mean(axis=(-2, -1), keepdims=True)
        std = jnp.std(x, axis=(-2, -1), keepdims=True, ddof=1)
        x = (x - mean) / (1e-06 + std)
        x = x / math.sqrt(P)
        x = _conv2d(x, conv1_w, conv1_b)
        residual = x
        x = _group_norm(x, gn1_g, gn1_b)
        x = jax.nn.gelu(x, approximate=False)
        x = _conv2d(x, rconv1_w, rconv1_b)
        x = _group_norm(x, gn2_g, gn2_b)
        x = jax.nn.gelu(x, approximate=False)
        x = _conv2d(x, rconv2_w, rconv2_b)
        x = residual + x
        x = _conv2d(x, proj_w, proj_b, stride=P, pad=0)
        embeddings = x.reshape(bsz, seq_len, E)
        seq_idx = jnp.arange(seq_len)
        row_idx = seq_idx // w0
        col_idx = seq_idx % w0
        col_hi = ((col_idx + 1).astype(jnp.float32) / w0 * VOCAB).astype(jnp.int32)
        col_lo = (col_idx.astype(jnp.float32) / w0 * VOCAB).astype(jnp.int32)
        row_hi = ((row_idx + 1).astype(jnp.float32) / h0 * VOCAB).astype(jnp.int32)
        row_lo = (row_idx.astype(jnp.float32) / h0 * VOCAB).astype(jnp.int32)
        row_pos = (row_lo + row_hi) // 2
        col_pos = (col_lo + col_hi) // 2
        embeddings = embeddings + row_emb[row_pos][None] + col_emb[col_pos][None]
        return embeddings

    def _L0_attn_ref(x, Wqkv, bqkv, Wproj, bproj):
        import jax, jax.numpy as jnp
        import numpy as np
        B, T, C, NH = (8, 256, 192, 12)
        b, t, c = x.shape
        hs = c // NH
        qkv = x @ Wqkv + bqkv
        q, k, v = jnp.split(qkv, 3, axis=2)
        q = q.reshape(b, t, NH, hs).transpose(0, 2, 1, 3)
        k = k.reshape(b, t, NH, hs).transpose(0, 2, 1, 3)
        v = v.reshape(b, t, NH, hs).transpose(0, 2, 1, 3)
        att = jnp.einsum('bhqd,bhkd->bhqk', q, k) * hs ** (-0.5)
        causal = jnp.tril(jnp.ones((t, t), dtype=bool))
        att = jnp.where(causal[None, None], att, jnp.finfo(att.dtype).min)
        att = jax.nn.softmax(att, axis=-1)
        y = jnp.einsum('bhqk,bhkd->bhqd', att, v)
        y = y.transpose(0, 2, 1, 3).reshape(b, t, c)
        return y @ Wproj + bproj

    def _L0_ffn_ref(x, gumbel_weights, n1l_g, n1l_b, n1s_g, n1s_b, w_qkv, w_proj, b_proj, n2l_g, n2l_b, n2s_g, n2s_b, w_fc1, b_fc1, w_fc2, b_fc2):
        import jax, jax.numpy as jnp
        import numpy as np
        H = 12
        ALPHA = (1, 2, 3)
        DEPTH = 5
        BLOCK_DEPTH = 3
        TOTAL_DEPTH_M1 = 14 - 1
        SMALL_ACTIVE = BLOCK_DEPTH <= DEPTH <= TOTAL_DEPTH_M1 - BLOCK_DEPTH

        def _ln(x, g, b, eps=1e-05):
            m = jnp.mean(x, axis=-1, keepdims=True)
            v = jnp.mean((x - m) ** 2, axis=-1, keepdims=True)
            return (x - m) * jax.lax.rsqrt(v + eps) * g + b

        def _attn_branch(xp, w_qkv, w_proj, b_proj, keep_heads, keep_ch):
            B2, N, C = xp.shape
            hd = C // H
            scale = hd ** (-0.5)
            qkv = (xp @ w_qkv).reshape(B2, N, 3, H, hd).transpose(2, 0, 3, 1, 4)
            hmask = (jnp.arange(H) < keep_heads).astype(xp.dtype)[None, :, None, None]
            q, k, v = (qkv[0] * hmask, qkv[1] * hmask, qkv[2] * hmask)
            a = jax.nn.softmax(jnp.einsum('bhnd,bhmd->bhnm', q, k) * scale, axis=-1)
            o = jnp.einsum('bhnm,bhmd->bhnd', a, v).transpose(0, 2, 1, 3).reshape(B2, N, C)
            o = o @ w_proj + b_proj
            cmask = (jnp.arange(C) < keep_ch).astype(xp.dtype)
            return o * cmask

        def _mlp_branch(xp, w1, b1, w2, b2, keep_ch):
            C = xp.shape[-1]
            cmask = (jnp.arange(C) < keep_ch).astype(xp.dtype)
            h = jax.nn.gelu(xp * cmask @ w1 + b1, approximate=False)
            return (h @ w2 + b2) * cmask
        B, N, C = x.shape
        B2 = B // 2
        nl = _ln(x[:B2], n1l_g, n1l_b)
        ns = _ln(x[B2:], n1s_g, n1s_b)
        a_large = _attn_branch(nl, w_qkv, w_proj, b_proj, H, C)
        if SMALL_ACTIVE:
            a_small = sum((gumbel_weights[i] * _attn_branch(ns, w_qkv, w_proj, b_proj, H // ALPHA[i], C // ALPHA[i]) for i in range(3)))
            attn_out = jnp.concatenate([a_large, a_small], axis=0)
        else:
            attn_out = jnp.concatenate([a_large, a_large], axis=0)
        x = x + attn_out
        nl2 = _ln(x[:B2], n2l_g, n2l_b)
        ns2 = _ln(x[B2:], n2s_g, n2s_b)
        m_large = _mlp_branch(nl2, w_fc1, b_fc1, w_fc2, b_fc2, C)
        if SMALL_ACTIVE:
            m_small = sum((gumbel_weights[i] * _mlp_branch(ns2, w_fc1, b_fc1, w_fc2, b_fc2, C // ALPHA[i]) for i in range(3)))
            mlp_out = jnp.concatenate([m_large, m_small], axis=0)
        else:
            mlp_out = jnp.concatenate([m_large, m_large], axis=0)
        return x + mlp_out
    h = _L0_tok_ref(x, L0_tok_conv1_w, L0_tok_conv1_b, L0_tok_gn1_g, L0_tok_gn1_b, L0_tok_rconv1_w, L0_tok_rconv1_b, L0_tok_gn2_g, L0_tok_gn2_b, L0_tok_rconv2_w, L0_tok_rconv2_b, L0_tok_proj_w, L0_tok_proj_b, L0_tok_row_emb, L0_tok_col_emb)
    h = h + _L0_attn_ref(_layernorm(h, axis=-1), L0_attn_Wqkv, L0_attn_bqkv, L0_attn_Wproj, L0_attn_bproj)
    h = h + _L0_ffn_ref(_layernorm(h, axis=-1), L0_ffn_gumbel_weights, L0_ffn_n1l_g, L0_ffn_n1l_b, L0_ffn_n1s_g, L0_ffn_n1s_b, L0_ffn_w_qkv, L0_ffn_w_proj, L0_ffn_b_proj, L0_ffn_n2l_g, L0_ffn_n2l_b, L0_ffn_n2s_g, L0_ffn_n2s_b, L0_ffn_w_fc1, L0_ffn_b_fc1, L0_ffn_w_fc2, L0_ffn_b_fc2)
    return h

_drawn_inputs = setup_inputs


def setup_inputs(seed=0):
    import zlib

    import numpy as np

    out = dict(_drawn_inputs(seed))
    spreads = {'L0_tok_conv1_b': (0.0, 0.1),
     'L0_tok_gn1_g': (1.0, 0.2),
     'L0_tok_gn1_b': (0.0, 0.1),
     'L0_tok_rconv1_b': (0.0, 0.1),
     'L0_tok_gn2_g': (1.0, 0.2),
     'L0_tok_gn2_b': (0.0, 0.1),
     'L0_tok_rconv2_b': (0.0, 0.1),
     'L0_tok_proj_b': (0.0, 0.1),
     'L0_attn_bqkv': (0.0, 0.598),
     'L0_attn_bproj': (0.0, 0.1),
     'L0_ffn_n1l_g': (1.0, 0.6),
     'L0_ffn_n1l_b': (0.0, 0.8),
     'L0_ffn_n1s_g': (1.0, 0.6),
     'L0_ffn_n1s_b': (0.0, 0.8),
     'L0_ffn_b_proj': (0.0, 0.339),
     'L0_ffn_n2l_g': (1.0, 0.6),
     'L0_ffn_n2l_b': (0.0, 0.8),
     'L0_ffn_n2s_g': (1.0, 0.6),
     'L0_ffn_n2s_b': (0.0, 0.8),
     'L0_ffn_b_fc1': (0.0, 0.8),
     'L0_ffn_b_fc2': (0.0, 0.346)}
    factors = {'L0_tok_row_emb': 6.094,
     'L0_tok_col_emb': 5.982,
     'L0_attn_Wqkv': 2.671,
     'L0_ffn_gumbel_weights': 8.0,
     'L0_ffn_w_qkv': 5.047,
     'L0_ffn_w_proj': 5.202,
     'L0_ffn_w_fc1': 2.899,
     'L0_ffn_w_fc2': 2.794}
    for name, (base, spread) in spreads.items():
        noise = np.random.default_rng([zlib.crc32(name.encode()), seed]).standard_normal(out[name].shape)
        drawn = base * np.exp(spread * noise) if base else spread * noise
        out[name] = jnp.asarray(drawn.astype(out[name].dtype))
    for name, factor in factors.items():
        out[name] = (out[name] * factor).astype(out[name].dtype)
    return out
```

```python
import concourse.bass as bass
from concourse import mybir
from contextlib import ExitStack
import numpy as np

F32, F16 = mybir.dt.float32, mybir.dt.float16
ALU, ACT = mybir.AluOpType, mybir.ActivationFunctionType

B, C, P, CH, E = 16, 3, 16, 64, 192
HP = 7
ROWS = B * HP
NPAT = ROWS * HP
SL, WD = 9, 18
PAD = SL * WD
HALF = 8 * P
U = 8
Q = 4
UNITS = NPAT // U
GU = 14
GROUPS = UNITS // GU
G = GU * U
FU = E // U
RUN = (U - 1) * PAD + 7 * WD + P
PLANE = NPAT * PAD + U * PAD
KA, KC = 72, 108
WS = 64.0
EPS = 1e-5
TR = 55


class Chain:

    def __init__(self, eng, sem, base):
        self.eng, self.sem, self.at = eng, sem, base

    def did(self, ins):
        ins.then_inc(self.sem, 1)
        self.at = self.at + 1

    def wait(self):
        self.eng.wait_ge(self.sem, self.at)


def build_front(nc, a, emb, xs, ts):
    scr = nc.dram_tensor("x_planes", (12, PLANE), F16)
    with ExitStack() as ctx:
        def sb(name, shape, dt=F32):
            return ctx.enter_context(nc.sbuf_tensor("sb_" + name, shape, dt))

        def sem(name):
            return ctx.enter_context(nc.semaphore(name))

        weff = sb("weff", [128, HALF, 2, E], F16)
        arena = sb("arena", [128, 2 * G * HALF], F16)
        g2 = arena[:, :].rearrange("p (h g n) -> p h g n", h=2, g=G)
        f32b = [sb(f"f32_{i}", [128, U * PAD]) for i in range(2)]
        ghl = [sb(f"ghl_{i}", [128, 2, U * PAD], F16) for i in range(2)]
        g2f = sb("g2f", [128, U, HALF])
        im = [sb(f"im_{i}", [KC, U * PAD], F16) for i in range(2)]
        tev = [sb(f"tev_{i}", [TR, U, SL * P]) for i in range(2)]
        rws = sb("rws", [128, 2, 6, 128], F16)
        fws = sb("fws", [128, 2, 6, 128], F16)
        tws = sb("tws", [128, 2, TR], F16)
        w1hl = sb("w1hl", [KC, 2, 128], F16)
        w1s = sb("w1s", [KC, 128], F16)
        grp = sb("grp", [128, 128])
        par = sb("par", [128, 7])
        pars = sb("pars", [128, 3])
        stt6 = [sb(f"bn6_{s}", [128, U, 6]) for s in range(2)]
        ms = [sb(f"ms_{s}", [128, 2, U, 2]) for s in range(2)]
        mst = [sb(f"mst_{s}", [128, 2, U]) for s in range(2)]
        msq = [sb(f"msq_{s}", [128, U]) for s in range(2)]
        var = [sb(f"var_{s}", [128, U]) for s in range(2)]
        rst = [sb(f"rst_{s}", [128, U]) for s in range(2)]
        gsc = [sb(f"gsc_{s}", [128, U]) for s in range(2)]
        gsh = [sb(f"gsh_{s}", [128, U]) for s in range(2)]
        half_neg = sb("half_neg", [128, 21])
        half_pos = sb("half_pos", [128, 21])
        tok = sb("tok", [G, 2, E])
        x6 = sb("x6", [ROWS, 21, 6])
        xmv = sb("xmv", [ROWS, 21, 2])
        xsd = sb("xsd", [ROWS, 3, 21])
        zt = sb("zt", [12, U * PAD], F16)
        xt = arena[0:ROWS, 0:2 * C * 7 * 256].bitcast(F32).rearrange("p (c w n) -> p c w n", c=C, w=7)
        o = 2 * C * 7 * 256
        xhl = arena[0:ROWS, o:o + 12 * 7 * PAD].rearrange("p (q n) -> p q n", q=12)
        wst = weff[:, 0:12, :, :].rearrange("p a b c -> p (a b c)").bitcast(F32)
        rst32, fst32 = wst[:, 0:768], wst[:, 768:1536]
        tst32, w1st32 = wst[:, 1536:1536 + TR], wst[0:KC, 1600:1728]

        rc = [[ctx.enter_context(nc.psum_tensor(f"rc{i}{q}", [128, 512], F32)) for q in range(2)] for i in range(2)]
        c1 = [ctx.enter_context(nc.psum_tensor(f"c1_{q}", [128, 512], F32)) for q in range(2)]
        pj = ctx.enter_context(nc.psum_tensor("pj", [128, 512], F32))
        st = ctx.enter_context(nc.psum_tensor("st", [128, 512], F32))

        s_wld, s_xld, s_wprep, s_w1s = sem("weights_loaded"), sem("x_loaded"), sem("weights_prepared"), sem("w1_placed")
        s_cst, s_xvar, s_xstd, s_xz, s_xhl, s_xch = (sem("constants"), sem("x_var"), sem("x_std"), sem("x_zeroed"),
                                               sem("x_split"), sem("x_chain"))
        s_scr, s_zero = sem("x_stored"), sem("zero_tile")
        s_padz = sem("pads_zeroed")
        s_pld = [sem(f"proj_loaded{i}") for i in range(2)]
        s_psp, s_fold, s_tps = sem("proj_split"), sem("fold_done"), sem("t_done")
        s_whi, s_wlo, s_tev = sem("w_hi"), sem("w_lo"), sem("t_evacuated")
        s_ts = [sem(f"t_stored{i}") for i in range(2)]
        s_im = [sem(f"im_loaded{i}") for i in range(2)]
        s_c1, s_ms, s_st, s_rd = sem("conv1_done"), [sem("ms1"), sem("ms2")], [sem("st1"), sem("st2")], [sem("rd1"), sem("rd2")]
        s_var, s_pow, s_sh = [sem("var1"), sem("var2")], [sem("rstd1"), sem("rstd2")], [sem("aff1"), sem("aff2")]
        s_ch = [sem("chain1"), sem("chain2")]
        s_g1, s_sp1h, s_sp1, s_rc = sem("gelu1_done"), sem("split1_hi"), sem("split1_done"), sem("rconv_done")
        s_rfree, s_g2, s_sp2h, s_sp2 = sem("rconv_free"), sem("gelu2_done"), sem("split2_hi"), sem("split2_done")
        s_g2ff = sem("g2f_free")
        s_pj, s_tokc, s_pjr, s_tok, s_emb = sem("projected"), sem("tok_lo"), sem("proj_evac"), sem("tok_ready"), sem("emb_stored")

        block = ctx.enter_context(nc.Block())

        @block.sync
        def _(sp):
            sp.dma_start(xt, a["x"].rearrange("c p w n -> p c w n")).then_inc(s_xld, 16)
            sp.dma_start(par[:, :], a["params"]).then_inc(s_wld, 16)
            sp.dma_start(rst32, a["rbands"]).then_inc(s_wld, 16)
            sp.dma_start(fst32, a["fbands"]).then_inc(s_wld, 16)
            sp.dma_start(tst32, a["tband"]).then_inc(s_wld, 16)
            sp.dma_start(w1st32, a["w1band"]).then_inc(s_wld, 16)
            sp.dma_start(grp[:, :], a["grp"]).then_inc(s_wld, 16)

            def load_proj(n, p):
                sp.dma_start(f32b[p][:, :], a["proj"][:, bass.ds(n * (U * PAD), U * PAD)]).then_inc(s_pld[p], 16)

            load_proj(0, 0)
            load_proj(1, 1)
            sp.wait_ge(s_wprep, 11)
            sp.dma_start(w1s[0:KA, :], w1hl[0:KA, 0, :]).then_inc(s_w1s, 16)
            sp.dma_start(w1s[KA:KC, :], w1hl[KA:KC, 1, :]).then_inc(s_w1s, 16)
            sp.wait_ge(s_xch, 42)
            for c in range(C):
                sp.dma_start(xs.rearrange("(r w) (c n) -> r c w n", w=7, c=C)[:, c], xt[:, c]).then_inc(s_scr, 16)
            sp.wait_ge(s_xhl, 13)
            for h in range(2):
                sp.dma_start(bass.AP(tensor=scr, offset=h * 6 * PLANE, ap=[[7 * PAD, ROWS], [PLANE, 6], [1, 7 * PAD]]),
                             xhl[:, 6 * h:6 * h + 6, :]).then_inc(s_scr, 16)
            sp.wait_ge(s_zero, 1)
            sp.dma_start(bass.AP(tensor=scr, offset=NPAT * PAD, ap=[[PLANE, 12], [1, U * PAD]]), zt[:, :]).then_inc(s_scr, 16)

            def fold_io(i, p, last):
                n = 2 * i + p
                if not last:
                    sp.wait_ge(s_psp, 2 * n + 2)
                    load_proj(n + 2, p)
                sp.wait_ge(s_tev, 3 * n + 3)
                sp.dma_start(bass.AP(tensor=ts.tensor, offset=n * (U * TR * 144), ap=[[144, TR], [TR * 144, U], [1, 144]]),
                             tev[p][:, :, :]).then_inc(s_ts[p], 16)

            with sp.Fori(0, FU // 2 - 1) as i:
                for p in range(2):
                    fold_io(i, p, False)
            for p in range(2):
                fold_io(FU // 2 - 1, p, True)

            sp.wait_ge(s_scr, 16 * 6)

            def load_im(u, p):
                for kx in range(3):
                    sp.dma_start(im[p][24 * kx:24 * kx + 24, 0:RUN],
                                 bass.AP(tensor=scr, offset=u * (U * PAD) + kx,
                                         ap=[[PLANE, 12], [WD, 2], [1, RUN]])).then_inc(s_im[p], 16)
                    sp.dma_start(im[p][KA + 12 * kx:KA + 12 * kx + 12, 0:RUN],
                                 bass.AP(tensor=scr, offset=u * (U * PAD) + kx,
                                         ap=[[PLANE, 6], [WD, 2], [1, RUN]])).then_inc(s_im[p], 16)

            sp.sem_inc(s_emb, 16)
            load_im(0, 0)
            with sp.Fori(0, GROUPS) as g:
                with sp.Fori(0, GU // 2) as j:
                    for p in range(2):
                        u = g * GU + j * 2 + p
                        sp.wait_ge(s_c1, 2 * u + 1)
                        load_im(u + 1, 1 - p)
                sp.wait_ge(s_tok, g + 1)
                sp.dma_start(emb[bass.ds(g * G, G), :], tok[:, 0, :]).then_inc(s_emb, 16)
            sp.wait_ge(s_emb, 16 * GROUPS + 16)
            sp.wait_ge(s_ts[0], 16 * (FU // 2))
            sp.wait_ge(s_ts[1], 16 * (FU // 2))

        @block.gpsimd
        def _(pool):
            nc.gpsimd.memset(half_neg[:, :], -0.5).then_inc(s_cst, 1)
            nc.gpsimd.memset(half_pos[:, :], 0.5).then_inc(s_cst, 1)
            nc.gpsimd.memset(zt[:, :], 0.0).then_inc(s_zero, 1)
            nc.gpsimd.memset(xhl.bitcast(F32), 0.0).then_inc(s_xz, 1)
            pool.wait_ge(s_cst, 2)
            pool.wait_ge(s_xvar, 1)
            nc.gpsimd.tensor_tensor(xsd[:, 1, :], xsd[:, 0, :], half_pos[0:ROWS, :], ALU.pow).then_inc(s_xstd, 1)

            def rstd(s, count):
                pool.wait_ge(s_var[s], count)
                nc.gpsimd.tensor_tensor(rst[s][:, :], var[s][:, :], half_neg[:, 0:U], ALU.pow).then_inc(s_pow[s], 1)

            def step(u, first):
                rstd(0, u + 2)
                if not first:
                    rstd(1, u)

            rstd(0, 1)
            with pool.Fori(0, GROUPS) as g:
                for p in range(2):
                    step(g * GU + p, p == 0)
                with pool.Fori(1, GU // 2) as j:
                    for p in range(2):
                        step(g * GU + j * 2 + p, False)
                rstd(1, g * GU + GU)

        @block.scalar
        def _(act):
            def t_evac(n, p):
                act.wait_ge(s_tps, n + 1)
                for k, bank in enumerate((c1[0], c1[1], pj)):
                    nc.scalar.activation(tev[p][:, :, 3 * P * k:3 * P * (k + 1)],
                                         bank[0:TR, 0:384].rearrange("p (e n) -> p e n", e=U),
                                         ACT.Copy, scale=1.0 / (WS * WS)).then_inc(s_tev, 1)

            def fold_step(i, p, first):
                n = 2 * i + p
                for q in range(2):
                    act.wait_ge(s_fold, 2 * n + q + 1)
                    nc.scalar.activation(weff[:, :, 0, bass.ds(n * U + q * Q, Q)].rearrange("p n e -> p e n"),
                                         rc[p][q][:, :].rearrange("p (e n) -> p e n", e=Q),
                                         ACT.Copy, scale=1.0 / WS).then_inc(s_whi, 1)
                if not first:
                    act.wait_ge(s_ts[p], 16 * i)
                t_evac(n, p)

            act.wait_ge(s_wprep, 12)
            for p in range(2):
                fold_step(0, p, True)
            with act.Fori(1, FU // 2) as i:
                for p in range(2):
                    fold_step(i, p, False)

            def gelu1(u, q, p):
                buf = f32b[0][:, :].rearrange("p (g r w) -> p g r w", g=U, r=SL)
                for k in range(Q):
                    for h in range(2):
                        ins = nc.scalar.activation(
                            buf[64 * h:64 * h + 64, q * Q + k, 1 - h:9 - h, 1:17],
                            c1[q][64 * h:64 * h + 64, k * HALF:(k + 1) * HALF].rearrange("p (r w) -> p r w", r=8),
                            ACT.Gelu, bias=gsh[0][64 * h:64 * h + 64, q * Q + k:q * Q + k + 1],
                            scale=gsc[0][64 * h:64 * h + 64, q * Q + k:q * Q + k + 1])
                ins.then_inc(s_g1, 1)

            def gelu2(u, p):
                act.wait_ge(s_sh[1], u + 1)
                for q in range(2):
                    act.wait_ge(s_g2ff, 2 * u + q + 1)
                    for k in range(Q):
                        ins = nc.scalar.activation(g2f[:, q * Q + k, :], rc[p][q][:, k * HALF:(k + 1) * HALF], ACT.Gelu,
                                                   bias=gsh[1][:, q * Q + k:q * Q + k + 1],
                                                   scale=gsc[1][:, q * Q + k:q * Q + k + 1])
                    ins.then_inc(s_g2, 1)

            def step(u, p, first):
                act.wait_ge(s_sh[0], u + 2)
                act.wait_ge(s_sp1, 2 * u + 1)
                gelu1(u + 1, 0, 1 - p)
                if not first:
                    gelu2(u - 1, 1 - p)
                act.wait_ge(s_sp1, 2 * u + 2)
                gelu1(u + 1, 1, 1 - p)

            act.wait_ge(s_padz, 1)
            act.wait_ge(s_sh[0], 1)
            gelu1(0, 0, 0)
            gelu1(0, 1, 0)
            with act.Fori(0, GROUPS) as g:
                for p in range(2):
                    step(g * GU + p, p, p == 0)
                with act.Fori(1, GU // 2) as j:
                    for p in range(2):
                        step(g * GU + j * 2 + p, p, False)
                gelu2(g * GU + GU - 1, 1)

        @block.tensor
        def _(pe):
            def bands(out, w, buf, q, width=HALF):
                v = buf[:, :, :].rearrange("p h (g r w) -> p h g r w", g=U, r=SL)
                n = 0
                for t in range(2):
                    for m in range(3):
                        for wp, xp in ((0, 0), (0, 1), (1, 0)):
                            last = nc.tensor.matmul(out, w[:, wp, 3 * t + m, :],
                                                    v[:, xp, q * Q:q * Q + Q, t:t + 8, m:m + P],
                                                    start=(n == 0), stop=(n == 17))
                            n += 1
                            yield last

            def run(gen, count=None):
                last = None
                for k, last in enumerate(gen):
                    if count is not None and k + 1 == count:
                        break
                return last

            def fold_step(i, p, first):
                n = 2 * i + p
                pe.wait_ge(s_psp, 2 * n + 2)
                for q in range(2):
                    if not first:
                        pe.wait_ge(s_wlo, 2 * (n - 2) + q + 1)
                    run(bands(rc[p][q][:, :], fws, ghl[p], q)).then_inc(s_fold, 1)
                if not (first and p == 0):
                    pe.wait_ge(s_tev, 3 * n)
                v = ghl[p][:, :, :].rearrange("p h (g r w) -> p h g r w", g=U, r=SL)
                for k, bank in enumerate((c1[0], c1[1], pj)):
                    for m, (wp, xp) in enumerate(((0, 0), (0, 1), (1, 0))):
                        last = nc.tensor.matmul(bank[0:TR, 0:384], tws[:, wp, :], v[:, xp, :, 3 * k:3 * k + 3, 1:17],
                                                start=(m == 0), stop=(m == 2))
                last.then_inc(s_tps, 1)

            pe.wait_ge(s_wprep, 12)
            for p in range(2):
                fold_step(0, p, True)
            with pe.Fori(1, FU // 2) as i:
                for p in range(2):
                    fold_step(i, p, False)

            def conv1(p):
                v = im[p][:, :].rearrange("p (g r w) -> p g r w", g=U, r=SL)
                for q in range(2):
                    nc.tensor.matmul(c1[q][:, :], w1s[:, :], v[:, q * Q:q * Q + Q, 0:8, 0:P],
                                     start=True, stop=True).then_inc(s_c1, 1)

            def stats(s, count, before):
                pe.wait_ge(s_ms[s], count)
                pe.wait_ge(s_rd[1 - s], before + 1)
                pe.wait_ge(s_rd[s], count)
                for k in range(2):
                    last = nc.tensor.matmul(st[:, 0:2 * U], grp[:, :], ms[s][:, :, :, k],
                                            start=(k == 0), stop=(k == 1))
                last.then_inc(s_st[s], 1)

            pe.sem_inc(s_c1, 1)
            pe.sem_inc(s_rc, 1)
            pe.wait_ge(s_w1s, 32)
            pe.wait_ge(s_im[0], 96)
            pe.wait_ge(s_tev, 3 * FU)
            pe.wait_ge(s_wlo, 2 * FU)
            conv1(0)
            stats(0, 1, 0)

            def step(u, im_count, p, first):
                pe.wait_ge(s_im[1 - p], im_count)
                pe.wait_ge(s_g1, 2 * u + 2)
                conv1(1 - p)
                pe.wait_ge(s_sp1, 2 * u + 1)
                pe.wait_ge(s_rfree, 2 * u + 1)
                b0 = bands(rc[p][0][:, :], rws, ghl[p], 0)
                run(b0, 12)
                stats(0, u + 2, u if first else u - 1)
                run(b0).then_inc(s_rc, 1)
                if not first:
                    stats(1, u, u + 2)
                pe.wait_ge(s_sp1, 2 * u + 2)
                pe.wait_ge(s_rfree, 2 * u + 2)
                run(bands(rc[p][1][:, :], rws, ghl[p], 1)).then_inc(s_rc, 1)

            def project(g):
                pe.wait_ge(s_sp2, 2 * GU * (g + 1))
                pe.wait_ge(s_pjr, g + 1)
                for n in range(HALF):
                    both = (pj[0:G, 0:2 * E], g2[:, 0, :, n], weff[:, n, :, :].rearrange("p h e -> p (h e)"))
                    low = (pj[0:G, 0:E], g2[:, 1, :, n], weff[:, n, 0, :])
                    for k, ops in enumerate((both, low) if n == 0 else (low, both)):
                        last = nc.tensor.matmul(*ops, start=(n == 0 and k == 0), stop=(n == HALF - 1 and k == 1),
                                                skip_group_check=True)
                last.then_inc(s_pj, 1)

            with pe.Fori(0, GROUPS) as g:
                for p in range(2):
                    step(g * GU + p, 96 * (g * (GU // 2) + 1 + p), p, p == 0)
                with pe.Fori(1, GU // 2) as j:
                    for p in range(2):
                        step(g * GU + j * 2 + p, 96 * (g * (GU // 2) + j + 1 + p), p, False)
                stats(1, g * GU + GU, g * GU + GU + 1)
                project(g)

        @block.vector
        def _(dve):
            v = nc.vector
            dve.wait_ge(s_wld, 16 * 6)
            v.tensor_scalar(pars[:, 0:1], par[:, 0:1], WS, None, ALU.mult).then_inc(s_wprep, 1)
            v.tensor_scalar(pars[:, 1:2], par[:, 3:4], WS, None, ALU.mult).then_inc(s_wprep, 1)
            v.tensor_tensor(tst32[:, TR - 1:TR], par[:, 0:1], par[:, 6:7], ALU.add).then_inc(s_wprep, 1)
            dve.wait_ge(s_wprep, 3)
            n = 3
            for src, dst in ((rst32, rws), (fst32, fws), (tst32, tws), (w1st32, w1hl)):
                hi, lo = (dst[:, k].rearrange("p a b -> p (a b)") if len(dst.shape) == 4 else dst[:, k, :] for k in range(2))
                v.tensor_scalar(hi, src, WS, None, ALU.mult).then_inc(s_wprep, 1)
                dve.wait_ge(s_wprep, n + 1)
                v.scalar_tensor_tensor(lo, src, WS, hi, ALU.mult, ALU.subtract).then_inc(s_wprep, 1)
                n += 2
            v.memset(pars[:, 2:3], 0.0).then_inc(s_wprep, 1)
            dve.wait_ge(s_xld, 16)
            for k in range(21):
                v.bn_stats(x6[:, k, :], xt[:, k // 7, k % 7, :]).then_inc(s_xch, 1)
            dve.wait_ge(s_xch, 21)
            for k in range(21):
                ins = v.bn_aggr(xmv[:, k, :], x6[:, k, :])
            ins.then_inc(s_xhl, 1)
            dve.wait_ge(s_xhl, 1)
            v.tensor_scalar(xsd[:, 0, :], xmv[:, :, 1], 256.0 / 255.0, None, ALU.mult).then_inc(s_xvar, 1)
            dve.wait_ge(s_xstd, 1)
            v.tensor_scalar(xsd[:, 2, :], xsd[:, 1, :], 1e-6, float(P) ** 0.5, ALU.add, ALU.mult).then_inc(s_xvar, 1)
            dve.wait_ge(s_xvar, 2)
            v.reciprocal(xsd[:, 0, :], xsd[:, 2, :]).then_inc(s_xvar, 1)
            dve.wait_ge(s_xvar, 3)
            for k in range(21):
                t = xt[:, k // 7, k % 7, :]
                v.tensor_scalar(t, t, xmv[:, k, 0:1], xsd[:, 0, k:k + 1], ALU.subtract, ALU.mult).then_inc(s_xch, 1)
            dve.wait_ge(s_xch, 42)
            dve.wait_ge(s_xz, 1)
            for q in range(6):
                c, pr = q // 2, q % 2
                src = xt[:, c].rearrange("p w (r k j) -> p w r k j", k=2, j=P)[:, :, :, 1 - pr, :]
                dst = [xhl[:, 6 * h + q, :].rearrange("p (w r j) -> p w r j", w=7, r=SL)[:, :, 1 - pr:9 - pr, 1:17]
                       for h in range(2)]
                v.tensor_copy(dst[0], src).then_inc(s_xhl, 1)
                dve.wait_ge(s_xhl, 2 * q + 2)
                v.tensor_tensor(dst[1], src, dst[0], ALU.subtract).then_inc(s_xhl, 1)

            def proj_split(i, p, first):
                n = 2 * i + p
                dve.wait_ge(s_pld[p], 16 * (i + 1))
                if not first:
                    dve.wait_ge(s_tps, n - 1)
                v.tensor_scalar(ghl[p][:, 0, :], f32b[p][:, :], WS, None, ALU.mult).then_inc(s_psp, 1)
                dve.wait_ge(s_psp, 2 * n + 1)
                v.scalar_tensor_tensor(ghl[p][:, 1, :], f32b[p][:, :], WS, ghl[p][:, 0, :], ALU.mult,
                                       ALU.subtract).then_inc(s_psp, 1)

            def w_lo(i, p):
                n = 2 * i + p
                for q in range(2):
                    dve.wait_ge(s_whi, 2 * n + q + 1)
                    sl = bass.ds(n * U + q * Q, Q)
                    v.scalar_tensor_tensor(weff[:, :, 1, sl].rearrange("p n e -> p e n"),
                                           rc[p][q][:, :].rearrange("p (e n) -> p e n", e=Q), 1.0 / WS,
                                           weff[:, :, 0, sl].rearrange("p n e -> p e n"), ALU.mult,
                                           ALU.subtract).then_inc(s_wlo, 1)

            proj_split(0, 0, True)
            proj_split(0, 1, True)
            with dve.Fori(0, FU // 2 - 1) as i:
                w_lo(i, 0)
                proj_split(i + 1, 0, False)
                w_lo(i, 1)
                proj_split(i + 1, 1, False)
            for p in range(2):
                w_lo(FU // 2 - 1, p)
            dve.wait_ge(s_tps, FU)
            v.memset(f32b[0][:, :], 0.0).then_inc(s_padz, 1)
            dve.wait_ge(s_scr, 16 * 6)
            v.sem_inc(s_rfree, 4)
            v.sem_inc(s_rd[0], 1)
            v.sem_inc(s_rd[1], 1)
            v.sem_inc(s_pjr, 1)
            v.sem_inc(s_g2ff, 2)

            K = 14
            bias = (pars[:, 0:1], pars[:, 1:2])
            gam = (par[:, 1:2], par[:, 4:5])
            bet = (par[:, 2:3], par[:, 5:6])

            def moments(s, u, src):
                ch = Chain(dve, s_ch[s], u * K)
                for q in range(2):
                    for k in range(Q):
                        ch.did(v.bn_stats(stt6[s][:, q * Q + k, :], src[q][:, k * HALF:(k + 1) * HALF]))
                ch.wait()
                b6 = stt6[s][:, :, :].rearrange("p g (e k) -> p g e k", e=2)
                ch.did(v.tensor_scalar(ms[s][:, 0, :, :], b6[:, :, :, 1], bias[s], None, ALU.add))
                ch.wait()
                ch.did(v.tensor_tensor(ms[s][:, 1, :, :], ms[s][:, 0, :, :], ms[s][:, 0, :, :], ALU.mult))
                ch.wait()
                v.scalar_tensor_tensor(ms[s][:, 1, :, :], b6[:, :, :, 2], 2.0 / HALF, ms[s][:, 1, :, :], ALU.mult,
                                       ALU.add).then_inc(s_ms[s], 1)

            def variance(s, u):
                dve.wait_ge(s_st[s], u + 1)
                v.tensor_copy(mst[s][:, :, :], st[:, 0:2 * U].rearrange("p (a b) -> p a b", a=2)).then_inc(s_rd[s], 1)
                ch = Chain(dve, s_ch[s], u * K + 10)
                dve.wait_ge(s_rd[s], u + 2)
                ch.did(v.tensor_tensor(msq[s][:, :], mst[s][:, 0, :], mst[s][:, 0, :], ALU.mult))
                ch.wait()
                v.scalar_tensor_tensor(var[s][:, :], mst[s][:, 1, :], EPS * WS * WS, msq[s][:, :], ALU.add,
                                       ALU.subtract).then_inc(s_var[s], 1)

            def affine(s, u):
                ch = Chain(dve, s_ch[s], u * K + 11)
                dve.wait_ge(s_pow[s], u + 1)
                ch.did(v.tensor_scalar(gsc[s][:, :], rst[s][:, :], gam[s], None, ALU.mult))
                ch.wait()
                ch.did(v.scalar_tensor_tensor(gsh[s][:, :], mst[s][:, 0, :], bias[s], gsc[s][:, :], ALU.subtract, ALU.mult))
                ch.wait()
                ch.did(v.tensor_scalar(gsh[s][:, :], gsh[s][:, :], -1.0, bet[s], ALU.mult, ALU.add))
                ch.wait()
                v.sem_inc(s_sh[s], 1)

            def split1(u, q, p):
                dve.wait_ge(s_g1, 2 * u + q + 1)
                n = slice(q * Q * PAD, (q + 1) * Q * PAD)
                v.tensor_copy(ghl[p][:, 0, n], f32b[0][:, n]).then_inc(s_sp1h, 1)
                dve.wait_ge(s_sp1h, 2 * u + q + 1)
                v.tensor_tensor(ghl[p][:, 1, n], f32b[0][:, n], ghl[p][:, 0, n], ALU.subtract).then_inc(s_sp1, 1)

            def split2(u, slot):
                for q in range(2):
                    dve.wait_ge(s_g2, 2 * u + q + 1)
                    v.sem_inc(s_rfree, 1)
                    src = g2f[:, q * Q:q * Q + Q, :]
                    dst = [g2[:, h, bass.ds(slot + q * Q, Q), :] for h in range(2)]
                    v.tensor_copy(dst[0], src).then_inc(s_sp2h, 1)
                    dve.wait_ge(s_sp2h, 2 * u + q + 1)
                    v.tensor_tensor(dst[1], src, dst[0], ALU.subtract).then_inc(s_sp2, 1)
                    dve.wait_ge(s_sp2, 2 * u + q + 1)
                    v.sem_inc(s_g2ff, 1)

            def step(u, slot, p, first):
                dve.wait_ge(s_c1, 2 * u + 5)
                moments(0, u + 1, c1)
                if not first:
                    dve.wait_ge(s_rc, 2 * u + 1)
                    moments(1, u - 1, rc[1 - p])
                variance(0, u + 1)
                if not first:
                    variance(1, u - 1)
                affine(0, u + 1)
                if not first:
                    affine(1, u - 1)
                dve.wait_ge(s_rc, 2 * u + 1)
                split1(u + 1, 0, 1 - p)
                if not first:
                    split2(u - 1, slot - U)
                split1(u + 1, 1, 1 - p)

            dve.wait_ge(s_c1, 3)
            moments(0, 0, c1)
            variance(0, 0)
            affine(0, 0)
            split1(0, 0, 0)
            split1(0, 1, 0)
            with dve.Fori(0, GROUPS) as g:
                for p in range(2):
                    step(g * GU + p, p * U, p, p == 0)
                with dve.Fori(1, GU // 2) as j:
                    for p in range(2):
                        step(g * GU + j * 2 + p, j * (2 * U) + p * U, p, False)
                ul = g * GU + GU - 1
                dve.wait_ge(s_rc, 2 * (g * GU + GU) + 1)
                moments(1, ul, rc[1])
                variance(1, ul)
                affine(1, ul)
                split2(ul, (GU - 1) * U)
                dve.wait_ge(s_pj, g + 1)
                dve.wait_ge(s_emb, 16 * g + 16)
                v.tensor_scalar(tok[:, 1, :], pj[0:G, E:2 * E], 1.0 / WS, None, ALU.mult).then_inc(s_tokc, 1)
                dve.wait_ge(s_tokc, g + 1)
                v.scalar_tensor_tensor(tok[:, 0, :], pj[0:G, 0:E], 1.0 / WS, tok[:, 1, :], ALU.mult,
                                       ALU.add).then_inc(s_tok, 1)
                dve.wait_ge(s_tok, g + 1)
                v.sem_inc(s_pjr, 1)


NT = 8
TI = HP * HP
NH, HS = 12, 16
HID = 4 * E
HC = E // 2
HT = NH // 2
NTOK = NT * 128
LOWEST = float(np.finfo(np.float32).min)


def build_tail(nc, a, emb, xs, ts, out):
    with ExitStack() as ctx:
        def sb(name, shape, dt=F32):
            return ctx.enter_context(nc.sbuf_tensor("tl_" + name, shape, dt))

        def sem(name):
            return ctx.enter_context(nc.semaphore("t_" + name))

        ident = sb("ident", [128, 128])
        ones = sb("ones", [1, 128])
        khalf = sb("khalf", [128, NT])
        hmask = sb("hmask", [HC, HT])
        causal = sb("causal", [128, TI])
        pos = sb("pos", [128, 2, E])
        big = sb("big", [128, 2 * TR * 144])
        tl = big[0:HC, :].rearrange("p (e t n) -> p e t n", e=2, t=TR)
        wr = sb("wr", [HC, 2, C * P * P])
        wrb = sb("wrb", [HC, 2])
        wrT = sb("wrT", [128, 6, E])
        brow = sb("brow", [1, 5, E])
        brow2 = sb("brow2", [1, 2, E])
        mrow = sb("mrow", [1, E])
        pjb = sb("pjb", [1, E])
        embt = sb("embt", [128, NT, E])
        xst = sb("xst", [128, NT, C * P * P])
        xsT = [sb(f"xsT{i}", [128, 6, 128]) for i in range(2)]
        h = sb("h", [128, NT, E])
        xn = sb("xn", [128, NT, E])
        h1, x2 = xst[:, :, 0:E], xst[:, :, E:2 * E]
        st6 = sb("st6", [128, NT, 6])
        mv = sb("mv", [128, NT, 2])
        ve = sb("ve", [128, NT])
        rs = sb("rs", [128, NT])
        xT = sb("xT", [HC, 2, NTOK])
        qkT = big[0:HC, 6144:6144 + 4 * NTOK].rearrange("p (m n) -> p m n", m=4)
        vt = big[0:64, 10240:10240 + 2 * NT * E].rearrange("p (i n) -> p i n", n=E)
        kb = [sb(f"kb{i}", [HC, 2, 2, HT, TI]) for i in range(2)]
        pr = [sb(f"pr{i}", [128, NH, TI]) for i in range(2)]
        mx = [sb(f"mx{i}", [128, NH]) for i in range(2)]
        sm = [sb(f"sm{i}", [128, NH]) for i in range(2)]
        ri = [sb(f"ri{i}", [128, NH]) for i in range(2)]
        pT = sb("pT", [TI, NH, 128])
        y = sb("y", [128, E])
        yT = sb("yT", [HC, 2, 128])
        wqkv = [sb(f"wqkv{i}", [HC, 2, 3 * E]) for i in range(2)]
        wpr = [sb(f"wpr{i}", [HC, 2, E]) for i in range(3)]
        qb = sb("qb", [HC, 4])
        vb = sb("vb", [1, E])
        lnp = sb("lnp", [HC, 2, 8])
        w1 = sb("w1", [HC, 2, HID])
        b1 = sb("b1", [128, 6])
        w2 = sb("w2", [128, 6, E])
        w2v = sb("w2v", [128, 3, 6, E])
        gw = sb("gw", [128, 3])
        hid = [big[:, i * 3072:(i + 1) * 3072].rearrange("p (j n) -> p j n", j=6) for i in range(2)]

        bank = [ctx.enter_context(nc.psum_tensor(f"bank{i}", [128, 512], F32)) for i in range(8)]

        d_w, d_tl, d_x, d_out = sem("weights"), sem("tl"), sem("tokens"), sem("out")
        zer = sem("zeroed")
        dch, pch = sem("dve_chain"), sem("pool_chain")
        wprep = sem("wprep")
        wrs, wrt_p, wrt_c = sem("wr_sum"), sem("wrT_psum"), sem("wrT_copied")
        AX = mybir.AxisListType
        xt_p, xt_c, tk_p, tk_c = sem("xT_psum"), sem("xT_copied"), sem("tok_psum"), sem("tok_done")
        ln_v, ln_r, ln_x, ln_tp, ln_tc = sem("ln_var"), sem("ln_rstd"), sem("ln_x"), sem("ln_t_psum"), sem("ln_t_copied")
        qk_p, qk_c, v_p, v_c = sem("qk_psum"), sem("qk_copied"), sem("v_psum"), sem("v_copied")
        kb_r, sc_p, sc_r, ex, pt_p, pt_c = (sem("kblocks"), sem("scores"), sem("scores_shifted"), sem("exp"),
                                           sem("pT_psum"), sem("pT_copied"))
        y_p, y_c, yt_p, yt_c, o_p, o_c = (sem("y_psum"), sem("y_done"), sem("yT_psum"), sem("yT_copied"),
                                          sem("o_psum"), sem("o_added"))
        h_p, h_c, m_p, m_c = sem("hid_psum"), sem("hid_gelu"), sem("mlp_psum"), sem("mlp_added")
        block = ctx.enter_context(nc.Block())

        @block.sync
        def _(sp):
            def ld(dst, src):
                sp.dma_start(dst, src).then_inc(d_w, 16)

            for e in range(2):
                sp.dma_start(tl[:, e], ts[e * HC:(e + 1) * HC]).then_inc(d_tl, 16)
            sp.wait_ge(zer, 4)
            for i in range(2):
                sl = slice(64 * i, 64 * i + TI)
                sp.dma_start(xst[sl, :, :], xs.rearrange("(t i n) e -> i n t e", i=2, n=TI)[i]).then_inc(d_x, 16)
                sp.dma_start(embt[sl, :, :], emb.rearrange("(t i n) e -> i n t e", i=2, n=TI)[i]).then_inc(d_x, 16)
            ld(ident[:, :], a["ident"])
            ld(hmask[:, :], a["hmask"])
            ld(causal[:, :], a["causal"])
            ld(pos[:, :, :], a["pos"])
            ld(pjb[:, :], a["proj_b"])
            ld(wqkv[0][:, :, :], a["wqkv1"].rearrange("(k p) n -> p k n", k=2))
            ld(wqkv[1][:, :, :], a["wqkv2"].rearrange("(k p) n -> p k n", k=2))
            ld(wpr[0][:, :, :], a["wproj1"].rearrange("(k p) n -> p k n", k=2))
            ld(wpr[1][:, :, :], a["wproj2"].rearrange("(k p) n -> p k n", k=2))
            ld(qb[:, :], a["qkb"])
            ld(vb[:, :], a["vb"])
            ld(lnp[:, :, :], a["lnp"])
            ld(w1[:, :, :], a["w1"].rearrange("(k p) n -> p k n", k=2))
            ld(b1[:, :], a["b1"])
            ld(w2[:, :, :], a["w2"].rearrange("(k p) n -> p k n", p=128))
            ld(gw[:, :], a["gw"])
            ld(brow[:, 1:3, :], a["brow"])
            ld(brow2[:, 0, :], a["b2"])
            for t in range(NT):
                sp.wait_ge(m_c, t + 1)
                for i in range(2):
                    sp.dma_start(out[2 * t + i], h[64 * i:64 * i + TI, t, :]).then_inc(d_out, 16)
            sp.wait_ge(d_out, 16 * 2 * NT)

        NW = 18

        @block.gpsimd
        def _(pool):
            nc.gpsimd.memset(xst[:, :, :], 0.0).then_inc(zer, 1)
            nc.gpsimd.memset(embt[:, :, :], 0.0).then_inc(zer, 1)
            nc.gpsimd.memset(khalf[:, :], -0.5).then_inc(zer, 1)
            nc.gpsimd.memset(ones[:, :], 1.0).then_inc(zer, 1)
            pool.wait_ge(zer, 4)

            def rstd(n):
                pool.wait_ge(ln_v, n + 1)
                nc.gpsimd.tensor_tensor(rs[:, :], ve[:, :], khalf[:, :], ALU.pow).then_inc(ln_r, 1)

            def kblocks(at):
                for t in range(NT):
                    n = at * NT + t
                    pool.wait_ge(qk_c, 8 * at + 8)
                    if n >= 2:
                        pool.wait_ge(sc_p, n - 1)
                    for i in range(2):
                        for k in range(2):
                            src = qkT[:, 2 + k, t * 128 + 64 * i:t * 128 + 64 * i + TI]
                            ins = nc.gpsimd.tensor_tensor(
                                kb[n % 2][:, i, k, :, :], src.unsqueeze(1).broadcast_to((HC, HT, TI)),
                                hmask[:, :].unsqueeze(2).broadcast_to((HC, HT, TI)), ALU.mult)
                    ins.then_inc(kb_r, 1)

            rstd(0)
            kblocks(0)
            rstd(1)
            rstd(2)
            kblocks(1)
            rstd(3)

        @block.scalar
        def _(act):
            act.wait_ge(d_w, 16 * NW)

            def copy(dst, src, done, **kw):
                nc.scalar.activation(dst, src, ACT.Identity if kw else ACT.Copy, **kw).then_inc(done, 1)

            for k in range(3):
                act.wait_ge(wrt_p, k + 1)
                for j in range(2):
                    copy(wrT[:, 2 * k + j, :], bank[k][:, j * E:(j + 1) * E], wrt_c)
            for t in range(NT):
                for k in range(2):
                    act.wait_ge(xt_p, 2 * t + k + 1)
                    n = (4, 2)[k]
                    if t >= 2 and k == 0:
                        act.wait_ge(tk_p, t - 1)
                    copy(xsT[t % 2][:, 4 * k:4 * k + n, :], bank[2 * (t % 2) + k][:, 0:n * 128].rearrange("p (a b) -> p a b", b=128), xt_c)

            def transposed(n, g=None):
                for t in range(NT):
                    act.wait_ge(ln_tp, n * NT + t + 1)
                    for k in range(2):
                        kw = {}
                        if g is not None:
                            c = g + (0 if t < NT // 2 else 2)
                            kw = dict(scale=lnp[:, k, c:c + 1], bias=lnp[:, k, c + 1:c + 2])
                        copy(xT[:, k, t * 128:(t + 1) * 128], bank[t % 4][0:HC, k * 128:(k + 1) * 128], ln_tc, **kw)

            def attention(at):
                for m in range(4):
                    for hf in range(2):
                        n = 2 * m + hf
                        act.wait_ge(qk_p, 8 * at + n + 1)
                        kw = dict(bias=qb[:, m:m + 1], scale=1.0) if at == 0 else {}
                        copy(qkT[:, m, 512 * hf:512 * hf + 512], bank[4 + n % 4][0:HC, :], qk_c, **kw)
                for i in range(NT):
                    act.wait_ge(v_p, NT * at + i + 1)
                    copy(vt[:, 2 * i:2 * i + 2, :], bank[i % 4][0:64, 0:2 * E].rearrange("p (a b) -> p a b", a=2), v_c)
                for t in range(NT):
                    n = at * NT + t
                    act.wait_ge(sc_r, n + 1)
                    nc.scalar.activation(pr[n % 2][:, :, :], pr[n % 2][:, :, :], ACT.Exp).then_inc(ex, 1)
                    for k in range(3):
                        act.wait_ge(pt_p, 3 * n + k + 1)
                        copy(pT[:, 4 * k:4 * k + 4, :], bank[4 + k][0:TI, :].rearrange("p (a b) -> p a b", a=4), pt_c)
                    act.wait_ge(yt_p, n + 1)
                    copy(yT[:, :, :], bank[7][0:HC, 0:256].rearrange("p (a b) -> p a b", a=2), yt_c)

            transposed(0)
            attention(0)
            transposed(1, 0)
            attention(1)
            transposed(2, 4)
            n = 0
            for v in range(4):
                for j in range(6):
                    act.wait_ge(h_p, n + 1)
                    if v >= 2:
                        act.wait_ge(m_p, (0, 0, 4, 8)[v])
                    nc.scalar.activation(hid[v % 2][:, j, :], bank[n % 4][:, :], ACT.Gelu, bias=b1[:, j:j + 1],
                                         scale=1.0).then_inc(h_c, 1)
                    n += 1

        @block.tensor
        def _(pe):
            mm = nc.tensor.matmul
            pe.wait_ge(d_w, 16 * NW)
            pe.wait_ge(wrs, 1)
            for k in range(3):
                for j in range(2):
                    for e in range(2):
                        last = nc.tensor.transpose(bank[k][:, j * E + e * HC:j * E + (e + 1) * HC],
                                                   wr[:, e, (2 * k + j) * 128:(2 * k + j + 1) * 128], ident[0:HC, 0:HC])
                last.then_inc(wrt_p, 1)
            for e in range(2):
                last = nc.tensor.transpose(bank[3][0:1, e * HC:(e + 1) * HC], wrb[:, e:e + 1], ident[0:HC, 0:HC])
            last.then_inc(wrt_p, 1)
            pe.wait_ge(wrt_c, 6)
            pe.wait_ge(wprep, 1)

            def xt(t):
                for k in range(2):
                    if t >= 2:
                        pe.wait_ge(xt_c, 2 * (t - 2) + k + 1)
                    for j in range((4, 2)[k]):
                        m = 4 * k + j
                        last = nc.tensor.transpose(bank[2 * (t % 2) + k][:, j * 128:(j + 1) * 128],
                                                   xst[:, t, m * 128:(m + 1) * 128], ident[:, :])
                    last.then_inc(xt_p, 1)

            pe.wait_ge(d_x, 64)
            xt(0)
            for t in range(NT):
                if t + 1 < NT:
                    xt(t + 1)
                pe.wait_ge(xt_c, 2 * t + 2)
                if t >= 4:
                    pe.wait_ge(tk_c, t - 3)
                o = bank[4 + t % 4][:, 0:E]
                mm(o, ones[:, :], brow[:, 0, :], start=True, stop=False)
                for m in range(6):
                    last = mm(o, xsT[t % 2][:, m, :], wrT[:, m, :], start=False, stop=(m == 5))
                last.then_inc(tk_p, 1)

            def transposed(n, free):
                for t in range(NT):
                    pe.wait_ge(ln_x, free[0] + t + 1)
                    if t >= 4:
                        pe.wait_ge(ln_tc, 2 * (n * NT + t - 4) + 2)
                    for k in range(2):
                        last = nc.tensor.transpose(bank[t % 4][0:HC, k * 128:(k + 1) * 128],
                                                   xn[:, t, k * HC:(k + 1) * HC], ident[:, :])
                    last.then_inc(ln_tp, 1)

            def attention(at, n_tc):
                w = wqkv[at]
                pe.wait_ge(ln_tc, n_tc)
                for m in range(4):
                    for hf in range(2):
                        n = 2 * m + hf
                        if n >= 4:
                            pe.wait_ge(qk_c, 8 * at + n - 3)
                        for k in range(2):
                            last = mm(bank[4 + n % 4][0:HC, :], w[:, k, m * HC:(m + 1) * HC],
                                      xT[:, k, 512 * hf:512 * hf + 512], start=(k == 0), stop=(k == 1))
                        last.then_inc(qk_p, 1)
                for i in range(NT):
                    if i >= 4:
                        pe.wait_ge(v_c, NT * at + i - 3)
                    for s in range(2):
                        o = bank[i % 4][0:64, s * E:(s + 1) * E]
                        for k in range(2):
                            last = mm(o, xT[:, k, i * 128 + 64 * s:i * 128 + 64 * s + 64], w[:, k, 2 * E:3 * E],
                                      start=(k == 0), stop=(at == 1 and k == 1))
                        if at == 0:
                            last = mm(o, ones[:, 0:64], vb[:, :], start=False, stop=True)
                    last.then_inc(v_p, 1)

                def scores(t):
                    n = at * NT + t
                    pe.wait_ge(kb_r, n + 1)
                    if n >= 2:
                        pe.wait_ge(sc_r, n - 1)
                    for k in range(2):
                        for i in range(2):
                            last = mm(bank[2 * (n % 2) + k][64 * i:64 * i + 64, 0:HT * TI],
                                      qkT[:, k, t * 128 + 64 * i:t * 128 + 64 * i + 64],
                                      kb[n % 2][:, i, k, :, :].rearrange("p a b -> p (a b)"), start=True, stop=True)
                    last.then_inc(sc_p, 1)

                pe.wait_ge(qk_c, 8 * at + 8)
                pe.wait_ge(v_c, NT * (at + 1))
                scores(0)
                for t in range(NT):
                    n = at * NT + t
                    if t + 1 < NT:
                        scores(t + 1)
                    pe.wait_ge(ex, n + 1)
                    for k in range(3):
                        for j in range(4):
                            last = nc.tensor.transpose(bank[4 + k][0:TI, j * 128:(j + 1) * 128],
                                                       pr[n % 2][:, 4 * k + j, :], ident[:, :])
                        last.then_inc(pt_p, 1)
                    if n:
                        pe.wait_ge(o_c, n)
                    for hd in range(NH):
                        pe.wait_ge(pt_c, 3 * n + hd // 4 + 1) if hd % 4 == 0 else None
                        for i in range(2):
                            last = mm(bank[7][64 * i:64 * i + 64, hd * HS:(hd + 1) * HS], pT[:, hd, 64 * i:64 * i + 64],
                                      vt[0:TI, 2 * t + i, hd * HS:(hd + 1) * HS], start=True, stop=True)
                    last.then_inc(y_p, 1)
                    pe.wait_ge(y_c, n + 1)
                    for k in range(2):
                        last = nc.tensor.transpose(bank[7][0:HC, k * 128:(k + 1) * 128], y[:, k * HC:(k + 1) * HC],
                                                   ident[:, :])
                    last.then_inc(yt_p, 1)
                    pe.wait_ge(yt_c, n + 1)
                    small = at == 1 and t >= NT // 2
                    wp = wpr[at + small]
                    o = bank[7][:, 256:256 + E]
                    mm(o, ones[:, :], brow[:, 1 + at + small, :], start=True, stop=False)
                    for k in range(2):
                        last = mm(o, yT[:, k, :], wp[:, k, :], start=False, stop=(k == 1))
                    last.then_inc(o_p, 1)

            pe.wait_ge(tk_c, NT)
            transposed(0, (0,))
            attention(0, 2 * NT)
            transposed(1, (2 * NT,))
            attention(1, 4 * NT)
            pe.wait_ge(o_c, 2 * NT)
            transposed(2, (3 * NT,))
            pe.wait_ge(ln_tc, 6 * NT)
            keep = (E, E, E // 2, E // 3)

            def hidden(v):
                for j in range(6):
                    n = 6 * v + j
                    if n >= 4:
                        pe.wait_ge(h_c, n - 3)
                    ks = [(k, min(HC, keep[v] - HC * k)) for k in range(2) if keep[v] > HC * k]
                    for x, (k, c) in enumerate(ks):
                        last = mm(bank[n % 4][:, :], w1[0:c, k, j * 128:(j + 1) * 128],
                                  xT[0:c, k, 512 * (v > 0):512 * (v > 0) + 512], start=(x == 0), stop=(x == len(ks) - 1))
                    last.then_inc(h_p, 1)

            def second(v):
                pe.wait_ge(h_c, 6 * v + 6)
                w = keep[v]
                for t in range(4):
                    o = bank[4 + t]
                    if v == 1:
                        pe.wait_ge(m_c, t + 1)
                    if v <= 1:
                        mm(o[:, 0:E], ones[:, :], brow2[:, v, :], start=True, stop=False, skip_group_check=True)
                    for j in range(6):
                        rhs = w2[:, j, :] if v == 0 else w2v[:, v - 1, j, 0:w]
                        last = mm(o[:, 0:w], hid[v % 2][:, j, t * 128:(t + 1) * 128], rhs, start=False,
                                  stop=(j == 5), skip_group_check=True)
                    last.then_inc(m_p, 1)

            hidden(0)
            for v in range(4):
                if v < 3:
                    hidden(v + 1)
                second(v)

        @block.vector
        def _(dve):
            v = nc.vector
            count = [0]

            def link(ins):
                count[0] += 1
                ins.then_inc(dch, 1)
                dve.wait_ge(dch, count[0])

            link(v.memset(wr[:, :, :], 0.0))
            dve.wait_ge(d_tl, 32)
            for e in range(2):
                T = tl[:, e].rearrange("p t (s x) -> p t s x", x=P)
                W = wr[:, e, :].rearrange("p (c r k x) -> p c r k x", c=C, k=2, x=P)
                for ky in range(3):
                    for kx in range(3):
                        for py in range(2):
                            d = py - ky + 1
                            half, off = (0, (d + 1) // 2) if d % 2 else (1, d // 2)
                            lo, hi = max(0, kx - 1), min(P, P + kx - 1)
                            row = 27 * half + 3 * ky + kx
                            o = W[:, :, :, py, lo:hi]
                            link(v.tensor_tensor(o, o, T[:, row:row + 19:9, off:off + 8, lo - kx + 1:hi - kx + 1], ALU.add))
            v.tensor_reduce(wrb[:, :], tl[:, :, TR - 1, :], AX.X, ALU.add).then_inc(wrs, 1)
            dve.wait_ge(d_w, 16 * NW)
            for i in range(3):
                v.tensor_scalar(w2v[:, i, :, :], w2[:, :, :], gw[:, i:i + 1], None, ALU.mult)
            link(v.memset(mrow[:, :], 0.0))
            for i, c in enumerate((E, E // 2, E // 3)):
                link(v.tensor_scalar(mrow[:, 0:c], mrow[:, 0:c], gw[0:1, i:i + 1], None, ALU.add))
            link(v.tensor_tensor(brow[:, 3, :], brow[:, 2, :], mrow[:, :], ALU.mult))
            link(v.tensor_tensor(brow2[:, 1, :], brow2[:, 0, :], mrow[:, :], ALU.mult))
            link(v.tensor_scalar(wpr[2][:, :, :], wpr[1][:, :, :], gw[0:HC, 0:1], None, ALU.mult))
            for i, c in ((1, HC), (2, E // 3)):
                link(v.scalar_tensor_tensor(wpr[2][0:c, 0, 0:c], wpr[1][0:c, 0, 0:c], gw[0:c, i:i + 1],
                                            wpr[2][0:c, 0, 0:c], ALU.mult, ALU.add))
            dve.wait_ge(wrt_p, 4)
            v.tensor_tensor(brow[:, 0, :], bank[3][0:1, 0:E], pjb[:, :], ALU.add).then_inc(wprep, 1)
            dve.wait_ge(d_x, 64)
            dve.wait_ge(zer, 4)
            for k in range(2):
                link(v.tensor_tensor(embt[:, :, :], embt[:, :, :], pos[:, k, :].unsqueeze(1).broadcast_to((128, NT, E)),
                                     ALU.add))
            for t in range(NT):
                dve.wait_ge(tk_p, t + 1)
                v.tensor_tensor(h[:, t, :], bank[4 + t % 4][:, 0:E], embt[:, t, :], ALU.add).then_inc(tk_c, 1)
            dve.wait_ge(tk_c, NT)

            ln = [0]

            def layernorm(src, dst, tiles_read):
                n = ln[0]
                ln[0] += 1
                for t in range(NT):
                    ins = v.bn_stats(st6[:, t, :], src[:, t, :])
                link(ins)
                for t in range(NT):
                    ins = v.bn_aggr(mv[:, t, :], st6[:, t, :])
                link(ins)
                v.tensor_scalar(ve[:, :], mv[:, :, 1], EPS, None, ALU.add).then_inc(ln_v, 1)
                dve.wait_ge(ln_r, n + 1)
                for t in range(NT):
                    v.tensor_scalar(dst[:, t, :], src[:, t, :], mv[:, t, 0:1], rs[:, t:t + 1], ALU.subtract,
                                    ALU.mult).then_inc(ln_x, 1)
                dve.wait_ge(ln_x, NT * (n + 1))

            def attention(at):
                def soft(t):
                    n = at * NT + t
                    dve.wait_ge(sc_p, n + 1)
                    if n >= 2:
                        dve.wait_ge(pt_p, 3 * (n - 1))
                    p = pr[n % 2]
                    for k in range(2):
                        src = bank[2 * (n % 2) + k][:, 0:HT * TI].rearrange("p (a b) -> p a b", a=HT)
                        dst = p[:, HT * k:HT * k + HT, :]
                        if at == 0:
                            ins = v.tensor_tensor(dst, src, causal[:, :].unsqueeze(1).broadcast_to((128, HT, TI)), ALU.add)
                        else:
                            ins = v.tensor_copy(dst, src)
                    link(ins)
                    link(v.tensor_reduce(mx[n % 2][:, :], p[:, :, :], AX.X, ALU.max))
                    v.tensor_tensor(p[:, :, :], p[:, :, :], mx[n % 2][:, :].unsqueeze(2).broadcast_to((128, NH, TI)),
                                    ALU.subtract).then_inc(sc_r, 1)

                soft(0)
                for t in range(NT):
                    n = at * NT + t
                    if t + 1 < NT:
                        soft(t + 1)
                    dve.wait_ge(ex, n + 1)
                    link(v.tensor_reduce(sm[n % 2][:, :], pr[n % 2][:, :, :], AX.X, ALU.add))
                    link(v.reciprocal(ri[n % 2][:, :], sm[n % 2][:, :]))
                    dve.wait_ge(y_p, n + 1)
                    v.tensor_tensor(y[:, :].rearrange("p (a b) -> p a b", a=NH),
                                    bank[7][:, 0:E].rearrange("p (a b) -> p a b", a=NH),
                                    ri[n % 2][:, :].unsqueeze(2).broadcast_to((128, NH, HS)), ALU.mult).then_inc(y_c, 1)
                    dve.wait_ge(o_p, n + 1)
                    v.tensor_tensor(h[:, t, :], h[:, t, :], bank[7][:, 256:256 + E], ALU.add).then_inc(o_c, 1)
                dve.wait_ge(o_c, NT * (at + 1))

            layernorm(h, xn, 0)
            attention(0)
            layernorm(h, x2, 0)
            link(v.tensor_copy(h1[:, :, :], h[:, :, :]))
            link(v.tensor_copy(h[:, :, :], x2[:, :, :]))
            layernorm(h, xn, 0)
            attention(1)
            layernorm(h, xn, 0)
            link(v.tensor_tensor(h1[:, :, :], h1[:, :, :], h[:, :, :], ALU.add))
            for half in range(2):
                for t in range(4):
                    dve.wait_ge(m_p, t + 1 if half == 0 else 12 + t + 1)
                    n = 4 * half + t
                    v.tensor_tensor(h[:, n, :], h1[:, n, :], bank[4 + t][:, 0:E], ALU.add).then_inc(m_c, 1)


def build_program(nc, a, out):
    emb = nc.dram_tensor("scratch_emb", (NPAT, E), F32).ap()
    xs = nc.dram_tensor("scratch_x", (NPAT, C * P * P), F32).ap()
    ts = nc.dram_tensor("scratch_fold", (E, TR, SL * P), F32).ap()
    build_front(nc, a, emb, xs, ts)
    build_tail(nc, a, emb, xs, ts, out)


def layout(inp):
    o = {}
    tokp = {k[7:]: v for k, v in inp.items() if k.startswith("L0_tok_")}
    o["x"] = inp["x"].reshape(B, C, HP, P, HP, P).transpose(1, 0, 2, 4, 3, 5).reshape(C, ROWS, HP, P * P)
    names = ("conv1_b", "gn1_g", "gn1_b", "rconv1_b", "gn2_g", "gn2_b", "rconv2_b")
    o["params"] = np.stack([np.concatenate([tokp[n], tokp[n]]) for n in names], 1)
    r1 = tokp["rconv1_w"].transpose(1, 2, 3, 0)
    r2 = tokp["rconv2_w"].transpose(0, 2, 3, 1)
    rb, fb = np.zeros((2, CH, 2, 3, 2, CH), r1.dtype), np.zeros((2, CH, 2, 3, 2, CH), r1.dtype)
    for slot, hin, hout, ky in ((0, 0, 1, 0), (0, 1, 0, 0), (0, 1, 1, 1), (1, 0, 0, 1), (1, 0, 1, 2), (1, 1, 0, 2)):
        rb[hin, :, slot, :, hout] = r1[:, ky]
        fb[hin, :, slot, :, hout] = r2[:, 2 - ky, ::-1]
    o["rbands"], o["fbands"] = rb.reshape(128, 768), fb.reshape(128, 768)
    w1 = tokp["conv1_w"]
    tb = np.zeros((2, CH, TR), w1.dtype)
    for half in range(2):
        tb[half, :, 27 * half:27 * half + 27] = w1.reshape(CH, 27)
    o["tband"] = tb.reshape(128, TR)
    wb = np.zeros((KC, 2, CH), w1.dtype)
    for kx in range(3):
        for c in range(C):
            for dy in range(4):
                par, up = dy % 2, dy // 2
                rows = [kx * 24 + (6 * k + 2 * c + par) * 2 + up for k in range(2)] + [KA + kx * 12 + (2 * c + par) * 2 + up]
                for half in range(2):
                    if 0 <= dy - 1 + half <= 2:
                        wb[rows, half] = w1[:, c, dy - 1 + half, kx]
    o["w1band"] = wb.reshape(KC, 128)
    i = (np.arange(128) % CH) // 2
    o["grp"] = ((i[:, None] == i[None, :]) / 8.0).astype(np.float32)
    pw = np.zeros((2, CH, E, SL, WD), tokp["proj_w"].dtype)
    w = tokp["proj_w"].transpose(1, 0, 2, 3)
    pw[0, :, :, 1:9, 1:17], pw[1, :, :, 0:8, 1:17] = w[:, :, 1::2], w[:, :, 0::2]
    o["proj"] = pw.reshape(128, E * PAD)

    o["ident"] = np.eye(128, dtype=np.float32)
    o["hmask"] = ((np.arange(HC)[:, None] // HS == np.arange(HT)[None]) * HS ** -0.5).astype(np.float32)
    cm = np.zeros((2, 64, TI), np.float32)
    cm[:, :TI] = np.where(np.tril(np.ones((TI, TI), bool)), 0.0, LOWEST)
    o["causal"] = cm.reshape(128, TI)
    vocab = tokp["row_emb"].shape[0]
    at = []
    for k in range(HP):
        low = int(np.float32(k) / np.float32(HP) * np.float32(vocab))
        high = int(np.float32(k + 1) / np.float32(HP) * np.float32(vocab))
        at.append((low + high) // 2)
    pos = np.zeros((2, 64, 2, E), tokp["row_emb"].dtype)
    for r in range(HP):
        for c in range(HP):
            pos[:, r * HP + c, 0], pos[:, r * HP + c, 1] = tokp["row_emb"][at[r]], tokp["col_emb"][at[c]]
    o["pos"] = pos.reshape(128, 2, E)
    o["proj_b"] = tokp["proj_b"][None]
    o["wqkv1"], o["wproj1"] = inp["L0_attn_Wqkv"], inp["L0_attn_Wproj"]
    o["qkb"] = inp["L0_attn_bqkv"][:2 * E].reshape(4, HC).T
    o["vb"] = inp["L0_attn_bqkv"][2 * E:][None]
    f = {k[7:]: v for k, v in inp.items() if k.startswith("L0_ffn_")}
    o["wqkv2"], o["wproj2"] = f["w_qkv"], f["w_proj"]
    ln = [f[k] for k in ("n1l_g", "n1l_b", "n1s_g", "n1s_b", "n2l_g", "n2l_b", "n2s_g", "n2s_b")]
    o["lnp"] = np.stack(ln, 1).reshape(2, HC, 8).transpose(1, 0, 2)
    o["w1"], o["w2"] = f["w_fc1"], f["w_fc2"]
    o["b1"] = f["b_fc1"].reshape(6, 128).T
    o["b2"] = f["b_fc2"][None]
    o["gw"] = np.tile(f["gumbel_weights"], (128, 1))
    o["brow"] = np.stack([inp["L0_attn_bproj"], f["b_proj"]])[None]
    return o


def kernel(**inputs):
    import numpy as _np
    import concourse.bacc as _bacc
    from concourse.bass_utils import run_bass_kernel_spmd as _run

    arr = layout({k: _np.asarray(v) for k, v in inputs.items()})
    nc = _bacc.Bacc("TRN2", target_bir_lowering=False, num_devices=1)
    arrays, a = {}, {}
    for name, v in arr.items():
        v = _np.ascontiguousarray(v)
        arrays[f"in_{name}"] = v
        a[name] = nc.dram_tensor(f"in_{name}", v.shape, mybir.dt.from_np(v.dtype), kind="ExternalInput").ap()
    out = nc.dram_tensor("out_tokens", (B, TI, E), F32, kind="ExternalOutput").ap()
    build_program(nc, a, out)
    r = _run(nc, [arrays], core_ids=[0])
    return r.results[0]["out_tokens"]
```

```python
import concourse.bass as bass
from concourse import mybir
from contextlib import ExitStack
import numpy as np

F32, F16 = mybir.dt.float32, mybir.dt.float16
ALU, ACT = mybir.AluOpType, mybir.ActivationFunctionType

B, C, P, CH, E = 16, 3, 16, 64, 192
HP = 7
ROWS = B * HP
NPAT = ROWS * HP
SL, WD = 9, 18
PAD = SL * WD
HALF = 8 * P
U = 8
Q = 4
UNITS = NPAT // U
GU = 14
GROUPS = UNITS // GU
G = GU * U
FU = E // U
RUN = (U - 1) * PAD + 8 * WD + P
PLANE = (NPAT + 2 * U + 1) * PAD
KA, KC = 72, 108
WS = 64.0
EPS = 1e-5
TR = 55


DENSE = SL * P
NCH = 6
CHN = [22, 22, 21, 21, 21, 21]
CHS = [sum(CHN[:c]) for c in range(NCH)]
WCH = max(CHN)
W1_READY = W_READY = 9


class Chain:

    def __init__(self, eng, sem, base):
        self.eng, self.sem, self.at = eng, sem, base

    def did(self, ins):
        ins.then_inc(self.sem, 1)
        self.at = self.at + 1

    def wait(self):
        self.eng.wait_ge(self.sem, self.at)


def build_front(nc, a, emb, xs, ts):
    scr = nc.dram_tensor("x_planes", (12, PLANE), F16)
    wlod = nc.dram_tensor("w_lo", (128, HALF * E), F16)
    with ExitStack() as ctx:
        def sb(name, shape, dt=F32):
            return ctx.enter_context(nc.sbuf_tensor("sb_" + name, shape, dt))

        def sem(name):
            return ctx.enter_context(nc.semaphore(name))

        whi = sb("whi", [128, HALF, E], F16)
        wlo = sb("wlo", [128, 2, WCH, E], F16)
        arena = sb("arena", [128, 2, 2 * G * HALF], F16)
        g2 = arena[:, :, :].rearrange("p b (h g n) -> p b h g n", h=2, g=G)
        f32q = sb("f32q", [128, U * DENSE])
        g1f = f32q[:, 0:U * HALF].rearrange("p (g n) -> p g n", g=U)
        ghl = [sb(f"ghl_{i}", [128, 2, U * PAD], F16) for i in range(2)]
        g2f = sb("g2f", [128, U, HALF])
        im = [sb(f"im_{i}", [KC, U * PAD], F16) for i in range(2)]
        rws = sb("rws", [128, 2, 6, 128], F16)
        w1s = sb("w1s", [KC, 128], F16)
        grp = sb("grp", [128, 128])
        par = sb("par", [128, 7])
        N1, N2 = (0, 1), (2, 3)
        wide = (Q, Q, U, U)
        bn6 = [sb(f"bn6_{s}", [128, w, 6]) for s, w in enumerate(wide)]
        ms = [sb(f"ms_{s}", [128, 2, w, 2]) for s, w in enumerate(wide)]
        mst = [sb(f"mst_{s}", [128, 2, w]) for s, w in enumerate(wide)]
        tmp = [sb(f"tmp_{s}", [128, 5, w]) for s, w in enumerate(wide)]
        gsc = [sb(f"gsc_{s}", [128, w]) for s, w in enumerate(wide)]
        gsh = [sb(f"gsh_{s}", [128, w]) for s, w in enumerate(wide)]
        wid = sb("wid", [128, 2, 3, U])
        eps = sb("eps", [128, 2, U])
        half_neg = sb("half_neg", [128, U])
        half_pos = sb("half_pos", [128, 21])
        tok = sb("tok", [G, E])

        b0, b1 = arena[:, 0, :], arena[:, 1, :]
        n = 2 * C * 7 * 256
        xt = b0[0:ROWS, 0:n].bitcast(F32).rearrange("p (c w n) -> p c w n", c=C, w=7)
        xhl = b0[0:ROWS, n:n + 12 * 7 * PAD].rearrange("p (q n) -> p q n", q=12)
        n += 12 * 7 * PAD
        fws = b0[:, n:n + 1536].rearrange("p (h t m) -> p h t m", h=2, t=6)
        n += 1536
        tws = b0[:, n:n + 2 * TR].rearrange("p (h m) -> p h m", h=2)
        n += 2 * TR
        w1hl = b0[0:KC, n:n + 256].rearrange("p (h m) -> p h m", h=2)
        n += 256
        zt = b0[0:12, n:n + U * PAD]
        wlst = b1[:, 0:HALF * E].rearrange("p (n e) -> p n e", n=HALF)
        stage = [f32q[:, :], b1[:, HALF * E:HALF * E + 2 * U * DENSE].bitcast(F32)]
        wv = wlo[0:TR, :, :, :].rearrange("p a b c -> p (a b c)").bitcast(F32)
        tev = [wv[:, i * U * DENSE:(i + 1) * U * DENSE].rearrange("p (e n) -> p e n", e=U) for i in range(2)]
        wst = whi[:, 0:24, :].rearrange("p a c -> p (a c)").bitcast(F32)
        rst32, fst32 = wst[:, 0:768], wst[:, 768:1536]
        tst32, w1st32 = wst[:, 1536:1536 + TR], wst[0:KC, 1600:1728]
        xsm = g2f[0:ROWS, :, :].rearrange("p a b -> p (a b)")
        x6 = xsm[:, 0:126].rearrange("p (k n) -> p k n", n=6)
        xmv = xsm[:, 126:168].rearrange("p (k n) -> p k n", n=2)
        xsd = xsm[:, 168:231].rearrange("p (k n) -> p k n", k=3)

        rc = [[ctx.enter_context(nc.psum_tensor(f"rc{i}{q}", [128, 512], F32)) for q in range(2)] for i in range(2)]
        c1 = [ctx.enter_context(nc.psum_tensor(f"c1_{q}", [128, 512], F32)) for q in range(2)]
        pj = ctx.enter_context(nc.psum_tensor("pj", [128, 512], F32))
        st = ctx.enter_context(nc.psum_tensor("st", [128, 512], F32))

        s_wld, s_xld, s_wprep, s_w1s = sem("weights_loaded"), sem("x_loaded"), sem("weights_prepared"), sem("w1_placed")
        s_cst, s_xvar, s_xstd, s_xz, s_xhl, s_xch = (sem("constants"), sem("x_var"), sem("x_std"), sem("x_zeroed"),
                                               sem("x_split"), sem("x_chain"))
        s_scr, s_zero, s_padz = sem("x_stored"), sem("zero_tile"), sem("pads_zeroed")
        s_wid = sem("parameters_widened")
        s_pld = [sem(f"proj_loaded{i}") for i in range(2)]
        s_psp, s_fold, s_tps = sem("proj_split"), sem("fold_done"), sem("t_done")
        s_whi, s_wlo, s_tev = sem("w_hi"), sem("w_lo_done"), sem("t_evacuated")
        s_ts = [sem(f"t_stored{i}") for i in range(2)]
        s_wst = sem("w_lo_stored")
        s_wch = [sem(f"w_chunk{i}") for i in range(2)]
        s_im = [sem(f"im_loaded{i}") for i in range(2)]
        s_c1, s_rc = sem("conv1_done"), sem("rconv_done")
        s_ms, s_st, s_rd = ([sem(f"{n}{s}") for s in (1, 2)] for n in ("moments", "group_means", "means_read"))
        s_dch, s_pch, s_sh = ([sem(f"{n}{s}") for s in (1, 2)] for n in ("dve_chain", "pool_chain", "affine"))
        s_g1, s_sp1h, s_sp1 = sem("gelu1_done"), sem("split1_hi"), sem("split1_done")
        s_g2, s_sp2h, s_sp2 = sem("gelu2_done"), sem("split2_hi"), sem("split2_done")
        s_pc, s_pj, s_pjr, s_emb = sem("chunk_used"), sem("projected"), sem("tokens_out"), sem("emb_stored")

        block = ctx.enter_context(nc.Block())

        def over_groups(eng, group):
            group(0, 0, True)
            with eng.Fori(0, (GROUPS - 1) // 2) as i:
                group(2 * i + 1, 1, False)
                group(2 * i + 2, 0, False)

        def over_units(eng, g, pair, first):
            pair(g * GU, 0, first)
            with eng.Fori(1, GU // 2) as j:
                pair(g * GU + 2 * j, j, False)

        @block.sync
        def _(sp):
            sp.dma_start(par[:, :], a["params"]).then_inc(s_wld, 16)
            sp.dma_start(rst32, a["rbands"]).then_inc(s_wld, 16)
            sp.dma_start(fst32, a["fbands"]).then_inc(s_wld, 16)
            sp.dma_start(tst32, a["tband"]).then_inc(s_wld, 16)
            sp.dma_start(w1st32, a["w1band"]).then_inc(s_wld, 16)
            sp.dma_start(grp[:, :], a["grp"]).then_inc(s_wld, 16)

            def load_proj(n, p):
                sp.dma_start(stage[p], a["proj"][:, bass.ds(n * (U * DENSE), U * DENSE)]).then_inc(s_pld[p], 16)

            load_proj(0, 0)
            load_proj(1, 1)
            sp.dma_start(xt, a["x"].rearrange("c p w n -> p c w n")).then_inc(s_xld, 16)
            sp.wait_ge(s_wprep, W1_READY)
            sp.dma_start(w1s[0:KA, :], w1hl[0:KA, 0, :]).then_inc(s_w1s, 16)
            sp.dma_start(w1s[KA:KC, :], w1hl[KA:KC, 1, :]).then_inc(s_w1s, 16)

            def fold_io(i, p, last):
                n = 2 * i + p
                if not last:
                    sp.wait_ge(s_psp, 2 * n + 2)
                    load_proj(n + 2, p)
                sp.wait_ge(s_tev, 3 * n + 3)
                sp.dma_start(bass.AP(tensor=ts.tensor, offset=n * (U * TR * DENSE),
                                     ap=[[DENSE, TR], [TR * DENSE, U], [1, DENSE]]),
                             tev[p][:, :, :]).then_inc(s_ts[p], 16)

            with sp.Fori(0, 3) as i:
                for p in range(2):
                    fold_io(i, p, False)
            sp.wait_ge(s_xch, 42)
            for c in range(C):
                sp.dma_start(xs.rearrange("(r w) (c n) -> r c w n", w=7, c=C)[:, c], xt[:, c]).then_inc(s_scr, 16)
            sp.wait_ge(s_xhl, 13)
            for h in range(2):
                sp.dma_start(bass.AP(tensor=scr, offset=h * 6 * PLANE, ap=[[7 * PAD, ROWS], [PLANE, 6], [1, 7 * PAD]]),
                             xhl[:, 6 * h:6 * h + 6, :]).then_inc(s_scr, 16)
            sp.wait_ge(s_zero, 1)
            for n, k in ((NPAT, U), (NPAT + U, U), (NPAT + 2 * U, 1)):
                sp.dma_start(bass.AP(tensor=scr, offset=n * PAD, ap=[[PLANE, 12], [1, k * PAD]]),
                             zt[:, 0:k * PAD]).then_inc(s_scr, 16)
            with sp.Fori(3, FU // 2 - 1) as i:
                for p in range(2):
                    fold_io(i, p, False)
            for p in range(2):
                fold_io(FU // 2 - 1, p, True)
            sp.wait_ge(s_wlo, 2 * FU)
            sp.dma_start(wlod.ap(), b1[:, 0:HALF * E]).then_inc(s_wst, 16)
            sp.wait_ge(s_scr, 16 * 8)
            sp.sem_inc(s_emb, 16)

            def load_im(u, p):
                for kx in range(3):
                    sp.dma_start(im[p][24 * kx:24 * kx + 24, 0:RUN],
                                 bass.AP(tensor=scr, offset=u * (U * PAD) + kx,
                                         ap=[[PLANE, 12], [WD, 2], [1, RUN]])).then_inc(s_im[p], 16)
                    sp.dma_start(im[p][KA + 12 * kx:KA + 12 * kx + 12, 0:RUN],
                                 bass.AP(tensor=scr, offset=u * (U * PAD) + kx,
                                         ap=[[PLANE, 6], [WD, 2], [1, RUN]])).then_inc(s_im[p], 16)

            def load_chunk(g, c):
                sp.wait_ge(s_pc, (g - 1) * NCH + c + 1)
                sp.dma_start(wlo[:, c % 2, 0:CHN[c], :].rearrange("p n e -> p (n e)"),
                             wlod.ap()[:, CHS[c] * E:(CHS[c] + CHN[c]) * E]).then_inc(s_wch[c % 2], 16)

            def group(g, b, first):
                if not first:
                    sp.wait_ge(s_wst, 16)
                for j in range(GU // 2):
                    for p in range(2):
                        u = g * GU + 2 * j + p
                        sp.wait_ge(s_c1, 2 * u + 3)
                        load_im(u + 2, p)
                    if not first and j < NCH:
                        load_chunk(g, j)
                if not first:
                    sp.wait_ge(s_pjr, g + 1)
                    sp.dma_start(emb[bass.ds((g - 1) * G, G), :], tok[:, :]).then_inc(s_emb, 16)

            load_im(0, 0)
            load_im(1, 1)
            over_groups(sp, group)
            for c in range(NCH):
                load_chunk(GROUPS, c)
            sp.wait_ge(s_pjr, GROUPS + 1)
            sp.dma_start(emb[(GROUPS - 1) * G:NPAT, :], tok[:, :]).then_inc(s_emb, 16)
            sp.wait_ge(s_emb, 16 * GROUPS + 16)
            sp.wait_ge(s_ts[0], 16 * (FU // 2))
            sp.wait_ge(s_ts[1], 16 * (FU // 2))

        @block.gpsimd
        def _(pool):
            gp = nc.gpsimd
            gp.memset(half_neg[:, :], -0.5).then_inc(s_cst, 1)
            gp.memset(half_pos[:, :], 0.5).then_inc(s_cst, 1)
            gp.memset(eps[:, 0, :], 0.0).then_inc(s_cst, 1)
            gp.memset(eps[:, 1, :], EPS * WS * WS).then_inc(s_cst, 1)
            gp.memset(zt, 0.0).then_inc(s_zero, 1)
            gp.memset(xhl.bitcast(F32), 0.0).then_inc(s_xz, 1)
            pool.wait_ge(s_cst, 4)
            pool.wait_ge(s_xvar, 1)
            gp.tensor_tensor(xsd[:, 1, :], xsd[:, 0, :], half_pos[0:ROWS, :], ALU.pow).then_inc(s_xstd, 1)

            def norm(stage_, s, n):
                w = wide[s]
                ch = Chain(pool, s_pch[stage_], n * 6)
                mean, sq, (t1, t2, t3, t4, t5) = mst[s][:, 0, :], mst[s][:, 1, :], (tmp[s][:, k, :] for k in range(5))
                bias, gam, bet = (wid[:, stage_, k, 0:w] for k in range(3))
                pool.wait_ge(s_rd[stage_], n + 2)
                ch.did(gp.tensor_tensor(t1, mean, mean, ALU.mult))
                ch.did(gp.tensor_tensor(t2, mean, bias, ALU.subtract))
                ch.wait()
                ch.did(gp.tensor_tensor(t3, sq, t1, ALU.subtract))
                ch.wait()
                ch.did(gp.tensor_tensor(t5, t3, half_neg[:, 0:w], ALU.pow))
                ch.wait()
                ch.did(gp.tensor_tensor(gsc[s][:, :], t5, gam, ALU.mult))
                ch.wait()
                ch.did(gp.tensor_tensor(t4, t2, gsc[s][:, :], ALU.mult))
                ch.wait()
                gp.tensor_tensor(gsh[s][:, :], bet, t4, ALU.subtract).then_inc(s_sh[stage_], 1)

            def pair(u0, j, first):
                for p in range(2):
                    u = u0 + p
                    norm(0, 0, 2 * u + 2)
                    if not (first and p == 0):
                        norm(1, N2[1 - p], u - 1)
                    norm(0, 1, 2 * u + 3)

            pool.wait_ge(s_padz, 3)
            norm(0, 0, 0)
            norm(0, 1, 1)
            over_groups(pool, lambda g, b, first: over_units(pool, g, pair, first))
            norm(1, N2[1], UNITS - 1)

        @block.scalar
        def _(act):
            def fold_step(i, p, first):
                n = 2 * i + p
                for q in range(2):
                    act.wait_ge(s_fold, 2 * n + q + 1)
                    nc.scalar.activation(whi[:, :, bass.ds(n * U + q * Q, Q)].rearrange("p n e -> p e n"),
                                         rc[p][q][:, :].rearrange("p (e n) -> p e n", e=Q),
                                         ACT.Copy, scale=1.0 / WS).then_inc(s_whi, 1)
                if not first:
                    act.wait_ge(s_ts[p], 16 * i)
                act.wait_ge(s_tps, n + 1)
                for k, bank in enumerate((c1[0], c1[1], pj)):
                    nc.scalar.activation(tev[p][:, :, 3 * P * k:3 * P * (k + 1)],
                                         bank[0:TR, 0:384].rearrange("p (e n) -> p e n", e=U),
                                         ACT.Copy, scale=1.0 / (WS * WS)).then_inc(s_tev, 1)

            act.wait_ge(s_wprep, W_READY)
            for p in range(2):
                fold_step(0, p, True)
            with act.Fori(1, FU // 2) as i:
                for p in range(2):
                    fold_step(i, p, False)

            def gelu1(k, q, guard=True):
                act.wait_ge(s_sh[0], k + 1)
                if guard:
                    act.wait_ge(s_sp1, k - 1)
                for m in range(Q):
                    ins = nc.scalar.activation(g1f[:, q * Q + m, :], c1[q][:, m * HALF:(m + 1) * HALF], ACT.Gelu,
                                               bias=gsh[q][:, m:m + 1], scale=gsc[q][:, m:m + 1])
                ins.then_inc(s_g1, 1)

            def pair(u0, j, first):
                for p in range(2):
                    u = u0 + p
                    gelu1(2 * u + 1, 1, not (first and p == 0))
                    if not (first and p == 0):
                        if not (first and p == 1):
                            gelu2_at(u - 2, 1, p)
                    gelu1(2 * u + 2, 0)
                    if not (first and p == 0):
                        gelu2_at(u - 1, 0, 1 - p)

            def gelu2_at(u, q, p):
                s = N2[p]
                act.wait_ge(s_sh[1], u + 1)
                act.wait_ge(s_sp2, 2 * u + q + 1)
                for m in range(Q):
                    ins = nc.scalar.activation(g2f[:, q * Q + m, :], rc[p][q][:, m * HALF:(m + 1) * HALF], ACT.Gelu,
                                               bias=gsh[s][:, q * Q + m:q * Q + m + 1],
                                               scale=gsc[s][:, q * Q + m:q * Q + m + 1])
                ins.then_inc(s_g2, 1)

            act.sem_inc(s_g2, 4)
            gelu1(0, 0, False)
            over_groups(act, lambda g, b, first: over_units(act, g, pair, first))
            gelu2_at(UNITS - 2, 1, 0)
            gelu2_at(UNITS - 1, 0, 1)
            gelu2_at(UNITS - 1, 1, 1)

        @block.tensor
        def _(pe):
            def bands(out, w, buf, q):
                v = buf[:, :, :].rearrange("p h (g r w) -> p h g r w", g=U, r=SL)
                n = 0
                for t in range(2):
                    for m in range(3):
                        for wp, xp in ((0, 0), (0, 1), (1, 0)):
                            last = nc.tensor.matmul(out, w[:, wp, 3 * t + m, :],
                                                    v[:, xp, q * Q:q * Q + Q, t:t + 8, m:m + P],
                                                    start=(n == 0), stop=(n == 17))
                            n += 1
                            yield last

            def run(gen, count=None):
                last = None
                for k, last in enumerate(gen):
                    if count is not None and k + 1 == count:
                        break
                return last

            def fold_step(i, p, first):
                n = 2 * i + p
                pe.wait_ge(s_psp, 2 * n + 2)
                for q in range(2):
                    if not first:
                        pe.wait_ge(s_wlo, 2 * (n - 2) + q + 1)
                    run(bands(rc[p][q][:, :], fws, ghl[p], q)).then_inc(s_fold, 1)
                if not (first and p == 0):
                    pe.wait_ge(s_tev, 3 * n)
                v = ghl[p][:, :, :].rearrange("p h (g r w) -> p h g r w", g=U, r=SL)
                for k, bank in enumerate((c1[0], c1[1], pj)):
                    for m, (wp, xp) in enumerate(((0, 0), (0, 1), (1, 0))):
                        last = nc.tensor.matmul(bank[0:TR, 0:384], tws[:, wp, :], v[:, xp, :, 3 * k:3 * k + 3, 1:17],
                                                start=(m == 0), stop=(m == 2))
                last.then_inc(s_tps, 1)

            pe.wait_ge(s_wprep, W_READY)
            for p in range(2):
                fold_step(0, p, True)
            with pe.Fori(1, FU // 2) as i:
                for p in range(2):
                    fold_step(i, p, False)

            def conv1(q, p):
                v = im[p][:, :].rearrange("p (g r w) -> p g r w", g=U, r=SL)
                nc.tensor.matmul(c1[q][:, :], w1s[:, :], v[:, q * Q:q * Q + Q, 0:8, 0:P], start=True, stop=True)
                nc.tensor.matmul(c1[q][0:CH, :].rearrange("p (g n) -> p g n", g=Q)[:, :, 0:P], w1s[:, 0:CH],
                                 v[:, q * Q:q * Q + Q, 8, 0:P], start=True, stop=True).then_inc(s_c1, 1)

            def means(stage_, s, n, other):
                pe.wait_ge(s_ms[stage_], n + 1)
                pe.wait_ge(s_rd[stage_], n + 1)
                pe.wait_ge(s_rd[1 - stage_], other + 1)
                for k in range(2):
                    last = nc.tensor.matmul(st[:, 0:2 * wide[s]], grp[:, :], ms[s][:, :, :, k], start=(k == 0), stop=(k == 1))
                last.then_inc(s_st[stage_], 1)

            def project(b, n0, n1):
                for n in range(n0, n1):
                    c = max(k for k in range(NCH) if CHS[k] <= n)
                    yield nc.tensor.matmul(pj[0:G, 0:E], g2[:, b, 0, :, n], whi[:, n, :], start=(n == 0), stop=False)
                    yield nc.tensor.matmul(pj[0:G, 0:E], g2[:, b, 0, :, n], wlo[:, c % 2, n - CHS[c], :], start=False, stop=False)
                    yield nc.tensor.matmul(pj[0:G, 0:E], g2[:, b, 1, :, n], whi[:, n, :], start=False, stop=(n == HALF - 1))

            def chunk_waits(g, c):
                if c == 0:
                    pe.wait_ge(s_sp2, 2 * GU * g + 2)
                    pe.wait_ge(s_pjr, g)
                pe.wait_ge(s_wch[c % 2], 16 * ((NCH // 2) * (g - 1) + c // 2 + 1))

            def emit(u, q, p, g, b, first, im_count, s_idx=None):
                k2 = not (first and p == 0)
                pe.wait_ge(s_sp1, 2 * u + q + 1)
                pe.wait_ge(s_g2, 2 * u + q + 1)
                conv = bands(rc[p][q][:, :], rws, ghl[p], q)
                proj, c, part = iter(()), 0, 0
                if s_idx is not None and s_idx >= 4:
                    c, part = divmod(s_idx - 4, 4)
                    if part == 0:
                        chunk_waits(g, c)
                    lo, hi = (CHS[c] + (CHN[c] * (part + x)) // 4 for x in range(2))
                    proj = project(1 - b, lo, hi)
                run(conv, 8)
                means(0, N1[q], 2 * u + q + 2, u - (q == 0) if k2 else 0)
                last = run(proj)
                if last is not None and part == 3:
                    last.then_inc(s_pj if c == NCH - 1 else s_pc, 1)
                    if c == NCH - 1:
                        pe.sem_inc(s_pc, 1)
                run(conv, 4)
                if q == 1:
                    pe.wait_ge(s_im[p], im_count)
                pe.wait_ge(s_g1, 2 * u + q + 2)
                conv1(1 - q, 1 - p if q == 0 else p)
                if q == 0 and k2:
                    means(1, N2[1 - p], u - 1, 2 * u + q + 3)
                run(conv).then_inc(s_rc, 1)

            def group0(g, b, first):
                def pair(u0, j, first):
                    for p in range(2):
                        for q in range(2):
                            emit(u0 + p, q, p, 0, 0, first, 96 * (j + 2))
                over_units(pe, 0, pair, True)

            def group(g, b, first):
                if first:
                    return group0(g, b, first)
                for j in range(GU // 2):
                    for p in range(2):
                        for q in range(2):
                            emit(g * GU + 2 * j + p, q, p, g, b, False, 96 * (g * (GU // 2) + j + 2), 4 * j + 2 * p + q)

            pe.sem_inc(s_c1, 1)
            pe.sem_inc(s_pc, 2)
            pe.sem_inc(s_pj, 1)
            pe.wait_ge(s_w1s, 32)
            pe.wait_ge(s_im[0], 96)
            pe.wait_ge(s_tev, 3 * FU)
            pe.wait_ge(s_wlo, 2 * FU)
            conv1(0, 0)
            conv1(1, 0)
            means(0, 0, 0, 0)
            means(0, 1, 1, 0)
            pe.wait_ge(s_im[1], 96)
            pe.wait_ge(s_g1, 1)
            conv1(0, 1)
            over_groups(pe, group)
            means(1, N2[1], UNITS - 1, 2 * UNITS + 2)
            for c in range(NCH):
                chunk_waits(GROUPS, c)
                last = run(project(0, CHS[c], CHS[c] + CHN[c]))
                last.then_inc(s_pj if c == NCH - 1 else s_pc, 1)

        @block.vector
        def _(dve):
            v = nc.vector
            for p in range(2):
                v.memset(ghl[p][:, :, :].rearrange("p a b -> p (a b)").bitcast(F32), 0.0).then_inc(s_padz, 1)
            dve.wait_ge(s_wld, 16 * 6)
            v.tensor_tensor(tst32[:, TR - 1:TR], par[:, 0:1], par[:, 6:7], ALU.add).then_inc(s_wprep, 1)
            dve.wait_ge(s_wprep, 1)
            n = 1
            for src, dst in ((rst32, rws), (fst32, fws), (tst32, tws), (w1st32, w1hl)):
                hi, lo = (dst[:, k].rearrange("p a b -> p (a b)") if len(dst.shape) == 4 else dst[:, k, :] for k in range(2))
                v.tensor_scalar(hi, src, WS, None, ALU.mult).then_inc(s_wprep, 1)
                dve.wait_ge(s_wprep, n + 1)
                v.scalar_tensor_tensor(lo, src, WS, hi, ALU.mult, ALU.subtract).then_inc(s_wprep, 1)
                n += 2
            assert n == W1_READY == W_READY

            def proj_split(i, p, first):
                n = 2 * i + p
                dve.wait_ge(s_pld[p], 16 * (i + 1))
                if not first:
                    dve.wait_ge(s_tps, n - 1)
                hi, lo = (ghl[p][:, h, :].rearrange("p (r w) -> p r w", w=WD)[:, :, 1:17] for h in range(2))
                src = stage[p].rearrange("p (r w) -> p r w", w=P)
                v.tensor_scalar(hi, src, WS, None, ALU.mult).then_inc(s_psp, 1)
                dve.wait_ge(s_psp, 2 * n + 1)
                v.scalar_tensor_tensor(lo, src, WS, hi, ALU.mult, ALU.subtract).then_inc(s_psp, 1)

            def w_lo(i, p):
                n = 2 * i + p
                for q in range(2):
                    dve.wait_ge(s_whi, 2 * n + q + 1)
                    sl = bass.ds(n * U + q * Q, Q)
                    v.scalar_tensor_tensor(wlst[:, :, sl].rearrange("p n e -> p e n"),
                                           rc[p][q][:, :].rearrange("p (e n) -> p e n", e=Q), 1.0 / WS,
                                           whi[:, :, sl].rearrange("p n e -> p e n"), ALU.mult,
                                           ALU.subtract).then_inc(s_wlo, 1)

            dve.wait_ge(s_padz, 2)
            proj_split(0, 0, True)
            proj_split(0, 1, True)
            dve.wait_ge(s_xld, 16)
            for k in range(21):
                v.bn_stats(x6[:, k, :], xt[:, k // 7, k % 7, :]).then_inc(s_xch, 1)
            dve.wait_ge(s_xch, 21)
            for k in range(21):
                ins = v.bn_aggr(xmv[:, k, :], x6[:, k, :])
            ins.then_inc(s_xhl, 1)
            dve.wait_ge(s_xhl, 1)
            v.tensor_scalar(xsd[:, 0, :], xmv[:, :, 1], 256.0 / 255.0, None, ALU.mult).then_inc(s_xvar, 1)

            def fold_pair(i):
                w_lo(i, 0)
                proj_split(i + 1, 0, False)
                w_lo(i, 1)
                proj_split(i + 1, 1, False)

            fold_pair(0)
            dve.wait_ge(s_xstd, 1)
            v.tensor_scalar(xsd[:, 2, :], xsd[:, 1, :], 1e-6, float(P) ** 0.5, ALU.add, ALU.mult).then_inc(s_xvar, 1)
            dve.wait_ge(s_xvar, 2)
            v.reciprocal(xsd[:, 0, :], xsd[:, 2, :]).then_inc(s_xvar, 1)
            dve.wait_ge(s_xvar, 3)
            for k in range(21):
                t = xt[:, k // 7, k % 7, :]
                v.tensor_scalar(t, t, xmv[:, k, 0:1], xsd[:, 0, k:k + 1], ALU.subtract, ALU.mult).then_inc(s_xch, 1)
            fold_pair(1)
            dve.wait_ge(s_xch, 42)
            dve.wait_ge(s_xz, 1)
            for q in range(6):
                c, pr = q // 2, q % 2
                src = xt[:, c].rearrange("p w (r k j) -> p w r k j", k=2, j=P)[:, :, :, pr, :]
                dst = [xhl[:, 6 * h + q, :].rearrange("p (w r j) -> p w r j", w=7, r=SL)[:, :, 1:9, 1:17]
                       for h in range(2)]
                v.tensor_copy(dst[0], src).then_inc(s_xhl, 1)
                dve.wait_ge(s_xhl, 2 * q + 2)
                v.tensor_tensor(dst[1], src, dst[0], ALU.subtract).then_inc(s_xhl, 1)
            with dve.Fori(2, FU // 2 - 1) as i:
                fold_pair(i)
            for p in range(2):
                w_lo(FU // 2 - 1, p)
            one = eps[:, 0, :]
            dve.wait_ge(s_cst, 4)
            for s in range(2):
                v.tensor_scalar(wid[:, s, 0, :], one, 0.0, par[:, 3 * s:3 * s + 1], ALU.mult, ALU.add)
                for k in (1, 2):
                    v.tensor_scalar(wid[:, s, k, :], one, 0.0, par[:, 3 * s + k:3 * s + k + 1], ALU.mult, ALU.add)
            v.tensor_scalar(par[:, 0:1], par[:, 0:1], WS, None, ALU.mult).then_inc(s_wid, 1)
            v.tensor_scalar(par[:, 3:4], par[:, 3:4], WS, None, ALU.mult).then_inc(s_wid, 1)
            dve.wait_ge(s_wid, 2)
            for s in range(2):
                ins = v.tensor_scalar(wid[:, s, 0, :], one, 0.0, par[:, 3 * s:3 * s + 1], ALU.mult, ALU.add)
            ins.then_inc(s_padz, 1)
            dve.wait_ge(s_tps, FU)
            dve.wait_ge(s_padz, 3)
            dve.wait_ge(s_scr, 16 * 8)
            v.sem_inc(s_rd[0], 1)
            v.sem_inc(s_rd[1], 1)
            v.sem_inc(s_pjr, 1)
            v.sem_inc(s_sp2, 2)

            def channel_stats(stage_, s, n0, src, at):
                for m in range(Q):
                    v.bn_stats(bn6[s][:, at + m, :], src[:, m * HALF:(m + 1) * HALF]).then_inc(s_dch[stage_], 1)

            def moments(stage_, s, n0):
                ch = Chain(dve, s_dch[stage_], n0)
                ch.wait()
                b6 = bn6[s][:, :, :].rearrange("p g (e k) -> p g e k", e=2)
                ch.did(v.tensor_scalar(ms[s][:, 0, :, :], b6[:, :, :, 1], par[:, 3 * stage_:3 * stage_ + 1], None, ALU.add))
                ch.wait()
                ch.did(v.tensor_tensor(ms[s][:, 1, :, :], ms[s][:, 0, :, :], ms[s][:, 0, :, :], ALU.mult))
                ch.wait()
                v.scalar_tensor_tensor(ms[s][:, 1, :, :], b6[:, :, :, 2], 2.0 / HALF, ms[s][:, 1, :, :], ALU.mult,
                                       ALU.add).then_inc(s_ms[stage_], 1)

            def read_means(stage_, s, n):
                dve.wait_ge(s_st[stage_], n + 1)
                v.tensor_tensor(mst[s][:, :, :], st[:, 0:2 * wide[s]].rearrange("p (a b) -> p a b", a=2),
                                eps[:, :, 0:wide[s]], ALU.add).then_inc(s_rd[stage_], 1)

            def split1(k, q, p):
                dve.wait_ge(s_g1, k + 1)
                src = g1f[:, q * Q:q * Q + Q, :].rearrange("p g (r w) -> p g r w", w=P)
                hi, lo = (ghl[p][:, h, :].rearrange("p (g r w) -> p g r w", g=U, r=SL)[:, q * Q:q * Q + Q, :, 1:17]
                          for h in range(2))
                parts = ((slice(0, 128), slice(1, 8), slice(1, 8)), (slice(0, 64), slice(8, 9), slice(0, 1)),
                         (slice(64, 128), slice(0, 1), slice(0, 1)))
                for half, to, at in parts:
                    ins = v.tensor_copy(hi[half, :, to, :], src[half, :, at, :])
                ins.then_inc(s_sp1h, 1)
                dve.wait_ge(s_sp1h, k + 1)
                for half, to, at in parts:
                    ins = v.tensor_tensor(lo[half, :, to, :], src[half, :, at, :], hi[half, :, to, :], ALU.subtract)
                ins.then_inc(s_sp1, 1)

            def split2(k, q, buf, slot):
                dve.wait_ge(s_g2, k + 5)
                src = g2f[:, q * Q:q * Q + Q, :]
                hi, lo = (g2[:, buf, h, bass.ds(slot, Q), :] for h in range(2))
                v.tensor_copy(hi, src).then_inc(s_sp2h, 1)
                dve.wait_ge(s_sp2h, k + 1)
                v.tensor_tensor(lo, src, hi, ALU.subtract).then_inc(s_sp2, 1)

            def group(g, b, first):
                def slot(u, q, p, j, head, first):
                    k = 2 * u + q
                    n2 = not (first and p == 0 and q == 0)
                    dve.wait_ge(s_c1, k + 4)
                    channel_stats(0, N1[q], None, c1[q], 0)
                    moments(0, N1[q], 6 * (k + 2) + 4)
                    if n2:
                        dve.wait_ge(s_rc, k)
                        if q == 1:
                            channel_stats(1, N2[p], None, rc[p][0], 0)
                        else:
                            channel_stats(1, N2[1 - p], None, rc[1 - p][1], Q)
                    read_means(0, N1[q], k + 2)
                    split1(k + 1, 1 - q, p if q == 0 else 1 - p)
                    if q == 0 and n2:
                        moments(1, N2[1 - p], 10 * (u - 1) + 8)
                    if not (first and p == 0) and not (first and p == 1 and q == 0):
                        old = head and 2 * p + q < 3
                        split2(k - 3, 1 - q, 1 - b if old else b,
                               (2 * GU + 2 * p + q - 3) * Q if old else j * U * 2 + (2 * p + q - 3) * Q)
                    if q == 0 and n2:
                        read_means(1, N2[1 - p], u - 1)

                def pair(u0, j, first, head):
                    for p in range(2):
                        for q in range(2):
                            if head and p == 1 and q == 1:
                                dve.wait_ge(s_pj, g if not first else 1)
                            slot(u0 + p, q, p, j, head, first)

                pair(g * GU, 0, first, True)
                with dve.Fori(1, GU // 2) as j:
                    pair(g * GU + 2 * j, j, False, False)

            def tokens(g):
                dve.wait_ge(s_pj, g + 2)
                dve.wait_ge(s_emb, 16 * g + 16)
                v.tensor_scalar(tok[:, :], pj[0:G, 0:E], 1.0 / WS, None, ALU.mult).then_inc(s_pjr, 1)

            dve.wait_ge(s_c1, 2)
            channel_stats(0, 0, None, c1[0], 0)
            moments(0, 0, 4)
            dve.wait_ge(s_c1, 3)
            channel_stats(0, 1, None, c1[1], 0)
            moments(0, 1, 10)
            read_means(0, 0, 0)
            read_means(0, 1, 1)
            split1(0, 0, 0)
            group(0, 0, True)
            dve.wait_ge(s_wst, 16)
            with dve.Fori(0, (GROUPS - 1) // 2) as i:
                group(2 * i + 1, 1, False)
                tokens(2 * i)
                group(2 * i + 2, 0, False)
                tokens(2 * i + 1)
            K = 2 * UNITS
            dve.wait_ge(s_rc, K)
            channel_stats(1, N2[1], None, rc[1][1], Q)
            moments(1, N2[1], 10 * (UNITS - 1) + 8)
            read_means(1, N2[1], UNITS - 1)
            for k in (K - 3, K - 2, K - 1):
                split2(k, k % 2, 0, (2 * GU + k - K) * Q)
            tokens(GROUPS - 1)


NT = 8
TI = HP * HP
NH, HS = 12, 16
HID = 4 * E
HC = E // 2
HT = NH // 2
NTOK = NT * 128
LOWEST = float(np.finfo(np.float32).min)


def build_tail(nc, a, emb, xs, ts, out):
    with ExitStack() as ctx:
        def sb(name, shape, dt=F32):
            return ctx.enter_context(nc.sbuf_tensor("tl_" + name, shape, dt))

        def sem(name):
            return ctx.enter_context(nc.semaphore("t_" + name))

        ident = sb("ident", [128, 128])
        ones = sb("ones", [1, 128])
        khalf = sb("khalf", [128, NT])
        hmask = sb("hmask", [HC, HT])
        causal = sb("causal", [128, TI])
        pos = sb("pos", [128, 2, E])
        big = sb("big", [128, 2 * TR * 144])
        tl = big[0:HC, :].rearrange("p (e t n) -> p e t n", e=2, t=TR)
        wr = sb("wr", [HC, 2, C * P * P])
        wrb = sb("wrb", [HC, 2])
        wrT = sb("wrT", [128, 6, E])
        brow = sb("brow", [1, 5, E])
        brow2 = sb("brow2", [1, 2, E])
        mrow = sb("mrow", [1, E])
        pjb = sb("pjb", [1, E])
        embt = sb("embt", [128, NT, E])
        xst = sb("xst", [128, NT, C * P * P])
        xsT = [sb(f"xsT{i}", [128, 6, 128]) for i in range(2)]
        h = sb("h", [128, NT, E])
        xn = sb("xn", [128, NT, E])
        h1, x2 = xst[:, :, 0:E], xst[:, :, E:2 * E]
        st6 = sb("st6", [128, NT, 6])
        mv = sb("mv", [128, NT, 2])
        ve = sb("ve", [128, NT])
        rs = sb("rs", [128, NT])
        xT = sb("xT", [HC, 2, NTOK])
        qkT = big[0:HC, 6144:6144 + 4 * NTOK].rearrange("p (m n) -> p m n", m=4)
        vt = big[0:64, 10240:10240 + 2 * NT * E].rearrange("p (i n) -> p i n", n=E)
        kb = [sb(f"kb{i}", [HC, 2, 2, HT, TI]) for i in range(2)]
        pr = [sb(f"pr{i}", [128, NH, TI]) for i in range(2)]
        mx = [sb(f"mx{i}", [128, NH]) for i in range(2)]
        sm = [sb(f"sm{i}", [128, NH]) for i in range(2)]
        ri = [sb(f"ri{i}", [128, NH]) for i in range(2)]
        pT = sb("pT", [TI, NH, 128])
        y = sb("y", [128, E])
        yT = sb("yT", [HC, 2, 128])
        wqkv = [sb(f"wqkv{i}", [HC, 2, 3 * E]) for i in range(2)]
        wpr = [sb(f"wpr{i}", [HC, 2, E]) for i in range(3)]
        qb = sb("qb", [HC, 4])
        vb = sb("vb", [1, E])
        lnp = sb("lnp", [HC, 2, 8])
        w1 = sb("w1", [HC, 2, HID])
        b1 = sb("b1", [128, 6])
        w2 = sb("w2", [128, 6, E])
        w2v = sb("w2v", [128, 3, 6, E])
        gw = sb("gw", [128, 3])
        hid = [big[:, i * 3072:(i + 1) * 3072].rearrange("p (j n) -> p j n", j=6) for i in range(2)]

        bank = [ctx.enter_context(nc.psum_tensor(f"bank{i}", [128, 512], F32)) for i in range(8)]

        d_w, d_tl, d_x, d_out = sem("weights"), sem("tl"), sem("tokens"), sem("out")
        zer = sem("zeroed")
        dch, pch = sem("dve_chain"), sem("pool_chain")
        wprep = sem("wprep")
        wrs, wrt_p, wrt_c = sem("wr_sum"), sem("wrT_psum"), sem("wrT_copied")
        AX = mybir.AxisListType
        xt_p, xt_c, tk_p, tk_c = sem("xT_psum"), sem("xT_copied"), sem("tok_psum"), sem("tok_done")
        ln_v, ln_r, ln_x, ln_tp, ln_tc = sem("ln_var"), sem("ln_rstd"), sem("ln_x"), sem("ln_t_psum"), sem("ln_t_copied")
        qk_p, qk_c, v_p, v_c = sem("qk_psum"), sem("qk_copied"), sem("v_psum"), sem("v_copied")
        kb_r, sc_p, sc_r, ex, pt_p, pt_c = (sem("kblocks"), sem("scores"), sem("scores_shifted"), sem("exp"),
                                           sem("pT_psum"), sem("pT_copied"))
        y_p, y_c, yt_p, yt_c, o_p, o_c = (sem("y_psum"), sem("y_done"), sem("yT_psum"), sem("yT_copied"),
                                          sem("o_psum"), sem("o_added"))
        h_p, h_c, m_p, m_c = sem("hid_psum"), sem("hid_gelu"), sem("mlp_psum"), sem("mlp_added")
        block = ctx.enter_context(nc.Block())

        @block.sync
        def _(sp):
            def ld(dst, src):
                sp.dma_start(dst, src).then_inc(d_w, 16)

            for e in range(2):
                sp.dma_start(tl[:, e], ts[e * HC:(e + 1) * HC]).then_inc(d_tl, 16)
            sp.wait_ge(zer, 4)
            for i in range(2):
                sl = slice(64 * i, 64 * i + TI)
                sp.dma_start(xst[sl, :, :], xs.rearrange("(t i n) e -> i n t e", i=2, n=TI)[i]).then_inc(d_x, 16)
                sp.dma_start(embt[sl, :, :], emb.rearrange("(t i n) e -> i n t e", i=2, n=TI)[i]).then_inc(d_x, 16)
            ld(ident[:, :], a["ident"])
            ld(hmask[:, :], a["hmask"])
            ld(causal[:, :], a["causal"])
            ld(pos[:, :, :], a["pos"])
            ld(pjb[:, :], a["proj_b"])
            ld(wqkv[0][:, :, :], a["wqkv1"].rearrange("(k p) n -> p k n", k=2))
            ld(wqkv[1][:, :, :], a["wqkv2"].rearrange("(k p) n -> p k n", k=2))
            ld(wpr[0][:, :, :], a["wproj1"].rearrange("(k p) n -> p k n", k=2))
            ld(wpr[1][:, :, :], a["wproj2"].rearrange("(k p) n -> p k n", k=2))
            ld(qb[:, :], a["qkb"])
            ld(vb[:, :], a["vb"])
            ld(lnp[:, :, :], a["lnp"])
            ld(w1[:, :, :], a["w1"].rearrange("(k p) n -> p k n", k=2))
            ld(b1[:, :], a["b1"])
            ld(w2[:, :, :], a["w2"].rearrange("(k p) n -> p k n", p=128))
            ld(gw[:, :], a["gw"])
            ld(brow[:, 1:3, :], a["brow"])
            ld(brow2[:, 0, :], a["b2"])
            for t in range(NT):
                sp.wait_ge(m_c, t + 1)
                for i in range(2):
                    sp.dma_start(out[2 * t + i], h[64 * i:64 * i + TI, t, :]).then_inc(d_out, 16)
            sp.wait_ge(d_out, 16 * 2 * NT)

        NW = 18

        @block.gpsimd
        def _(pool):
            nc.gpsimd.memset(xst[:, :, :], 0.0).then_inc(zer, 1)
            nc.gpsimd.memset(embt[:, :, :], 0.0).then_inc(zer, 1)
            nc.gpsimd.memset(khalf[:, :], -0.5).then_inc(zer, 1)
            nc.gpsimd.memset(ones[:, :], 1.0).then_inc(zer, 1)
            pool.wait_ge(zer, 4)

            def rstd(n):
                pool.wait_ge(ln_v, n + 1)
                nc.gpsimd.tensor_tensor(rs[:, :], ve[:, :], khalf[:, :], ALU.pow).then_inc(ln_r, 1)

            def kblocks(at):
                for t in range(NT):
                    n = at * NT + t
                    pool.wait_ge(qk_c, 8 * at + 8)
                    if n >= 2:
                        pool.wait_ge(sc_p, n - 1)
                    for i in range(2):
                        for k in range(2):
                            src = qkT[:, 2 + k, t * 128 + 64 * i:t * 128 + 64 * i + TI]
                            ins = nc.gpsimd.tensor_tensor(
                                kb[n % 2][:, i, k, :, :], src.unsqueeze(1).broadcast_to((HC, HT, TI)),
                                hmask[:, :].unsqueeze(2).broadcast_to((HC, HT, TI)), ALU.mult)
                    ins.then_inc(kb_r, 1)

            rstd(0)
            kblocks(0)
            rstd(1)
            rstd(2)
            kblocks(1)
            rstd(3)

        @block.scalar
        def _(act):
            act.wait_ge(d_w, 16 * NW)

            def copy(dst, src, done, **kw):
                nc.scalar.activation(dst, src, ACT.Identity if kw else ACT.Copy, **kw).then_inc(done, 1)

            for k in range(3):
                act.wait_ge(wrt_p, k + 1)
                for j in range(2):
                    copy(wrT[:, 2 * k + j, :], bank[k][:, j * E:(j + 1) * E], wrt_c)
            for t in range(NT):
                for k in range(2):
                    act.wait_ge(xt_p, 2 * t + k + 1)
                    n = (4, 2)[k]
                    if t >= 2 and k == 0:
                        act.wait_ge(tk_p, t - 1)
                    copy(xsT[t % 2][:, 4 * k:4 * k + n, :], bank[2 * (t % 2) + k][:, 0:n * 128].rearrange("p (a b) -> p a b", b=128), xt_c)

            def transposed(n, g=None):
                for t in range(NT):
                    act.wait_ge(ln_tp, n * NT + t + 1)
                    for k in range(2):
                        kw = {}
                        if g is not None:
                            c = g + (0 if t < NT // 2 else 2)
                            kw = dict(scale=lnp[:, k, c:c + 1], bias=lnp[:, k, c + 1:c + 2])
                        copy(xT[:, k, t * 128:(t + 1) * 128], bank[t % 4][0:HC, k * 128:(k + 1) * 128], ln_tc, **kw)

            def attention(at):
                for m in range(4):
                    for hf in range(2):
                        n = 2 * m + hf
                        act.wait_ge(qk_p, 8 * at + n + 1)
                        kw = dict(bias=qb[:, m:m + 1], scale=1.0) if at == 0 else {}
                        copy(qkT[:, m, 512 * hf:512 * hf + 512], bank[4 + n % 4][0:HC, :], qk_c, **kw)
                for i in range(NT):
                    act.wait_ge(v_p, NT * at + i + 1)
                    copy(vt[:, 2 * i:2 * i + 2, :], bank[i % 4][0:64, 0:2 * E].rearrange("p (a b) -> p a b", a=2), v_c)
                for t in range(NT):
                    n = at * NT + t
                    act.wait_ge(sc_r, n + 1)
                    nc.scalar.activation(pr[n % 2][:, :, :], pr[n % 2][:, :, :], ACT.Exp).then_inc(ex, 1)
                    for k in range(3):
                        act.wait_ge(pt_p, 3 * n + k + 1)
                        copy(pT[:, 4 * k:4 * k + 4, :], bank[4 + k][0:TI, :].rearrange("p (a b) -> p a b", a=4), pt_c)
                    act.wait_ge(yt_p, n + 1)
                    copy(yT[:, :, :], bank[7][0:HC, 0:256].rearrange("p (a b) -> p a b", a=2), yt_c)

            transposed(0)
            attention(0)
            transposed(1, 0)
            attention(1)
            transposed(2, 4)
            n = 0
            for v in range(4):
                for j in range(6):
                    act.wait_ge(h_p, n + 1)
                    if v >= 2:
                        act.wait_ge(m_p, (0, 0, 4, 8)[v])
                    nc.scalar.activation(hid[v % 2][:, j, :], bank[n % 4][:, :], ACT.Gelu, bias=b1[:, j:j + 1],
                                         scale=1.0).then_inc(h_c, 1)
                    n += 1

        @block.tensor
        def _(pe):
            mm = nc.tensor.matmul
            pe.wait_ge(d_w, 16 * NW)
            pe.wait_ge(wrs, 1)
            for k in range(3):
                for j in range(2):
                    for e in range(2):
                        last = nc.tensor.transpose(bank[k][:, j * E + e * HC:j * E + (e + 1) * HC],
                                                   wr[:, e, (2 * k + j) * 128:(2 * k + j + 1) * 128], ident[0:HC, 0:HC])
                last.then_inc(wrt_p, 1)
            for e in range(2):
                last = nc.tensor.transpose(bank[3][0:1, e * HC:(e + 1) * HC], wrb[:, e:e + 1], ident[0:HC, 0:HC])
            last.then_inc(wrt_p, 1)
            pe.wait_ge(wrt_c, 6)
            pe.wait_ge(wprep, 1)

            def xt(t):
                for k in range(2):
                    if t >= 2:
                        pe.wait_ge(xt_c, 2 * (t - 2) + k + 1)
                    for j in range((4, 2)[k]):
                        m = 4 * k + j
                        last = nc.tensor.transpose(bank[2 * (t % 2) + k][:, j * 128:(j + 1) * 128],
                                                   xst[:, t, m * 128:(m + 1) * 128], ident[:, :])
                    last.then_inc(xt_p, 1)

            pe.wait_ge(d_x, 64)
            xt(0)
            for t in range(NT):
                if t + 1 < NT:
                    xt(t + 1)
                pe.wait_ge(xt_c, 2 * t + 2)
                if t >= 4:
                    pe.wait_ge(tk_c, t - 3)
                o = bank[4 + t % 4][:, 0:E]
                mm(o, ones[:, :], brow[:, 0, :], start=True, stop=False)
                for m in range(6):
                    last = mm(o, xsT[t % 2][:, m, :], wrT[:, m, :], start=False, stop=(m == 5))
                last.then_inc(tk_p, 1)

            def transposed(n, free):
                for t in range(NT):
                    pe.wait_ge(ln_x, free[0] + t + 1)
                    if t >= 4:
                        pe.wait_ge(ln_tc, 2 * (n * NT + t - 4) + 2)
                    for k in range(2):
                        last = nc.tensor.transpose(bank[t % 4][0:HC, k * 128:(k + 1) * 128],
                                                   xn[:, t, k * HC:(k + 1) * HC], ident[:, :])
                    last.then_inc(ln_tp, 1)

            def attention(at, n_tc):
                w = wqkv[at]
                pe.wait_ge(ln_tc, n_tc)
                for m in range(4):
                    for hf in range(2):
                        n = 2 * m + hf
                        if n >= 4:
                            pe.wait_ge(qk_c, 8 * at + n - 3)
                        for k in range(2):
                            last = mm(bank[4 + n % 4][0:HC, :], w[:, k, m * HC:(m + 1) * HC],
                                      xT[:, k, 512 * hf:512 * hf + 512], start=(k == 0), stop=(k == 1))
                        last.then_inc(qk_p, 1)
                for i in range(NT):
                    if i >= 4:
                        pe.wait_ge(v_c, NT * at + i - 3)
                    for s in range(2):
                        o = bank[i % 4][0:64, s * E:(s + 1) * E]
                        for k in range(2):
                            last = mm(o, xT[:, k, i * 128 + 64 * s:i * 128 + 64 * s + 64], w[:, k, 2 * E:3 * E],
                                      start=(k == 0), stop=(at == 1 and k == 1))
                        if at == 0:
                            last = mm(o, ones[:, 0:64], vb[:, :], start=False, stop=True)
                    last.then_inc(v_p, 1)

                def scores(t):
                    n = at * NT + t
                    pe.wait_ge(kb_r, n + 1)
                    if n >= 2:
                        pe.wait_ge(sc_r, n - 1)
                    for k in range(2):
                        for i in range(2):
                            last = mm(bank[2 * (n % 2) + k][64 * i:64 * i + 64, 0:HT * TI],
                                      qkT[:, k, t * 128 + 64 * i:t * 128 + 64 * i + 64],
                                      kb[n % 2][:, i, k, :, :].rearrange("p a b -> p (a b)"), start=True, stop=True)
                    last.then_inc(sc_p, 1)

                pe.wait_ge(qk_c, 8 * at + 8)
                pe.wait_ge(v_c, NT * (at + 1))
                scores(0)
                for t in range(NT):
                    n = at * NT + t
                    if t + 1 < NT:
                        scores(t + 1)
                    pe.wait_ge(ex, n + 1)
                    for k in range(3):
                        for j in range(4):
                            last = nc.tensor.transpose(bank[4 + k][0:TI, j * 128:(j + 1) * 128],
                                                       pr[n % 2][:, 4 * k + j, :], ident[:, :])
                        last.then_inc(pt_p, 1)
                    if n:
                        pe.wait_ge(o_c, n)
                    for hd in range(NH):
                        pe.wait_ge(pt_c, 3 * n + hd // 4 + 1) if hd % 4 == 0 else None
                        for i in range(2):
                            last = mm(bank[7][64 * i:64 * i + 64, hd * HS:(hd + 1) * HS], pT[:, hd, 64 * i:64 * i + 64],
                                      vt[0:TI, 2 * t + i, hd * HS:(hd + 1) * HS], start=True, stop=True)
                    last.then_inc(y_p, 1)
                    pe.wait_ge(y_c, n + 1)
                    for k in range(2):
                        last = nc.tensor.transpose(bank[7][0:HC, k * 128:(k + 1) * 128], y[:, k * HC:(k + 1) * HC],
                                                   ident[:, :])
                    last.then_inc(yt_p, 1)
                    pe.wait_ge(yt_c, n + 1)
                    small = at == 1 and t >= NT // 2
                    wp = wpr[at + small]
                    o = bank[7][:, 256:256 + E]
                    mm(o, ones[:, :], brow[:, 1 + at + small, :], start=True, stop=False)
                    for k in range(2):
                        last = mm(o, yT[:, k, :], wp[:, k, :], start=False, stop=(k == 1))
                    last.then_inc(o_p, 1)

            pe.wait_ge(tk_c, NT)
            transposed(0, (0,))
            attention(0, 2 * NT)
            transposed(1, (2 * NT,))
            attention(1, 4 * NT)
            pe.wait_ge(o_c, 2 * NT)
            transposed(2, (3 * NT,))
            pe.wait_ge(ln_tc, 6 * NT)
            keep = (E, E, E // 2, E // 3)

            def hidden(v):
                for j in range(6):
                    n = 6 * v + j
                    if n >= 4:
                        pe.wait_ge(h_c, n - 3)
                    ks = [(k, min(HC, keep[v] - HC * k)) for k in range(2) if keep[v] > HC * k]
                    for x, (k, c) in enumerate(ks):
                        last = mm(bank[n % 4][:, :], w1[0:c, k, j * 128:(j + 1) * 128],
                                  xT[0:c, k, 512 * (v > 0):512 * (v > 0) + 512], start=(x == 0), stop=(x == len(ks) - 1))
                    last.then_inc(h_p, 1)

            def second(v):
                pe.wait_ge(h_c, 6 * v + 6)
                w = keep[v]
                for t in range(4):
                    o = bank[4 + t]
                    if v == 1:
                        pe.wait_ge(m_c, t + 1)
                    if v <= 1:
                        mm(o[:, 0:E], ones[:, :], brow2[:, v, :], start=True, stop=False, skip_group_check=True)
                    for j in range(6):
                        rhs = w2[:, j, :] if v == 0 else w2v[:, v - 1, j, 0:w]
                        last = mm(o[:, 0:w], hid[v % 2][:, j, t * 128:(t + 1) * 128], rhs, start=False,
                                  stop=(j == 5), skip_group_check=True)
                    last.then_inc(m_p, 1)

            hidden(0)
            for v in range(4):
                if v < 3:
                    hidden(v + 1)
                second(v)

        @block.vector
        def _(dve):
            v = nc.vector
            count = [0]

            def link(ins):
                count[0] += 1
                ins.then_inc(dch, 1)
                dve.wait_ge(dch, count[0])

            link(v.memset(wr[:, :, :], 0.0))
            dve.wait_ge(d_tl, 32)
            for e in range(2):
                T = tl[:, e].rearrange("p t (s x) -> p t s x", x=P)
                W = wr[:, e, :].rearrange("p (c r k x) -> p c r k x", c=C, k=2, x=P)
                for ky in range(3):
                    for kx in range(3):
                        for py in range(2):
                            d = py - ky + 1
                            half, off = (0, (d + 1) // 2) if d % 2 else (1, d // 2)
                            lo, hi = max(0, kx - 1), min(P, P + kx - 1)
                            row = 27 * half + 3 * ky + kx
                            o = W[:, :, :, py, lo:hi]
                            link(v.tensor_tensor(o, o, T[:, row:row + 19:9, off:off + 8, lo - kx + 1:hi - kx + 1], ALU.add))
            v.tensor_reduce(wrb[:, :], tl[:, :, TR - 1, :], AX.X, ALU.add).then_inc(wrs, 1)
            dve.wait_ge(d_w, 16 * NW)
            for i in range(3):
                v.tensor_scalar(w2v[:, i, :, :], w2[:, :, :], gw[:, i:i + 1], None, ALU.mult)
            link(v.memset(mrow[:, :], 0.0))
            for i, c in enumerate((E, E // 2, E // 3)):
                link(v.tensor_scalar(mrow[:, 0:c], mrow[:, 0:c], gw[0:1, i:i + 1], None, ALU.add))
            link(v.tensor_tensor(brow[:, 3, :], brow[:, 2, :], mrow[:, :], ALU.mult))
            link(v.tensor_tensor(brow2[:, 1, :], brow2[:, 0, :], mrow[:, :], ALU.mult))
            link(v.tensor_scalar(wpr[2][:, :, :], wpr[1][:, :, :], gw[0:HC, 0:1], None, ALU.mult))
            for i, c in ((1, HC), (2, E // 3)):
                link(v.scalar_tensor_tensor(wpr[2][0:c, 0, 0:c], wpr[1][0:c, 0, 0:c], gw[0:c, i:i + 1],
                                            wpr[2][0:c, 0, 0:c], ALU.mult, ALU.add))
            dve.wait_ge(wrt_p, 4)
            v.tensor_tensor(brow[:, 0, :], bank[3][0:1, 0:E], pjb[:, :], ALU.add).then_inc(wprep, 1)
            dve.wait_ge(d_x, 64)
            dve.wait_ge(zer, 4)
            for k in range(2):
                link(v.tensor_tensor(embt[:, :, :], embt[:, :, :], pos[:, k, :].unsqueeze(1).broadcast_to((128, NT, E)),
                                     ALU.add))
            for t in range(NT):
                dve.wait_ge(tk_p, t + 1)
                v.tensor_tensor(h[:, t, :], bank[4 + t % 4][:, 0:E], embt[:, t, :], ALU.add).then_inc(tk_c, 1)
            dve.wait_ge(tk_c, NT)

            ln = [0]

            def layernorm(src, dst, tiles_read):
                n = ln[0]
                ln[0] += 1
                for t in range(NT):
                    ins = v.bn_stats(st6[:, t, :], src[:, t, :])
                link(ins)
                for t in range(NT):
                    ins = v.bn_aggr(mv[:, t, :], st6[:, t, :])
                link(ins)
                v.tensor_scalar(ve[:, :], mv[:, :, 1], EPS, None, ALU.add).then_inc(ln_v, 1)
                dve.wait_ge(ln_r, n + 1)
                for t in range(NT):
                    v.tensor_scalar(dst[:, t, :], src[:, t, :], mv[:, t, 0:1], rs[:, t:t + 1], ALU.subtract,
                                    ALU.mult).then_inc(ln_x, 1)
                dve.wait_ge(ln_x, NT * (n + 1))

            def attention(at):
                def soft(t):
                    n = at * NT + t
                    dve.wait_ge(sc_p, n + 1)
                    if n >= 2:
                        dve.wait_ge(pt_p, 3 * (n - 1))
                    p = pr[n % 2]
                    for k in range(2):
                        src = bank[2 * (n % 2) + k][:, 0:HT * TI].rearrange("p (a b) -> p a b", a=HT)
                        dst = p[:, HT * k:HT * k + HT, :]
                        if at == 0:
                            ins = v.tensor_tensor(dst, src, causal[:, :].unsqueeze(1).broadcast_to((128, HT, TI)), ALU.add)
                        else:
                            ins = v.tensor_copy(dst, src)
                    link(ins)
                    link(v.tensor_reduce(mx[n % 2][:, :], p[:, :, :], AX.X, ALU.max))
                    v.tensor_tensor(p[:, :, :], p[:, :, :], mx[n % 2][:, :].unsqueeze(2).broadcast_to((128, NH, TI)),
                                    ALU.subtract).then_inc(sc_r, 1)

                soft(0)
                for t in range(NT):
                    n = at * NT + t
                    if t + 1 < NT:
                        soft(t + 1)
                    dve.wait_ge(ex, n + 1)
                    link(v.tensor_reduce(sm[n % 2][:, :], pr[n % 2][:, :, :], AX.X, ALU.add))
                    link(v.reciprocal(ri[n % 2][:, :], sm[n % 2][:, :]))
                    dve.wait_ge(y_p, n + 1)
                    v.tensor_tensor(y[:, :].rearrange("p (a b) -> p a b", a=NH),
                                    bank[7][:, 0:E].rearrange("p (a b) -> p a b", a=NH),
                                    ri[n % 2][:, :].unsqueeze(2).broadcast_to((128, NH, HS)), ALU.mult).then_inc(y_c, 1)
                    dve.wait_ge(o_p, n + 1)
                    v.tensor_tensor(h[:, t, :], h[:, t, :], bank[7][:, 256:256 + E], ALU.add).then_inc(o_c, 1)
                dve.wait_ge(o_c, NT * (at + 1))

            layernorm(h, xn, 0)
            attention(0)
            layernorm(h, x2, 0)
            link(v.tensor_copy(h1[:, :, :], h[:, :, :]))
            link(v.tensor_copy(h[:, :, :], x2[:, :, :]))
            layernorm(h, xn, 0)
            attention(1)
            layernorm(h, xn, 0)
            link(v.tensor_tensor(h1[:, :, :], h1[:, :, :], h[:, :, :], ALU.add))
            for half in range(2):
                for t in range(4):
                    dve.wait_ge(m_p, t + 1 if half == 0 else 12 + t + 1)
                    n = 4 * half + t
                    v.tensor_tensor(h[:, n, :], h1[:, n, :], bank[4 + t][:, 0:E], ALU.add).then_inc(m_c, 1)


def build_program(nc, a, out):
    emb = nc.dram_tensor("scratch_emb", (NPAT, E), F32).ap()
    xs = nc.dram_tensor("scratch_x", (NPAT, C * P * P), F32).ap()
    ts = nc.dram_tensor("scratch_fold", (E, TR, SL * P), F32).ap()
    build_front(nc, a, emb, xs, ts)
    build_tail(nc, a, emb, xs, ts, out)


def layout(inp):
    o = {}
    tokp = {k[7:]: v for k, v in inp.items() if k.startswith("L0_tok_")}
    o["x"] = inp["x"].reshape(B, C, HP, P, HP, P).transpose(1, 0, 2, 4, 3, 5).reshape(C, ROWS, HP, P * P)
    names = ("conv1_b", "gn1_g", "gn1_b", "rconv1_b", "gn2_g", "gn2_b", "rconv2_b")
    o["params"] = np.stack([np.concatenate([tokp[n], tokp[n]]) for n in names], 1)
    r1 = tokp["rconv1_w"].transpose(1, 2, 3, 0)
    r2 = tokp["rconv2_w"].transpose(0, 2, 3, 1)
    rb, fb = np.zeros((2, CH, 2, 3, 2, CH), r1.dtype), np.zeros((2, CH, 2, 3, 2, CH), r1.dtype)
    for slot, hin, hout, ky in ((0, 0, 1, 0), (0, 1, 0, 0), (0, 1, 1, 1), (1, 0, 0, 1), (1, 0, 1, 2), (1, 1, 0, 2)):
        rb[hin, :, slot, :, hout] = r1[:, ky]
        fb[hin, :, slot, :, hout] = r2[:, 2 - ky, ::-1]
    o["rbands"], o["fbands"] = rb.reshape(128, 768), fb.reshape(128, 768)
    w1 = tokp["conv1_w"]
    tb = np.zeros((2, CH, TR), w1.dtype)
    for half in range(2):
        tb[half, :, 27 * half:27 * half + 27] = w1.reshape(CH, 27)
    o["tband"] = tb.reshape(128, TR)
    wb = np.zeros((KC, 2, CH), w1.dtype)
    for kx in range(3):
        for c in range(C):
            for dy in range(4):
                par, up = dy % 2, dy // 2
                rows = [kx * 24 + (6 * k + 2 * c + par) * 2 + up for k in range(2)] + [KA + kx * 12 + (2 * c + par) * 2 + up]
                for half in range(2):
                    if 0 <= dy - half <= 2:
                        wb[rows, half] = w1[:, c, dy - half, kx]
    o["w1band"] = wb.reshape(KC, 128)
    i = (np.arange(128) % CH) // 2
    o["grp"] = ((i[:, None] == i[None, :]) / 8.0).astype(np.float32)
    pw = np.zeros((2, CH, E, SL, P), tokp["proj_w"].dtype)
    w = tokp["proj_w"].transpose(1, 0, 2, 3)
    pw[0, :, :, 1:9], pw[1, :, :, 0:8] = w[:, :, 1::2], w[:, :, 0::2]
    o["proj"] = pw.reshape(128, E * DENSE)

    o["ident"] = np.eye(128, dtype=np.float32)
    o["hmask"] = ((np.arange(HC)[:, None] // HS == np.arange(HT)[None]) * HS ** -0.5).astype(np.float32)
    cm = np.zeros((2, 64, TI), np.float32)
    cm[:, :TI] = np.where(np.tril(np.ones((TI, TI), bool)), 0.0, LOWEST)
    o["causal"] = cm.reshape(128, TI)
    vocab = tokp["row_emb"].shape[0]
    at = []
    for k in range(HP):
        low = int(np.float32(k) / np.float32(HP) * np.float32(vocab))
        high = int(np.float32(k + 1) / np.float32(HP) * np.float32(vocab))
        at.append((low + high) // 2)
    pos = np.zeros((2, 64, 2, E), tokp["row_emb"].dtype)
    for r in range(HP):
        for c in range(HP):
            pos[:, r * HP + c, 0], pos[:, r * HP + c, 1] = tokp["row_emb"][at[r]], tokp["col_emb"][at[c]]
    o["pos"] = pos.reshape(128, 2, E)
    o["proj_b"] = tokp["proj_b"][None]
    o["wqkv1"], o["wproj1"] = inp["L0_attn_Wqkv"], inp["L0_attn_Wproj"]
    o["qkb"] = inp["L0_attn_bqkv"][:2 * E].reshape(4, HC).T
    o["vb"] = inp["L0_attn_bqkv"][2 * E:][None]
    f = {k[7:]: v for k, v in inp.items() if k.startswith("L0_ffn_")}
    o["wqkv2"], o["wproj2"] = f["w_qkv"], f["w_proj"]
    ln = [f[k] for k in ("n1l_g", "n1l_b", "n1s_g", "n1s_b", "n2l_g", "n2l_b", "n2s_g", "n2s_b")]
    o["lnp"] = np.stack(ln, 1).reshape(2, HC, 8).transpose(1, 0, 2)
    o["w1"], o["w2"] = f["w_fc1"], f["w_fc2"]
    o["b1"] = f["b_fc1"].reshape(6, 128).T
    o["b2"] = f["b_fc2"][None]
    o["gw"] = np.tile(f["gumbel_weights"], (128, 1))
    o["brow"] = np.stack([inp["L0_attn_bproj"], f["b_proj"]])[None]
    return o


def kernel(**inputs):
    import numpy as _np
    import concourse.bacc as _bacc
    from concourse.bass_utils import run_bass_kernel_spmd as _run

    arr = layout({k: _np.asarray(v) for k, v in inputs.items()})
    nc = _bacc.Bacc("TRN2", target_bir_lowering=False, num_devices=1)
    arrays, a = {}, {}
    for name, v in arr.items():
        v = _np.ascontiguousarray(v)
        arrays[f"in_{name}"] = v
        a[name] = nc.dram_tensor(f"in_{name}", v.shape, mybir.dt.from_np(v.dtype), kind="ExternalInput").ap()
    out = nc.dram_tensor("out_tokens", (B, TI, E), F32, kind="ExternalOutput").ap()
    build_program(nc, a, out)
    r = _run(nc, [arrays], core_ids=[0])
    return r.results[0]["out_tokens"]
```

```python
import concourse.bass as bass
from concourse import mybir
from contextlib import ExitStack
import numpy as np

F32, F16 = mybir.dt.float32, mybir.dt.float16
ALU, ACT = mybir.AluOpType, mybir.ActivationFunctionType

B, C, P, CH, E = 16, 3, 16, 64, 192
HP = 7
ROWS = B * HP
NPAT = ROWS * HP
SL, WD = 9, 18
PAD = SL * WD
HALF = 8 * P
U = 8
Q = 4
UNITS = NPAT // U
GU = 14
GROUPS = UNITS // GU
G = GU * U
FU = E // U
RUN = (U - 1) * PAD + 8 * WD + P
PLANE = (NPAT + 2 * U + 1) * PAD
KA, KC = 72, 108
WS = 64.0
EPS = 1e-5
TR = 55


DENSE = SL * P
NCH = 6
CHN = [22, 22, 21, 21, 21, 21]
CHS = [sum(CHN[:c]) for c in range(NCH)]
WCH = max(CHN)
W_READY = 9


class Chain:

    def __init__(self, eng, sem, base):
        self.eng, self.sem, self.at = eng, sem, base

    def did(self, ins):
        ins.then_inc(self.sem, 1)
        self.at = self.at + 1

    def wait(self):
        self.eng.wait_ge(self.sem, self.at)


def build_front(nc, a, emb, xs, ts, wrd):
    scr = nc.dram_tensor("x_planes", (12, PLANE), F16)
    wlod = nc.dram_tensor("w_lo", (128, HALF * E), F16)
    with ExitStack() as ctx:
        def sb(name, shape, dt=F32):
            return ctx.enter_context(nc.sbuf_tensor("sb_" + name, shape, dt))

        def sem(name):
            return ctx.enter_context(nc.semaphore(name))

        whi = sb("whi", [128, HALF, E], F16)
        wlo = sb("wlo", [128, 2, WCH, E], F16)
        arena = sb("arena", [128, 2, 2 * G * HALF], F16)
        g2 = arena[:, :, :].rearrange("p b (h g n) -> p b h g n", h=2, g=G)
        f32q = sb("f32q", [128, U * DENSE])
        g1f = f32q[:, 0:U * HALF].rearrange("p (g n) -> p g n", g=U)
        ghl = [sb(f"ghl_{i}", [128, 2, U * PAD], F16) for i in range(2)]
        g2f = sb("g2f", [128, U, HALF])
        im = [sb(f"im_{i}", [KC, U * PAD], F16) for i in range(2)]
        rws = sb("rws", [128, 2, 6, 128], F16)
        w1s = sb("w1s", [KC, 128], F16)
        grp = sb("grp", [128, 128])
        par = sb("par", [128, 7])
        N1, N2 = (0, 1), (2, 3)
        wide = (Q, Q, U, U)
        bn6 = [sb(f"bn6_{s}", [128, w, 6]) for s, w in enumerate(wide)]
        ms = [sb(f"ms_{s}", [128, 2, w, 2]) for s, w in enumerate(wide)]
        msq = [sb(f"msq_{s}", [128, w, 2]) for s, w in enumerate(wide)]
        mst = [sb(f"mst_{s}", [128, 2, w]) for s, w in enumerate(wide)]
        tmp = [sb(f"tmp_{s}", [128, 5, w]) for s, w in enumerate(wide)]
        gsc = [sb(f"gsc_{s}", [128, w]) for s, w in enumerate(wide)]
        gsh = [sb(f"gsh_{s}", [128, w]) for s, w in enumerate(wide)]
        wid = sb("wid", [128, 2, 3, U])
        zeros = sb("zeros", [128, U])
        half_neg = sb("half_neg", [128, U])
        half_pos = sb("half_pos", [128, 21])
        tok = sb("tok", [G, E])

        COL = TR // C * DENSE
        b1f = arena[0:E // 2, 1, :].bitcast(F32)
        NTC = 5
        tc_ = [b1f[:, i * COL:(i + 1) * COL].rearrange("p (t n) -> p t n", n=DENSE) for i in range(NTC)]
        tbias = b1f[:, NTC * COL:NTC * COL + 2 * DENSE].rearrange("p (e n) -> p e n", e=2)
        WR = C * P * P
        wr = [f32q[0:E // 2, 0:WR + 1], g2f[0:E // 2, :, :].rearrange("p a b -> p (a b)")[:, 0:WR + 1]]

        b0, b1 = arena[:, 0, :], arena[:, 1, :]
        n = 2 * C * 7 * 256
        xt = b0[0:ROWS, 0:n].bitcast(F32).rearrange("p (c w n) -> p c w n", c=C, w=7)
        xhl = b0[0:ROWS, n:n + 12 * 7 * PAD].rearrange("p (q n) -> p q n", q=12)
        n += 12 * 7 * PAD
        fws = b0[:, n:n + 1536].rearrange("p (h t m) -> p h t m", h=2, t=6)
        n += 1536
        tws = b0[:, n:n + 2 * TR].rearrange("p (h m) -> p h m", h=2)
        n += 2 * TR
        w1hl = b0[0:KC, n:n + 256].rearrange("p (h m) -> p h m", h=2)
        n += 256
        zt = b0[0:12, n:n + U * PAD]
        wlst = b1[:, 0:HALF * E].rearrange("p (n e) -> p n e", n=HALF)
        stage = [f32q[:, :], b1[:, HALF * E:HALF * E + 2 * U * DENSE].bitcast(F32)]
        wv = wlo[0:TR, :, :, :].rearrange("p a b c -> p (a b c)").bitcast(F32)
        tev = [wv[:, i * U * DENSE:(i + 1) * U * DENSE].rearrange("p (e n) -> p e n", e=U) for i in range(2)]
        wst = whi[:, 0:24, :].rearrange("p a c -> p (a c)").bitcast(F32)
        rst32, fst32 = wst[:, 0:768], wst[:, 768:1536]
        tst32, w1st32 = wst[:, 1536:1536 + TR], wst[0:KC, 1600:1728]
        xsm = g2f[0:ROWS, :, :].rearrange("p a b -> p (a b)")
        x6 = xsm[:, 0:126].rearrange("p (k n) -> p k n", n=6)
        xmv = xsm[:, 126:168].rearrange("p (k n) -> p k n", n=2)
        xsd = xsm[:, 168:231].rearrange("p (k n) -> p k n", k=3)

        rc = [[ctx.enter_context(nc.psum_tensor(f"rc{i}{q}", [128, 512], F32)) for q in range(2)] for i in range(2)]
        c1 = [ctx.enter_context(nc.psum_tensor(f"c1_{q}", [128, 512], F32)) for q in range(2)]
        pj = ctx.enter_context(nc.psum_tensor("pj", [128, 512], F32))
        st = ctx.enter_context(nc.psum_tensor("st", [128, 512], F32))

        s_wld, s_xld, s_wprep, s_w1s = sem("weights_loaded"), sem("x_loaded"), sem("weights_prepared"), sem("w1_placed")
        s_cst, s_xvar, s_xstd, s_xz, s_xhl, s_xch = (sem("constants"), sem("x_var"), sem("x_std"), sem("x_zeroed"),
                                               sem("x_split"), sem("x_chain"))
        s_scr, s_zero, s_padz = sem("x_stored"), sem("zero_tile"), sem("pads_zeroed")
        s_wid = sem("parameters_widened")
        s_pld = [sem(f"proj_loaded{i}") for i in range(2)]
        s_psp, s_fold, s_tps = sem("proj_split"), sem("fold_done"), sem("t_done")
        s_whi, s_wlo, s_tev = sem("w_hi"), sem("w_lo_done"), sem("t_evacuated")
        s_ts = [sem(f"t_stored{i}") for i in range(2)]
        s_wst = sem("w_lo_stored")
        s_wch = [sem(f"w_chunk{i}") for i in range(2)]
        s_im = [sem(f"im_loaded{i}") for i in range(2)]
        s_c1, s_rc = sem("conv1_done"), sem("rconv_done")
        s_ms, s_st, s_rd = ([sem(f"{n}{s}") for s in (1, 2)] for n in ("moments", "group_means", "means_read"))
        s_dch, s_pch, s_sh = ([sem(f"{n}{s}") for s in (1, 2)] for n in ("dve_chain", "pool_chain", "affine"))
        s_g1, s_sp1h, s_sp1 = sem("gelu1_done"), sem("split1_hi"), sem("split1_done")
        s_g2, s_sp2h, s_sp2 = sem("gelu2_done"), sem("split2_hi"), sem("split2_done")
        s_pc, s_pj, s_pjr, s_emb = sem("chunk_used"), sem("projected"), sem("tokens_out"), sem("emb_stored")

        s_tc, s_tb = [sem(f"fold_colour{i}") for i in range(NTC)], sem("fold_bias")
        s_tcd, s_wz, s_wr = sem("colour_summed"), sem("wr_sums"), sem("wr_stored")

        block = ctx.enter_context(nc.Block())

        def over_groups(eng, group):
            group(0, 0, True)
            with eng.Fori(0, (GROUPS - 1) // 2) as i:
                group(2 * i + 1, 1, False)
                group(2 * i + 2, 0, False)

        def slot2(j, p, q, old):
            return (2 * GU + 2 * p + q - 3) * Q if old else j * U * 2 + (2 * p + q - 3) * Q

        def over_units(eng, g, pair, first):
            pair(g * GU, 0, first)
            with eng.Fori(1, GU // 2) as j:
                pair(g * GU + 2 * j, j, False)

        @block.sync
        def _(sp):
            sp.dma_start(par[:, :], a["params"]).then_inc(s_wld, 16)
            sp.dma_start(rst32, a["rbands"]).then_inc(s_wld, 16)
            sp.dma_start(fst32, a["fbands"]).then_inc(s_wld, 16)
            sp.dma_start(tst32, a["tband"]).then_inc(s_wld, 16)
            sp.dma_start(w1st32, a["w1band"]).then_inc(s_wld, 16)
            sp.dma_start(grp[:, :], a["grp"]).then_inc(s_wld, 16)

            def load_proj(n, p):
                sp.dma_start(stage[p], a["proj"][:, bass.ds(n * (U * DENSE), U * DENSE)]).then_inc(s_pld[p], 16)

            load_proj(0, 0)
            load_proj(1, 1)
            sp.dma_start(xt, a["x"].rearrange("c p w n -> p c w n")).then_inc(s_xld, 16)
            sp.wait_ge(s_wprep, W_READY)
            sp.dma_start(w1s[0:KA, :], w1hl[0:KA, 0, :]).then_inc(s_w1s, 16)
            sp.dma_start(w1s[KA:KC, :], w1hl[KA:KC, 1, :]).then_inc(s_w1s, 16)

            def fold_io(i, p, last):
                n = 2 * i + p
                if not last:
                    sp.wait_ge(s_psp, 2 * n + 2)
                    load_proj(n + 2, p)
                sp.wait_ge(s_tev, 3 * n + 3)
                sp.dma_start(bass.AP(tensor=ts.tensor, offset=n * (U * TR * DENSE),
                                     ap=[[DENSE, TR], [TR * DENSE, U], [1, DENSE]]),
                             tev[p][:, :, :]).then_inc(s_ts[p], 16)

            with sp.Fori(0, 3) as i:
                for p in range(2):
                    fold_io(i, p, False)
            sp.wait_ge(s_xch, 42)
            for c in range(C):
                sp.dma_start(xs.rearrange("(r w) (c n) -> r c w n", w=7, c=C)[:, c], xt[:, c]).then_inc(s_scr, 16)
            sp.wait_ge(s_xhl, 13)
            for h in range(2):
                sp.dma_start(bass.AP(tensor=scr, offset=h * 6 * PLANE, ap=[[7 * PAD, ROWS], [PLANE, 6], [1, 7 * PAD]]),
                             xhl[:, 6 * h:6 * h + 6, :]).then_inc(s_scr, 16)
            sp.wait_ge(s_zero, 1)
            for n, k in ((NPAT, U), (NPAT + U, U), (NPAT + 2 * U, 1)):
                sp.dma_start(bass.AP(tensor=scr, offset=n * PAD, ap=[[PLANE, 12], [1, k * PAD]]),
                             zt[:, 0:k * PAD]).then_inc(s_scr, 16)
            def load_im(u, p):
                for kx in range(3):
                    sp.dma_start(im[p][24 * kx:24 * kx + 24, 0:RUN],
                                 bass.AP(tensor=scr, offset=u * (U * PAD) + kx,
                                         ap=[[PLANE, 12], [WD, 2], [1, RUN]])).then_inc(s_im[p], 16)
                    sp.dma_start(im[p][KA + 12 * kx:KA + 12 * kx + 12, 0:RUN],
                                 bass.AP(tensor=scr, offset=u * (U * PAD) + kx,
                                         ap=[[PLANE, 6], [WD, 2], [1, RUN]])).then_inc(s_im[p], 16)

            with sp.Fori(3, FU // 2 - 1) as i:
                for p in range(2):
                    fold_io(i, p, False)
            sp.wait_ge(s_scr, 16 * 8)
            load_im(0, 0)
            load_im(1, 1)
            for p in range(2):
                fold_io(FU // 2 - 1, p, True)
            sp.wait_ge(s_wlo, 2 * FU)
            sp.dma_start(wlod.ap(), b1[:, 0:HALF * E]).then_inc(s_wst, 16)
            sp.sem_inc(s_emb, 16)

            def load_chunk(g, c):
                sp.wait_ge(s_pc, (g - 1) * NCH + c + 1)
                sp.dma_start(wlo[:, c % 2, 0:CHN[c], :].rearrange("p n e -> p (n e)"),
                             wlod.ap()[:, CHS[c] * E:(CHS[c] + CHN[c]) * E]).then_inc(s_wch[c % 2], 16)

            def group(g, b, first):
                if not first:
                    sp.wait_ge(s_wst, 16)
                for j in range(GU // 2):
                    for p in range(2):
                        u = g * GU + 2 * j + p
                        sp.wait_ge(s_c1, 2 * u + 3)
                        load_im(u + 2, p)
                    if not first and j < NCH:
                        load_chunk(g, j)
                if not first:
                    sp.wait_ge(s_pjr, g + 1)
                    sp.dma_start(emb[bass.ds((g - 1) * G, G), :], tok[:, :]).then_inc(s_emb, 16)

            over_groups(sp, group)

            def load_colour(m):
                c, e = m // 2, m % 2
                for half in range(2):
                    n = 27 * half + 9 * c
                    sp.dma_start(tc_[m % NTC][:, 9 * half:9 * half + 9, :].rearrange("p t n -> p (t n)"),
                                 ts[e * (E // 2):(e + 1) * (E // 2), n:n + 9, :].rearrange("e t n -> e (t n)")
                                 ).then_inc(s_tc[m % NTC], 16)

            sp.wait_ge(s_ts[0], 16 * (FU // 2))
            sp.wait_ge(s_ts[1], 16 * (FU // 2))
            load_chunk(GROUPS, 0)
            load_chunk(GROUPS, 1)
            for e in range(2):
                sp.dma_start(tbias[:, e, :], ts[e * (E // 2):(e + 1) * (E // 2), TR - 1, :]).then_inc(s_tb, 16)
            for m in range(4):
                load_colour(m)
            load_chunk(GROUPS, 2)
            load_colour(4)
            load_chunk(GROUPS, 3)
            sp.wait_ge(s_tcd, 1)
            load_colour(5)
            for c in range(4, NCH):
                load_chunk(GROUPS, c)
            sp.wait_ge(s_tcd, C)
            for e in range(2):
                sp.dma_start(wrd[e * (E // 2):(e + 1) * (E // 2), :], wr[e]).then_inc(s_wr, 16)
            sp.wait_ge(s_pjr, GROUPS + 1)
            sp.dma_start(emb[(GROUPS - 1) * G:NPAT, :], tok[:, :]).then_inc(s_emb, 16)
            sp.wait_ge(s_emb, 16 * GROUPS + 16)
            sp.wait_ge(s_wr, 32)

        @block.gpsimd
        def _(pool):
            gp = nc.gpsimd
            gp.memset(half_neg[:, :], -0.5).then_inc(s_cst, 1)
            gp.memset(half_pos[:, :], 0.5).then_inc(s_cst, 1)
            gp.memset(zeros[:, :], 0.0).then_inc(s_cst, 1)
            gp.memset(zt, 0.0).then_inc(s_zero, 1)
            gp.memset(xhl.bitcast(F32), 0.0).then_inc(s_xz, 1)
            pool.wait_ge(s_cst, 3)
            pool.wait_ge(s_xvar, 1)
            gp.tensor_tensor(xsd[:, 1, :], xsd[:, 0, :], half_pos[0:ROWS, :], ALU.pow).then_inc(s_xstd, 1)

            def norm(stage_, s, n):
                w = wide[s]
                ch = Chain(pool, s_pch[stage_], n * 6)
                mean, sq, (t1, t2, t3, t4, t5) = mst[s][:, 0, :], mst[s][:, 1, :], (tmp[s][:, k, :] for k in range(5))
                bias, gam, bet = (wid[:, stage_, k, 0:w] for k in range(3))
                pool.wait_ge(s_rd[stage_], n + 2)
                ch.did(gp.tensor_tensor(t1, mean, mean, ALU.mult))
                ch.did(gp.tensor_tensor(t2, mean, bias, ALU.subtract))
                ch.wait()
                ch.did(gp.tensor_tensor(t3, sq, t1, ALU.subtract))
                ch.wait()
                ch.did(gp.tensor_tensor(t5, t3, half_neg[:, 0:w], ALU.pow))
                ch.wait()
                ch.did(gp.tensor_tensor(gsc[s][:, :], t5, gam, ALU.mult))
                ch.wait()
                ch.did(gp.tensor_tensor(t4, t2, gsc[s][:, :], ALU.mult))
                ch.wait()
                gp.tensor_tensor(gsh[s][:, :], bet, t4, ALU.subtract).then_inc(s_sh[stage_], 1)

            def pair(u0, j, first):
                for p in range(2):
                    u = u0 + p
                    norm(0, 0, 2 * u + 2)
                    if not (first and p == 0):
                        norm(1, N2[1 - p], u - 1)
                    norm(0, 1, 2 * u + 3)

            pool.wait_ge(s_padz, 3)
            norm(0, 0, 0)
            norm(0, 1, 1)
            over_groups(pool, lambda g, b, first: over_units(pool, g, pair, first))
            norm(1, N2[1], UNITS - 1)

        @block.scalar
        def _(act):
            def fold_step(i, p, first):
                n = 2 * i + p
                for q in range(2):
                    act.wait_ge(s_fold, 2 * n + q + 1)
                    nc.scalar.activation(whi[:, :, bass.ds(n * U + q * Q, Q)].rearrange("p n e -> p e n"),
                                         rc[p][q][:, :].rearrange("p (e n) -> p e n", e=Q),
                                         ACT.Copy, scale=1.0 / WS).then_inc(s_whi, 1)
                if not first:
                    act.wait_ge(s_ts[p], 16 * i)
                act.wait_ge(s_tps, n + 1)
                for k, bank in enumerate((c1[0], c1[1], pj)):
                    nc.scalar.activation(tev[p][:, :, 3 * P * k:3 * P * (k + 1)],
                                         bank[0:TR, 0:384].rearrange("p (e n) -> p e n", e=U),
                                         ACT.Copy, scale=1.0 / (WS * WS)).then_inc(s_tev, 1)

            act.wait_ge(s_wprep, W_READY)
            for p in range(2):
                fold_step(0, p, True)
            with act.Fori(1, FU // 2) as i:
                for p in range(2):
                    fold_step(i, p, False)

            def gelu1(k, q, guard=True):
                act.wait_ge(s_sh[0], k + 1)
                if guard:
                    act.wait_ge(s_sp1, k - 1)
                for m in range(Q):
                    ins = nc.scalar.activation(g1f[:, q * Q + m, :], c1[q][:, m * HALF:(m + 1) * HALF], ACT.Gelu,
                                               bias=gsh[q][:, m:m + 1], scale=gsc[q][:, m:m + 1])
                ins.then_inc(s_g1, 1)

            def gelu2_at(u, q, p):
                s = N2[p]
                act.wait_ge(s_sh[1], u + 1)
                act.wait_ge(s_sp2, 2 * u + q + 1)
                for m in range(Q):
                    ins = nc.scalar.activation(g2f[:, q * Q + m, :], rc[p][q][:, m * HALF:(m + 1) * HALF], ACT.Gelu,
                                               bias=gsh[s][:, q * Q + m:q * Q + m + 1],
                                               scale=gsc[s][:, q * Q + m:q * Q + m + 1])
                ins.then_inc(s_g2, 1)

            def hi2(u, q, buf, slot):
                act.wait_ge(s_g2, 2 * u + q + 5)
                nc.scalar.activation(g2[:, buf, 0, bass.ds(slot, Q), :], g2f[:, q * Q:q * Q + Q, :],
                                     ACT.Copy).then_inc(s_sp2h, 1)

            def group(g, b, first):
                def pair(u0, j, first, head):
                    for p in range(2):
                        u = u0 + p
                        for q in range(2):
                            gelu1(2 * u + 1 + q, 1 - q, not (first and p == 0 and q == 0))
                            if first and 2 * p + q < 3:
                                continue
                            if head and 2 * p + q == 3:
                                act.wait_ge(s_pj, 1 if first else g)
                            uu, qq, pp = (u - 2, 1, p) if q == 0 else (u - 1, 0, 1 - p)
                            gelu2_at(uu, qq, pp)
                            old = head and 2 * p + q < 3
                            hi2(uu, qq, 1 - b if old else b, slot2(j, p, q, old))

                pair(g * GU, 0, first, True)
                with act.Fori(1, GU // 2) as j:
                    pair(g * GU + 2 * j, j, False, False)

            act.sem_inc(s_g2, 4)
            gelu1(0, 0, False)
            group(0, 0, True)
            act.wait_ge(s_wst, 16)
            with act.Fori(0, (GROUPS - 1) // 2) as i:
                group(2 * i + 1, 1, False)
                group(2 * i + 2, 0, False)
            for k in range(2 * UNITS - 3, 2 * UNITS):
                gelu2_at(k // 2, k % 2, k // 2 % 2)
                hi2(k // 2, k % 2, 0, (2 * GU + k - 2 * UNITS) * Q)

        @block.tensor
        def _(pe):
            def bands(out, w, buf, q):
                v = buf[:, :, :].rearrange("p h (g r w) -> p h g r w", g=U, r=SL)
                n = 0
                for t in range(2):
                    for m in range(3):
                        for wp, xp in ((0, 0), (0, 1), (1, 0)):
                            last = nc.tensor.matmul(out, w[:, wp, 3 * t + m, :],
                                                    v[:, xp, q * Q:q * Q + Q, t:t + 8, m:m + P],
                                                    start=(n == 0), stop=(n == 17))
                            n += 1
                            yield last

            def run(gen, count=None):
                last = None
                for k, last in enumerate(gen):
                    if count is not None and k + 1 == count:
                        break
                return last

            def fold_step(i, p, first):
                n = 2 * i + p
                pe.wait_ge(s_psp, 2 * n + 2)
                for q in range(2):
                    if not first:
                        pe.wait_ge(s_wlo, 2 * (n - 2) + q + 1)
                    run(bands(rc[p][q][:, :], fws, ghl[p], q)).then_inc(s_fold, 1)
                if not (first and p == 0):
                    pe.wait_ge(s_tev, 3 * n)
                v = ghl[p][:, :, :].rearrange("p h (g r w) -> p h g r w", g=U, r=SL)
                for k, bank in enumerate((c1[0], c1[1], pj)):
                    for m, (wp, xp) in enumerate(((0, 0), (0, 1), (1, 0))):
                        last = nc.tensor.matmul(bank[0:TR, 0:384], tws[:, wp, :], v[:, xp, :, 3 * k:3 * k + 3, 1:17],
                                                start=(m == 0), stop=(m == 2))
                last.then_inc(s_tps, 1)

            pe.wait_ge(s_wprep, W_READY)
            for p in range(2):
                fold_step(0, p, True)
            with pe.Fori(1, FU // 2) as i:
                for p in range(2):
                    fold_step(i, p, False)

            def conv1(q, p):
                v = im[p][:, :].rearrange("p (g r w) -> p g r w", g=U, r=SL)
                nc.tensor.matmul(c1[q][:, :], w1s[:, :], v[:, q * Q:q * Q + Q, 0:8, 0:P], start=True, stop=True)
                nc.tensor.matmul(c1[q][0:CH, :].rearrange("p (g n) -> p g n", g=Q)[:, :, 0:P], w1s[:, 0:CH],
                                 v[:, q * Q:q * Q + Q, 8, 0:P], start=True, stop=True).then_inc(s_c1, 1)

            def means(stage_, s, n, other):
                pe.wait_ge(s_ms[stage_], n + 1)
                pe.wait_ge(s_rd[stage_], n + 1)
                pe.wait_ge(s_rd[1 - stage_], other + 1)
                nc.tensor.matmul(st[:, 0:4 * wide[s]], grp[:, :], ms[s][:, :, :, :].rearrange("p a b k -> p (a b k)"),
                                 start=True, stop=True).then_inc(s_st[stage_], 1)

            def project(b, n0, n1):
                for n in range(n0, n1):
                    c = max(k for k in range(NCH) if CHS[k] <= n)
                    yield nc.tensor.matmul(pj[0:G, 0:E], g2[:, b, 0, :, n], whi[:, n, :], start=(n == 0), stop=False)
                    yield nc.tensor.matmul(pj[0:G, 0:E], g2[:, b, 0, :, n], wlo[:, c % 2, n - CHS[c], :], start=False, stop=False)
                    yield nc.tensor.matmul(pj[0:G, 0:E], g2[:, b, 1, :, n], whi[:, n, :], start=False, stop=(n == HALF - 1))

            def chunk_waits(g, c):
                if c == 0:
                    pe.wait_ge(s_sp2, 2 * GU * g + 2)
                    pe.wait_ge(s_pjr, g)
                pe.wait_ge(s_wch[c % 2], 16 * ((NCH // 2) * (g - 1) + c // 2 + 1))

            def emit(u, q, p, g, b, first, im_count, s_idx=None):
                k2 = not (first and p == 0)
                pe.wait_ge(s_sp1, 2 * u + q + 1)
                pe.wait_ge(s_g2, 2 * u + q + 1)
                conv = bands(rc[p][q][:, :], rws, ghl[p], q)
                proj, c, part = iter(()), 0, 0
                if s_idx is not None and s_idx >= 4:
                    c, part = divmod(s_idx - 4, 4)
                    if part == 0:
                        chunk_waits(g, c)
                    lo, hi = (CHS[c] + (CHN[c] * (part + x)) // 4 for x in range(2))
                    proj = project(1 - b, lo, hi)
                run(conv, 8)
                means(0, N1[q], 2 * u + q + 2, u - (q == 0) if k2 else 0)
                last = run(proj)
                if last is not None and part == 3:
                    last.then_inc(s_pj if c == NCH - 1 else s_pc, 1)
                    if c == NCH - 1:
                        pe.sem_inc(s_pc, 1)
                run(conv, 4)
                if q == 1:
                    pe.wait_ge(s_im[p], im_count)
                pe.wait_ge(s_g1, 2 * u + q + 2)
                conv1(1 - q, 1 - p if q == 0 else p)
                run(conv, 3)
                if q == 0 and k2:
                    means(1, N2[1 - p], u - 1, 2 * u + q + 3)
                run(conv).then_inc(s_rc, 1)

            def group0(g, b, first):
                def pair(u0, j, first):
                    for p in range(2):
                        for q in range(2):
                            emit(u0 + p, q, p, 0, 0, first, 96 * (j + 2))
                over_units(pe, 0, pair, True)

            def group(g, b, first):
                if first:
                    return group0(g, b, first)
                for j in range(GU // 2):
                    for p in range(2):
                        for q in range(2):
                            emit(g * GU + 2 * j + p, q, p, g, b, False, 96 * (g * (GU // 2) + j + 2), 4 * j + 2 * p + q)

            pe.sem_inc(s_c1, 1)
            pe.sem_inc(s_pc, 2)
            pe.sem_inc(s_pj, 1)
            pe.wait_ge(s_w1s, 32)
            pe.wait_ge(s_im[0], 96)
            pe.wait_ge(s_tev, 3 * FU)
            pe.wait_ge(s_wlo, 2 * FU)
            conv1(0, 0)
            conv1(1, 0)
            means(0, 0, 0, 0)
            means(0, 1, 1, 0)
            pe.wait_ge(s_im[1], 96)
            pe.wait_ge(s_g1, 1)
            conv1(0, 1)
            over_groups(pe, group)
            means(1, N2[1], UNITS - 1, 2 * UNITS + 2)
            for c in range(NCH):
                chunk_waits(GROUPS, c)
                last = run(project(0, CHS[c], CHS[c] + CHN[c]))
                last.then_inc(s_pj if c == NCH - 1 else s_pc, 1)

        @block.vector
        def _(dve):
            v = nc.vector
            for p in range(2):
                v.memset(ghl[p][:, :, :].rearrange("p a b -> p (a b)").bitcast(F32), 0.0).then_inc(s_padz, 1)
            dve.wait_ge(s_wld, 16 * 6)
            v.tensor_tensor(tst32[:, TR - 1:TR], par[:, 0:1], par[:, 6:7], ALU.add).then_inc(s_wprep, 1)
            dve.wait_ge(s_wprep, 1)
            n = 1
            for src, dst in ((rst32, rws), (fst32, fws), (tst32, tws), (w1st32, w1hl)):
                hi, lo = (dst[:, k].rearrange("p a b -> p (a b)") if len(dst.shape) == 4 else dst[:, k, :] for k in range(2))
                v.tensor_scalar(hi, src, WS, None, ALU.mult).then_inc(s_wprep, 1)
                dve.wait_ge(s_wprep, n + 1)
                v.scalar_tensor_tensor(lo, src, WS, hi, ALU.mult, ALU.subtract).then_inc(s_wprep, 1)
                n += 2
            assert n == W_READY

            def proj_split(i, p, first):
                n = 2 * i + p
                dve.wait_ge(s_pld[p], 16 * (i + 1))
                if not first:
                    dve.wait_ge(s_tps, n - 1)
                hi, lo = (ghl[p][:, h, :].rearrange("p (r w) -> p r w", w=WD)[:, :, 1:17] for h in range(2))
                src = stage[p].rearrange("p (r w) -> p r w", w=P)
                v.tensor_scalar(hi, src, WS, None, ALU.mult).then_inc(s_psp, 1)
                dve.wait_ge(s_psp, 2 * n + 1)
                v.scalar_tensor_tensor(lo, src, WS, hi, ALU.mult, ALU.subtract).then_inc(s_psp, 1)

            def w_lo(i, p):
                n = 2 * i + p
                for q in range(2):
                    dve.wait_ge(s_whi, 2 * n + q + 1)
                    sl = bass.ds(n * U + q * Q, Q)
                    v.scalar_tensor_tensor(wlst[:, :, sl].rearrange("p n e -> p e n"),
                                           rc[p][q][:, :].rearrange("p (e n) -> p e n", e=Q), 1.0 / WS,
                                           whi[:, :, sl].rearrange("p n e -> p e n"), ALU.mult,
                                           ALU.subtract).then_inc(s_wlo, 1)

            dve.wait_ge(s_padz, 2)
            proj_split(0, 0, True)
            proj_split(0, 1, True)
            dve.wait_ge(s_xld, 16)
            for k in range(21):
                v.bn_stats(x6[:, k, :], xt[:, k // 7, k % 7, :]).then_inc(s_xch, 1)
            dve.wait_ge(s_xch, 21)
            for k in range(21):
                ins = v.bn_aggr(xmv[:, k, :], x6[:, k, :])
            ins.then_inc(s_xhl, 1)
            dve.wait_ge(s_xhl, 1)
            v.tensor_scalar(xsd[:, 0, :], xmv[:, :, 1], 256.0 / 255.0, None, ALU.mult).then_inc(s_xvar, 1)

            def fold_pair(i):
                w_lo(i, 0)
                proj_split(i + 1, 0, False)
                w_lo(i, 1)
                proj_split(i + 1, 1, False)

            fold_pair(0)
            dve.wait_ge(s_xstd, 1)
            v.tensor_scalar(xsd[:, 2, :], xsd[:, 1, :], 1e-6, float(P) ** 0.5, ALU.add, ALU.mult).then_inc(s_xvar, 1)
            dve.wait_ge(s_xvar, 2)
            v.reciprocal(xsd[:, 0, :], xsd[:, 2, :]).then_inc(s_xvar, 1)
            dve.wait_ge(s_xvar, 3)
            for k in range(21):
                t = xt[:, k // 7, k % 7, :]
                v.tensor_scalar(t, t, xmv[:, k, 0:1], xsd[:, 0, k:k + 1], ALU.subtract, ALU.mult).then_inc(s_xch, 1)
            fold_pair(1)
            dve.wait_ge(s_xch, 42)
            dve.wait_ge(s_xz, 1)
            for q in range(6):
                c, pr = q // 2, q % 2
                src = xt[:, c].rearrange("p w (r k j) -> p w r k j", k=2, j=P)[:, :, :, pr, :]
                dst = [xhl[:, 6 * h + q, :].rearrange("p (w r j) -> p w r j", w=7, r=SL)[:, :, 1:9, 1:17]
                       for h in range(2)]
                v.tensor_copy(dst[0], src).then_inc(s_xhl, 1)
                dve.wait_ge(s_xhl, 2 * q + 2)
                v.tensor_tensor(dst[1], src, dst[0], ALU.subtract).then_inc(s_xhl, 1)
            with dve.Fori(2, FU // 2 - 1) as i:
                fold_pair(i)
            for p in range(2):
                w_lo(FU // 2 - 1, p)
            one = zeros[:, :]
            dve.wait_ge(s_cst, 3)
            for s in range(2):
                v.tensor_scalar(wid[:, s, 0, :], one, 0.0, par[:, 3 * s:3 * s + 1], ALU.mult, ALU.add)
                for k in (1, 2):
                    v.tensor_scalar(wid[:, s, k, :], one, 0.0, par[:, 3 * s + k:3 * s + k + 1], ALU.mult, ALU.add)
            v.tensor_scalar(par[:, 0:1], par[:, 0:1], WS, None, ALU.mult).then_inc(s_wid, 1)
            v.tensor_scalar(par[:, 3:4], par[:, 3:4], WS, None, ALU.mult).then_inc(s_wid, 1)
            dve.wait_ge(s_wid, 2)
            for s in range(2):
                ins = v.tensor_scalar(wid[:, s, 0, :], one, 0.0, par[:, 3 * s:3 * s + 1], ALU.mult, ALU.add)
            ins.then_inc(s_padz, 1)
            dve.wait_ge(s_tps, FU)
            dve.wait_ge(s_padz, 3)
            dve.wait_ge(s_scr, 16 * 8)
            v.sem_inc(s_rd[0], 1)
            v.sem_inc(s_rd[1], 1)
            v.sem_inc(s_pjr, 1)
            v.sem_inc(s_sp2, 2)

            def channel_stats(stage_, s, src, at):
                for m in range(Q):
                    v.bn_stats(bn6[s][:, at + m, :], src[:, m * HALF:(m + 1) * HALF]).then_inc(s_dch[stage_], 1)

            def moments(stage_, s, n0):
                ch = Chain(dve, s_dch[stage_], n0)
                ch.wait()
                b6 = bn6[s][:, :, :].rearrange("p g (e k) -> p g e k", e=2)
                ch.did(v.tensor_scalar(ms[s][:, 0, :, :], b6[:, :, :, 1], par[:, 3 * stage_:3 * stage_ + 1], None, ALU.add))
                ch.did(v.tensor_scalar(ms[s][:, 1, :, :], b6[:, :, :, 2], 2.0 / HALF, EPS * WS * WS, ALU.mult, ALU.add))
                dve.wait_ge(s_dch[stage_], ch.at - 1)
                ch.did(v.tensor_tensor(msq[s][:, :, :], ms[s][:, 0, :, :], ms[s][:, 0, :, :], ALU.mult))
                ch.wait()
                v.tensor_tensor(ms[s][:, 1, :, :], ms[s][:, 1, :, :], msq[s][:, :, :], ALU.add).then_inc(s_ms[stage_], 1)

            def read_means(stage_, s, n):
                dve.wait_ge(s_st[stage_], n + 1)
                v.tensor_reduce(mst[s][:, :, :], st[:, 0:4 * wide[s]].rearrange("p (a b k) -> p a b k", a=2, k=2),
                                mybir.AxisListType.X, ALU.add).then_inc(s_rd[stage_], 1)

            def split1(k, q, p):
                dve.wait_ge(s_g1, k + 1)
                src = g1f[:, q * Q:q * Q + Q, :].rearrange("p g (r w) -> p g r w", w=P)
                hi, lo = (ghl[p][:, h, :].rearrange("p (g r w) -> p g r w", g=U, r=SL)[:, q * Q:q * Q + Q, :, 1:17]
                          for h in range(2))
                parts = ((slice(0, 128), slice(1, 8), slice(1, 8)), (slice(0, 64), slice(8, 9), slice(0, 1)),
                         (slice(64, 128), slice(0, 1), slice(0, 1)))
                for half, to, at in parts:
                    ins = v.tensor_copy(hi[half, :, to, :], src[half, :, at, :])
                ins.then_inc(s_sp1h, 1)
                dve.wait_ge(s_sp1h, k + 1)
                for half, to, at in parts:
                    ins = v.tensor_tensor(lo[half, :, to, :], src[half, :, at, :], hi[half, :, to, :], ALU.subtract)
                ins.then_inc(s_sp1, 1)

            def split2(k, q, buf, slot):
                dve.wait_ge(s_sp2h, k + 1)
                src = g2f[:, q * Q:q * Q + Q, :]
                hi, lo = (g2[:, buf, h, bass.ds(slot, Q), :] for h in range(2))
                v.tensor_tensor(lo, src, hi, ALU.subtract).then_inc(s_sp2, 1)

            def group(g, b, first):
                def slot(u, q, p, j, head, first):
                    k = 2 * u + q
                    n2 = not (first and p == 0 and q == 0)
                    dve.wait_ge(s_c1, k + 4)
                    channel_stats(0, N1[q], c1[q], 0)
                    moments(0, N1[q], 7 * (k + 2) + 4)
                    if n2:
                        dve.wait_ge(s_rc, k)
                        if q == 1:
                            channel_stats(1, N2[p], rc[p][0], 0)
                        else:
                            channel_stats(1, N2[1 - p], rc[1 - p][1], Q)
                    read_means(0, N1[q], k + 2)
                    split1(k + 1, 1 - q, p if q == 0 else 1 - p)
                    if q == 0 and n2:
                        moments(1, N2[1 - p], 11 * (u - 1) + 8)
                    if not (first and p == 0) and not (first and p == 1 and q == 0):
                        old = head and 2 * p + q < 3
                        split2(k - 3, 1 - q, 1 - b if old else b, slot2(j, p, q, old))
                    if q == 0 and n2:
                        read_means(1, N2[1 - p], u - 1)

                def pair(u0, j, first, head):
                    for p in range(2):
                        for q in range(2):
                            if head and p == 1 and q == 1:
                                dve.wait_ge(s_pj, g if not first else 1)
                            slot(u0 + p, q, p, j, head, first)

                pair(g * GU, 0, first, True)
                with dve.Fori(1, GU // 2) as j:
                    pair(g * GU + 2 * j, j, False, False)

            def tokens(g):
                dve.wait_ge(s_pj, g + 2)
                dve.wait_ge(s_emb, 16 * g + 16)
                v.tensor_scalar(tok[:, :], pj[0:G, 0:E], 1.0 / WS, None, ALU.mult).then_inc(s_pjr, 1)

            dve.wait_ge(s_c1, 2)
            channel_stats(0, 0, c1[0], 0)
            moments(0, 0, 4)
            dve.wait_ge(s_c1, 3)
            channel_stats(0, 1, c1[1], 0)
            moments(0, 1, 11)
            read_means(0, 0, 0)
            read_means(0, 1, 1)
            split1(0, 0, 0)
            group(0, 0, True)
            dve.wait_ge(s_wst, 16)
            with dve.Fori(0, (GROUPS - 1) // 2) as i:
                group(2 * i + 1, 1, False)
                tokens(2 * i)
                group(2 * i + 2, 0, False)
                tokens(2 * i + 1)
            K = 2 * UNITS
            dve.wait_ge(s_rc, K)
            channel_stats(1, N2[1], rc[1][1], Q)
            moments(1, N2[1], 11 * (UNITS - 1) + 8)
            read_means(1, N2[1], UNITS - 1)
            for k in (K - 3, K - 2, K - 1):
                split2(k, k % 2, 0, (2 * GU + k - K) * Q)
            dve.wait_ge(s_pj, GROUPS)
            dve.wait_ge(s_sp1, K + 1)
            dve.wait_ge(s_sp2, K + 2)
            for e in range(2):
                v.memset(wr[e], 0.0).then_inc(s_wz, 1)
            n = 2
            for c in range(C):
                for m in (2 * c, 2 * c + 1):
                    dve.wait_ge(s_tc[m % NTC], 32 * (m // NTC + 1))
                for ky in range(3):
                    for kx in range(3):
                        for py in range(2):
                            d = py - ky + 1
                            half, off = (0, (d + 1) // 2) if d % 2 else (1, d // 2)
                            lo, hi = max(0, kx - 1), min(P, P + kx - 1)
                            for e in range(2):
                                T = tc_[(2 * c + e) % NTC].rearrange("p t (s x) -> p t s x", x=P)
                                o = wr[e][:, c * P * P:(c + 1) * P * P].rearrange("p (r k x) -> p r k x", k=2, x=P)
                                o = o[:, :, py, lo:hi]
                                dve.wait_ge(s_wz, n - 1)
                                v.tensor_tensor(o, o, T[:, 9 * half + 3 * ky + kx, off:off + 8, lo - kx + 1:hi - kx + 1],
                                                ALU.add).then_inc(s_wz, 1)
                                n += 1
                if c == 0:
                    dve.wait_ge(s_tb, 32)
                    for e in range(2):
                        v.tensor_reduce(wr[e][:, WR:WR + 1], tbias[:, e, :], mybir.AxisListType.X, ALU.add)
                dve.wait_ge(s_wz, n)
                v.sem_inc(s_tcd, 1)
            tokens(GROUPS - 1)


NT = 8
TI = HP * HP
NH, HS = 12, 16
HID = 4 * E
HC = E // 2
HT = NH // 2
NTOK = NT * 128
LOWEST = float(np.finfo(np.float32).min)


def build_tail(nc, a, emb, xs, wrd, out):
    with ExitStack() as ctx:
        def sb(name, shape, dt=F32):
            return ctx.enter_context(nc.sbuf_tensor("tl_" + name, shape, dt))

        def sem(name):
            return ctx.enter_context(nc.semaphore("t_" + name))

        ident = sb("ident", [128, 128])
        ones = sb("ones", [1, 128])
        khalf = sb("khalf", [128, NT])
        hmask = sb("hmask", [HC, HT])
        causal = sb("causal", [128, TI])
        pos = sb("pos", [128, 2, E])
        big = sb("big", [128, 10240 + 2 * NT * E])
        wr = sb("wr", [HC, 2, C * P * P + 1])
        wrT = sb("wrT", [128, 6, E])
        brow = sb("brow", [1, 4, E])
        brow2 = sb("brow2", [1, 2, E])
        mrow = sb("mrow", [1, E])
        pjb = sb("pjb", [1, E])
        embt = sb("embt", [128, NT, E])
        xst = sb("xst", [128, NT, C * P * P])
        xsT = [sb(f"xsT{i}", [128, 6, 128]) for i in range(2)]
        h = sb("h", [128, NT, E])
        xn = sb("xn", [128, NT, E])
        x2 = xst[:, :, 0:E]
        st6 = sb("st6", [128, NT, 6])
        mv = sb("mv", [128, NT, 2])
        ve = sb("ve", [128, NT])
        rs = sb("rs", [128, NT])
        xT = sb("xT", [HC, 2, NTOK])
        xTs = sb("xTs", [HC, 2, NTOK])
        qkT = big[0:HC, 6144:6144 + 4 * NTOK].rearrange("p (m n) -> p m n", m=4)
        vt = big[:, 10240:10240 + 2 * NT * E].rearrange("p (i j n) -> p i j n", j=HT, n=2 * HS)
        kb = [sb(f"kb{i}", [HC, 2, 2, HT, TI]) for i in range(2)]
        pr = [sb(f"pr{i}", [128, NH, 64]) for i in range(2)]
        mx = [sb(f"mx{i}", [128, NH]) for i in range(2)]
        sm = [sb(f"sm{i}", [128, NH]) for i in range(2)]
        ri = [sb(f"ri{i}", [128, NH]) for i in range(2)]
        pT = sb("pT", [128, HT, 128])
        y = sb("y", [128, E])
        yT = sb("yT", [HC, 2, 128])
        wqkv = [sb(f"wqkv{i}", [HC, 2, 3 * E]) for i in range(2)]
        wpr = [sb(f"wpr{i}", [HC, 2, E]) for i in range(3)]
        qb = sb("qb", [HC, 4])
        vb = sb("vb", [HC, 2])
        lnp = sb("lnp", [HC, 2, 8])
        w1 = sb("w1", [HC, 2, HID])
        b1 = sb("b1", [128, 6])
        w2 = sb("w2", [128, 6, E])
        w2v = sb("w2v", [128, 3, 6, E])
        gw = sb("gw", [128, 3])
        hid = [big[:, i * 3072:(i + 1) * 3072].rearrange("p (j n) -> p j n", j=6) for i in range(2)]

        bank = [ctx.enter_context(nc.psum_tensor(f"bank{i}", [128, 512], F32)) for i in range(8)]

        d_w, d_wb, d_tl, d_out = sem("weights"), sem("weights_of_branches"), sem("residual_weights"), sem("out")
        d_x = [sem(f"tokens{k}") for k in range(NT // 2)]
        zer = sem("zeroed")
        dch, pch = sem("dve_chain"), sem("pool_chain")
        wprep = sem("wprep")
        wrt_p, wrt_c = sem("wrT_psum"), sem("wrT_copied")
        AX = mybir.AxisListType
        xt_p, xt_c, tk_p, tk_c = sem("xT_psum"), sem("xT_copied"), sem("tok_psum"), sem("tok_done")
        ln_v, ln_r, ln_x = ([sem(f"{n}{k}") for k in range(4)] for n in ("ln_var", "ln_rstd", "ln_x"))
        ln_tp, ln_tc = sem("ln_t_psum"), sem("ln_t_copied")
        vz, prp, xch = sem("values_zeroed"), sem("gated_weights"), sem("images_exchanged")
        vbp, vbd = sem("value_bias_psum"), sem("value_bias_added")
        qk_p, qk_c, v_p, v_c = sem("qk_psum"), sem("qk_copied"), sem("v_psum"), sem("v_copied")
        kb_r, sc_p, sc_r, ex, pt_p, pt_c = (sem("kblocks"), sem("scores"), sem("scores_shifted"), sem("exp"),
                                           sem("pT_psum"), sem("pT_copied"))
        y_p, y_c, yt_p, yt_c, o_p, o_c = (sem("y_psum"), sem("y_done"), sem("yT_psum"), sem("yT_copied"),
                                          sem("o_psum"), sem("o_added"))
        h_p, h_c, m_p, m_c = sem("hid_psum"), sem("hid_gelu"), sem("mlp_psum"), sem("mlp_added")
        block = ctx.enter_context(nc.Block())

        @block.sync
        def _(sp):
            def ld(dst, src):
                sp.dma_start(dst, src).then_inc(done, 16)

            done = d_w

            sp.dma_start(wr[:, :, :], wrd.rearrange("(e p) n -> p e n", e=2)).then_inc(d_tl, 16)
            ld(ident[:, :], a["ident"])
            ld(pos[:, :, :], a["pos"])
            ld(pjb[:, :], a["proj_b"])
            ld(brow[:, 1:3, :], a["brow"])
            ld(brow2[:, 0, :], a["b2"])
            for k in range(NT // 2):
                for i in range(2):
                    for dst, src in ((xst, xs), (embt, emb)):
                        width = src.shape[1]
                        n = 2 - (k == NT // 2 - 1 and i == 1)
                        sp.dma_start(dst[64 * i:64 * i + 64, 2 * k:2 * k + n, :],
                                     bass.AP(tensor=src.tensor, offset=(4 * k + i) * TI * width,
                                             ap=[[width, 64], [2 * TI * width, n], [1, width]])).then_inc(d_x[k], 16)
            for dst, src in ((xst, xs), (embt, emb)):
                sp.dma_start(dst[64:64 + TI, NT - 1, :], src[NPAT - TI:NPAT, :]).then_inc(d_x[NT // 2 - 1], 16)
                sp.dma_start(dst[64 + TI:128, NT - 1, :], src[0:64 - TI, :]).then_inc(d_x[NT // 2 - 1], 16)
            done = d_wb
            ld(hmask[:, :], a["hmask"])
            ld(causal[:, :], a["causal"])
            ld(wqkv[0][:, :, :], a["wqkv1"].rearrange("(k p) n -> p k n", k=2))
            ld(wqkv[1][:, :, :], a["wqkv2"].rearrange("(k p) n -> p k n", k=2))
            ld(wpr[0][:, :, :], a["wproj1"].rearrange("(k p) n -> p k n", k=2))
            ld(wpr[1][:, :, :], a["wproj2"].rearrange("(k p) n -> p k n", k=2))
            ld(qb[:, :], a["qkb"])
            ld(vb[:, :], a["vb"])
            ld(lnp[:, :, :], a["lnp"])
            ld(w1[:, :, :], a["w1"].rearrange("(k p) n -> p k n", k=2))
            ld(b1[:, :], a["b1"])
            ld(w2[:, :, :], a["w2"].rearrange("(k p) n -> p k n", p=128))
            ld(gw[:, :], a["gw"])
            for t in range(NT):
                sp.wait_ge(m_c, t + 1)
                for i in range(2):
                    sp.dma_start(out[2 * t + i], h[64 * i:64 * i + TI, t, :]).then_inc(d_out, 16)
            sp.wait_ge(d_out, 16 * 2 * NT)

        NW, NWB = 5, 13

        @block.gpsimd
        def _(pool):
            nc.gpsimd.memset(khalf[:, :], -0.5).then_inc(zer, 1)
            nc.gpsimd.memset(ones[:, :], 1.0).then_inc(zer, 1)
            for i in range(2):
                nc.gpsimd.memset(pr[i][:, :, :], 0.0).then_inc(zer, 1)
            pool.wait_ge(zer, 4)

            nc.gpsimd.memset(vt[:, :, :, :], 0.0).then_inc(vz, 1)

            def rstd(n, t):
                pool.wait_ge(ln_v[n], t + 1)
                nc.gpsimd.tensor_tensor(rs[:, t:t + 1], ve[:, t:t + 1], khalf[:, 0:1], ALU.pow).then_inc(ln_r[n], 1)

            def kblocks(at, t):
                n = at * NT + t
                pool.wait_ge(qk_c, 8 * at + 8)
                if n >= 2:
                    pool.wait_ge(sc_p, n - 1)
                for i in range(2):
                    for k in range(2):
                        src = qkT[:, 2 + k, t * 128 + 64 * i:t * 128 + 64 * i + TI]
                        ins = nc.gpsimd.tensor_tensor(
                            kb[n % 2][:, i, k, :, :], src.unsqueeze(1).broadcast_to((HC, HT, TI)),
                            hmask[:, :].unsqueeze(2).broadcast_to((HC, HT, TI)), ALU.mult)
                ins.then_inc(kb_r, 1)

            for t in range(NT):
                rstd(0, t)
            for at in range(2):
                for t in range(3):
                    kblocks(at, t)
                for t in range(NT + 2):
                    if t + 3 < NT:
                        kblocks(at, t + 3)
                    if 1 <= t <= NT:
                        rstd(1 if at == 0 else 3, t - 1)
                    if at == 0 and t >= 2:
                        rstd(2, t - 2)

        @block.scalar
        def _(act):
            act.wait_ge(d_w, 16 * NW)

            def copy(dst, src, done, **kw):
                nc.scalar.activation(dst, src, ACT.Identity if kw else ACT.Copy, **kw).then_inc(done, 1)

            for k in range(3):
                act.wait_ge(wrt_p, k + 1)
                for j in range(2):
                    copy(wrT[:, 2 * k + j, :], bank[k][:, j * E:(j + 1) * E], wrt_c)
            for t in range(NT):
                for k in range(2):
                    act.wait_ge(xt_p, 2 * t + k + 1)
                    n = (4, 2)[k]
                    if t >= 2 and k == 0:
                        act.wait_ge(tk_p, t - 1)
                    copy(xsT[t % 2][:, 4 * k:4 * k + n, :], bank[2 * (t % 2) + k][:, 0:n * 128].rearrange("p (a b) -> p a b", b=128), xt_c)

            act.wait_ge(d_wb, 16 * NWB)

            def transposed(n, g=None):
                for t in range(NT):
                    act.wait_ge(ln_tp, n * NT + t + 1)
                    for k in range(2):
                        kw = {}
                        if g is not None:
                            c = g + (0 if t < NT // 2 else 2)
                            kw = dict(scale=lnp[:, k, c:c + 1], bias=lnp[:, k, c + 1:c + 2])
                        copy(xT[:, k, t * 128:(t + 1) * 128], bank[t % 4][0:HC, k * 128:(k + 1) * 128], ln_tc, **kw)

            def attention(at):
                for m in range(4):
                    for hf in range(2):
                        n = 2 * m + hf
                        act.wait_ge(qk_p, 8 * at + n + 1)
                        kw = dict(bias=qb[:, m:m + 1], scale=1.0) if at == 0 else {}
                        copy(qkT[:, m, 512 * hf:512 * hf + 512], bank[4 + n % 4][0:HC, :], qk_c, **kw)
                for i in range(NT):
                    act.wait_ge(v_p, NT * at + i + 1)
                    src = bank[i % 4][:, 0:2 * E].rearrange("p (a j n) -> p a j n", a=2, j=HT)
                    copy(vt[0:64, 2 * i:2 * i + 2, :, 0:HS], src[0:64, :, :, 0:HS], v_c)
                    for k in range(2):
                        copy(vt[64:128, 2 * i + k, :, HS:2 * HS], src[64:128, 1 - k, :, HS:2 * HS], v_c)

                def exp(t):
                    n = at * NT + t
                    act.wait_ge(sc_r, n + 1)
                    nc.scalar.activation(pr[n % 2][:, :, 0:TI], pr[n % 2][:, :, 0:TI], ACT.Exp).then_inc(ex, 1)

                exp(0)
                exp(1)
                for t in range(NT + 1):
                    n = at * NT + t
                    if t < NT:
                        for k in range(2):
                            act.wait_ge(pt_p, 2 * n + k + 1)
                            m = (4, 2)[k]
                            copy(pT[:, 4 * k:4 * k + m, :], bank[4 + k][:, 0:m * 128].rearrange("p (a b) -> p a b", a=m), pt_c)
                    if t >= 1:
                        act.wait_ge(yt_p, n)
                        copy(yT[:, :, :], bank[7][0:HC, 0:256].rearrange("p (a b) -> p a b", a=2), yt_c)
                    if t + 2 < NT:
                        exp(t + 2)

            act.wait_ge(vz, 1)
            transposed(0)
            attention(0)
            transposed(1, 0)
            attention(1)
            transposed(2, 4)
            n = 0
            for v in range(4):
                for j in range(6):
                    act.wait_ge(h_p, n + 1)
                    if v >= 2:
                        act.wait_ge(m_p, (0, 0, 4, 8)[v])
                    nc.scalar.activation(hid[v % 2][:, j, :], bank[n % 4][:, :], ACT.Gelu, bias=b1[:, j:j + 1],
                                         scale=1.0).then_inc(h_c, 1)
                    n += 1

        @block.tensor
        def _(pe):
            mm = nc.tensor.matmul
            pe.wait_ge(d_w, 16 * NW)
            pe.wait_ge(zer, 4)
            pe.wait_ge(d_tl, 16)
            for k in range(3):
                for j in range(2):
                    for e in range(2):
                        last = nc.tensor.transpose(bank[k][:, j * E + e * HC:j * E + (e + 1) * HC],
                                                   wr[:, e, (2 * k + j) * 128:(2 * k + j + 1) * 128], ident[0:HC, 0:HC])
                last.then_inc(wrt_p, 1)
            for e in range(2):
                last = nc.tensor.transpose(bank[3][0:1, e * HC:(e + 1) * HC], wr[:, e, C * P * P:], ident[0:HC, 0:HC])
            last.then_inc(wrt_p, 1)
            pe.wait_ge(wrt_c, 6)
            pe.wait_ge(wprep, 1)

            def xt(t):
                if t % 2 == 0:
                    pe.wait_ge(d_x[t // 2], 64 + 64 * (t == NT - 2))
                for k in range(2):
                    if t >= 2:
                        pe.wait_ge(xt_c, 2 * (t - 2) + k + 1)
                    for j in range((4, 2)[k]):
                        m = 4 * k + j
                        last = nc.tensor.transpose(bank[2 * (t % 2) + k][:, j * 128:(j + 1) * 128],
                                                   xst[:, t, m * 128:(m + 1) * 128], ident[:, :])
                    last.then_inc(xt_p, 1)

            xt(0)
            for t in range(NT):
                if t + 1 < NT:
                    xt(t + 1)
                pe.wait_ge(xt_c, 2 * t + 2)
                if t >= 4:
                    pe.wait_ge(tk_c, t - 3)
                o = bank[4 + t % 4][:, 0:E]
                mm(o, ones[:, :], brow[:, 0, :], start=True, stop=False)
                for m in range(6):
                    last = mm(o, xsT[t % 2][:, m, :], wrT[:, m, :], start=False, stop=(m == 5))
                last.then_inc(tk_p, 1)

            def transposed(n, m):
                for t in range(NT):
                    pe.wait_ge(ln_x[m], t + 1)
                    if t >= 4:
                        pe.wait_ge(ln_tc, 2 * (n * NT + t - 4) + 2)
                    for k in range(2):
                        last = nc.tensor.transpose(bank[t % 4][0:HC, k * 128:(k + 1) * 128],
                                                   xn[:, t, k * HC:(k + 1) * HC], ident[:, :])
                    last.then_inc(ln_tp, 1)

            def attention(at, n_tc):
                w = wqkv[at]
                pe.wait_ge(ln_tc, n_tc)
                for m in range(4):
                    for hf in range(2):
                        n = 2 * m + hf
                        if n >= 4:
                            pe.wait_ge(qk_c, 8 * at + n - 3)
                        for k in range(2):
                            last = mm(bank[4 + n % 4][0:HC, :], w[:, k, m * HC:(m + 1) * HC],
                                      xT[:, k, 512 * hf:512 * hf + 512], start=(k == 0), stop=(k == 1))
                        last.then_inc(qk_p, 1)
                for i in range(NT):
                    if i >= 4:
                        pe.wait_ge(v_c, 3 * (NT * at + i - 3))
                    if i == 0:
                        pe.wait_ge(xch, at + 1)
                    for m, x in enumerate((xT, xTs)):
                        for k in range(2):
                            last = mm(bank[i % 4][:, m * E:(m + 1) * E], x[:, k, i * 128:(i + 1) * 128],
                                      w[:, k, 2 * E:3 * E], start=(k == 0), stop=(k == 1))
                    last.then_inc(v_p, 1)

                def scores(t):
                    n = at * NT + t
                    pe.wait_ge(kb_r, n + 1)
                    if n >= 2:
                        pe.wait_ge(sc_r, n - 1)
                    for k in range(2):
                        for i in range(2):
                            last = mm(bank[2 * (n % 2) + k][64 * i:64 * i + 64, 0:HT * TI],
                                      qkT[:, k, t * 128 + 64 * i:t * 128 + 64 * i + 64],
                                      kb[n % 2][:, i, k, :, :].rearrange("p a b -> p (a b)"), start=True, stop=True)
                    last.then_inc(sc_p, 1)

                pe.wait_ge(qk_c, 8 * at + 8)
                pe.wait_ge(v_c, 3 * NT * (at + 1))
                scores(0)
                scores(1)
                for t in range(NT + 1):
                    n = at * NT + t
                    if t < NT:
                        pe.wait_ge(ex, n + 1)
                        for j in range(HT):
                            last = nc.tensor.transpose(bank[4 + j // 4][:, (j % 4) * 128:(j % 4 + 1) * 128],
                                                       pr[n % 2][:, 2 * j:2 * j + 2, :].rearrange("p a b -> p (a b)"),
                                                       ident[:, :])
                            if j in (3, 5):
                                last.then_inc(pt_p, 1)
                    if t >= 1:
                        pe.wait_ge(y_c, n)
                        if n >= 2:
                            pe.wait_ge(o_c, n - 1)
                        for k in range(2):
                            last = nc.tensor.transpose(bank[7][0:HC, k * 128:(k + 1) * 128], y[:, k * HC:(k + 1) * HC],
                                                       ident[:, :])
                        last.then_inc(yt_p, 1)
                    if t + 2 < NT:
                        scores(t + 2)
                    if t < NT:
                        for j in range(HT):
                            if j % 4 == 0:
                                pe.wait_ge(pt_c, 2 * n + j // 4 + 1)
                            for i in range(2):
                                last = mm(bank[6][64 * i:64 * i + 64, j * 2 * HS:(j + 1) * 2 * HS],
                                          pT[:, j, 64 * i:64 * i + 64], vt[:, 2 * t + i, j, :], start=True, stop=True)
                        last.then_inc(y_p, 1)
                    if t >= 1:
                        pe.wait_ge(yt_c, n)
                        small = at == 1 and t - 1 >= NT // 2
                        wp = wpr[at + small]
                        o = bank[7][:, 256:256 + E]
                        mm(o, ones[:, :], brow[:, 1 + at + small, :], start=True, stop=False)
                        for k in range(2):
                            last = mm(o, yT[:, k, :], wp[:, k, :], start=False, stop=(k == 1))
                        last.then_inc(o_p, 1)

            pe.wait_ge(d_wb, 16 * NWB)
            pe.wait_ge(tk_c, NT)
            for k in range(2):
                last = mm(bank[7][0:1, 0:E], vb[:, k:k + 1], wpr[0][:, k, :], start=(k == 0), stop=(k == 1))
            last.then_inc(vbp, 1)
            transposed(0, 0)
            pe.wait_ge(vbd, 1)
            attention(0, 2 * NT)
            transposed(1, 2)
            pe.wait_ge(prp, 1)
            attention(1, 4 * NT)
            transposed(2, 3)
            pe.wait_ge(ln_tc, 6 * NT)
            keep = (E, E, E // 2, E // 3)

            def hidden(v):
                for j in range(6):
                    n = 6 * v + j
                    if n >= 4:
                        pe.wait_ge(h_c, n - 3)
                    ks = [(k, min(HC, keep[v] - HC * k)) for k in range(2) if keep[v] > HC * k]
                    for x, (k, c) in enumerate(ks):
                        last = mm(bank[n % 4][:, :], w1[0:c, k, j * 128:(j + 1) * 128],
                                  xT[0:c, k, 512 * (v > 0):512 * (v > 0) + 512], start=(x == 0), stop=(x == len(ks) - 1))
                    last.then_inc(h_p, 1)

            def second(v):
                pe.wait_ge(h_c, 6 * v + 6)
                w = keep[v]
                for t in range(4):
                    o = bank[4 + t]
                    if v == 1:
                        pe.wait_ge(m_c, t + 1)
                    if v <= 1:
                        mm(o[:, 0:E], ones[:, :], brow2[:, v, :], start=True, stop=False, skip_group_check=True)
                    for j in range(6):
                        rhs = w2[:, j, :] if v == 0 else w2v[:, v - 1, j, 0:w]
                        last = mm(o[:, 0:w], hid[v % 2][:, j, t * 128:(t + 1) * 128], rhs, start=False,
                                  stop=(j == 5), skip_group_check=True)
                    last.then_inc(m_p, 1)

            hidden(0)
            for v in range(4):
                if v < 3:
                    hidden(v + 1)
                second(v)

        @block.vector
        def _(dve):
            v = nc.vector
            count = [0]

            def link(ins):
                count[0] += 1
                ins.then_inc(dch, 1)
                dve.wait_ge(dch, count[0])

            def exchange(at):
                dve.wait_ge(ln_tc, 2 * NT * (at + 1))
                a4, b4 = (t[:, :, :].rearrange("p k (t i n) -> p (k t) i n", i=2, n=64) for t in (xTs, xT))
                for i in range(2):
                    ins = v.tensor_copy(a4[:, :, i, :], b4[:, :, 1 - i, :])
                ins.then_inc(xch, 1)

            def variance(n, t, x):
                link(v.bn_stats(st6[:, t, :], x[:, t, :]))
                link(v.bn_aggr(mv[:, t, :], st6[:, t, :]))
                v.tensor_scalar(ve[:, t:t + 1], mv[:, t, 1:2], EPS, None, ALU.add).then_inc(ln_v[n], 1)

            def normed(n, t, x, dst):
                dve.wait_ge(ln_r[n], t + 1)
                v.tensor_scalar(dst[:, t, :], x[:, t, :], mv[:, t, 0:1], rs[:, t:t + 1], ALU.subtract,
                                ALU.mult).then_inc(ln_x[n], 1)

            dve.wait_ge(d_w, 16 * NW)
            dve.wait_ge(wrt_p, 4)
            v.tensor_tensor(brow[:, 0, :], bank[3][0:1, 0:E], pjb[:, :], ALU.add).then_inc(wprep, 1)

            def token(t):
                dve.wait_ge(tk_p, t + 1)
                v.tensor_tensor(h[:, t, :], bank[4 + t % 4][:, 0:E], embt[:, t, :], ALU.add).then_inc(tk_c, 1)
                dve.wait_ge(tk_c, t + 1)
                variance(0, t, h)
                if t >= 1:
                    normed(0, t - 1, h, xn)

            dve.wait_ge(zer, 4)
            for k in range(NT // 2):
                dve.wait_ge(d_x[k], 64 + 64 * (k == NT // 2 - 1))
                tiles = embt[:, 2 * k:2 * k + 2, :]
                for m in range(2):
                    link(v.tensor_tensor(tiles, tiles, pos[:, m, :].unsqueeze(1).broadcast_to((128, 2, E)), ALU.add))
                for t in (2 * k, 2 * k + 1):
                    token(t)
            normed(0, NT - 1, h, xn)
            dve.wait_ge(d_wb, 16 * NWB)
            dve.wait_ge(vbp, 1)
            v.tensor_tensor(brow[:, 1, :], brow[:, 1, :], bank[7][0:1, 0:E], ALU.add).then_inc(vbd, 1)
            exchange(0)
            for i in range(3):
                v.tensor_scalar(w2v[:, i, :, :], w2[:, :, :], gw[:, i:i + 1], None, ALU.mult)
            link(v.memset(mrow[:, :], 0.0))
            for i, c in enumerate((E, E // 2, E // 3)):
                link(v.tensor_scalar(mrow[:, 0:c], mrow[:, 0:c], gw[0:1, i:i + 1], None, ALU.add))
            link(v.tensor_tensor(brow[:, 3, :], brow[:, 2, :], mrow[:, :], ALU.mult))
            link(v.tensor_tensor(brow2[:, 1, :], brow2[:, 0, :], mrow[:, :], ALU.mult))
            link(v.tensor_scalar(wpr[2][:, :, :], wpr[1][:, :, :], gw[0:HC, 0:1], None, ALU.mult))
            for i, c in ((1, HC), (2, E // 3)):
                link(v.scalar_tensor_tensor(wpr[2][0:c, 0, 0:c], wpr[1][0:c, 0, 0:c], gw[0:c, i:i + 1],
                                            wpr[2][0:c, 0, 0:c], ALU.mult, ALU.add))
            v.sem_inc(prp, 1)

            def attention(at, x):
                def soft(t):
                    n = at * NT + t
                    dve.wait_ge(sc_p, n + 1)
                    if n >= 2:
                        dve.wait_ge(pt_p, 2 * (n - 1))
                    p, m = pr[n % 2], mx[n % 2]
                    src = [bank[2 * (n % 2) + k][:, 0:HT * TI].rearrange("p (a b) -> p a b", a=HT) for k in range(2)]
                    heads = [slice(HT * k, HT * k + HT) for k in range(2)]
                    if at == 0:
                        for k in range(2):
                            ins = v.tensor_tensor(p[:, heads[k], 0:TI], src[k],
                                                  causal[:, :].unsqueeze(1).broadcast_to((128, HT, TI)), ALU.add)
                        link(ins)
                        src = [p[:, heads[k], 0:TI] for k in range(2)]
                    for k in range(2):
                        ins = v.tensor_reduce(m[:, heads[k]], src[k], AX.X, ALU.max)
                    link(ins)
                    for k in range(2):
                        ins = v.tensor_tensor(p[:, heads[k], 0:TI], src[k],
                                              m[:, heads[k]].unsqueeze(2).broadcast_to((128, HT, TI)), ALU.subtract)
                    ins.then_inc(sc_r, 1)

                soft(0)
                soft(1)
                for t in range(NT + 1):
                    n = at * NT + t
                    if t < NT:
                        dve.wait_ge(ex, n + 1)
                        link(v.tensor_reduce(sm[n % 2][:, :], pr[n % 2][:, :, 0:TI], AX.X, ALU.add))
                        v.reciprocal(ri[n % 2][:, :], sm[n % 2][:, :]).then_inc(dch, 1)
                        count[0] += 1
                    if t + 2 < NT:
                        soft(t + 2)
                    if t < NT:
                        dve.wait_ge(y_p, n + 1)
                        dve.wait_ge(dch, count[0])
                        v.tensor_tensor(y[:, :].rearrange("p (a b) -> p a b", a=NH),
                                        bank[6][:, 0:E].rearrange("p (a b) -> p a b", a=NH),
                                        ri[n % 2][:, :].unsqueeze(2).broadcast_to((128, NH, HS)), ALU.mult).then_inc(y_c, 1)
                    if t >= 1:
                        dve.wait_ge(o_p, n)
                        v.tensor_tensor(x[:, t - 1, :], x[:, t - 1, :], bank[7][:, 256:256 + E], ALU.add).then_inc(o_c, 1)
                        dve.wait_ge(o_c, n)
                        norms(at, t - 1)

            def norms(at, t):
                if at == 0:
                    if t < NT:
                        variance(1, t, h)
                    if 1 <= t <= NT:
                        normed(1, t - 1, h, x2)
                        dve.wait_ge(ln_x[1], t)
                        variance(2, t - 1, x2)
                    if t >= 2:
                        normed(2, t - 2, x2, xn)
                else:
                    if t < NT:
                        variance(3, t, x2)
                    if 1 <= t <= NT:
                        normed(3, t - 1, x2, xn)
                        ins = v.tensor_tensor(h[:, t - 1, :], h[:, t - 1, :], x2[:, t - 1, :], ALU.add)
                        if t == NT:
                            link(ins)

            attention(0, h)
            norms(0, NT)
            norms(0, NT + 1)
            exchange(1)
            attention(1, x2)
            norms(1, NT)
            for half in range(2):
                for t in range(4):
                    dve.wait_ge(m_p, t + 1 if half == 0 else 12 + t + 1)
                    n = 4 * half + t
                    v.tensor_tensor(h[:, n, :], h[:, n, :], bank[4 + t][:, 0:E], ALU.add).then_inc(m_c, 1)


def build_program(nc, a, out):
    emb = nc.dram_tensor("scratch_emb", (NPAT, E), F32).ap()
    xs = nc.dram_tensor("scratch_x", (NPAT, C * P * P), F32).ap()
    ts = nc.dram_tensor("scratch_fold", (E, TR, SL * P), F32).ap()
    wrd = nc.dram_tensor("scratch_residual", (E, C * P * P + 1), F32).ap()
    build_front(nc, a, emb, xs, ts, wrd)
    build_tail(nc, a, emb, xs, wrd, out)


def layout(inp):
    o = {}
    tokp = {k[7:]: v for k, v in inp.items() if k.startswith("L0_tok_")}
    o["x"] = inp["x"].reshape(B, C, HP, P, HP, P).transpose(1, 0, 2, 4, 3, 5).reshape(C, ROWS, HP, P * P)
    names = ("conv1_b", "gn1_g", "gn1_b", "rconv1_b", "gn2_g", "gn2_b", "rconv2_b")
    o["params"] = np.stack([np.concatenate([tokp[n], tokp[n]]) for n in names], 1)
    r1 = tokp["rconv1_w"].transpose(1, 2, 3, 0)
    r2 = tokp["rconv2_w"].transpose(0, 2, 3, 1)
    rb, fb = np.zeros((2, CH, 2, 3, 2, CH), r1.dtype), np.zeros((2, CH, 2, 3, 2, CH), r1.dtype)
    for slot, hin, hout, ky in ((0, 0, 1, 0), (0, 1, 0, 0), (0, 1, 1, 1), (1, 0, 0, 1), (1, 0, 1, 2), (1, 1, 0, 2)):
        rb[hin, :, slot, :, hout] = r1[:, ky]
        fb[hin, :, slot, :, hout] = r2[:, 2 - ky, ::-1]
    o["rbands"], o["fbands"] = rb.reshape(128, 768), fb.reshape(128, 768)
    w1 = tokp["conv1_w"]
    tb = np.zeros((2, CH, TR), w1.dtype)
    for half in range(2):
        tb[half, :, 27 * half:27 * half + 27] = w1.reshape(CH, 27)
    o["tband"] = tb.reshape(128, TR)
    wb = np.zeros((KC, 2, CH), w1.dtype)
    for kx in range(3):
        for c in range(C):
            for dy in range(4):
                par, up = dy % 2, dy // 2
                rows = [kx * 24 + (6 * k + 2 * c + par) * 2 + up for k in range(2)] + [KA + kx * 12 + (2 * c + par) * 2 + up]
                for half in range(2):
                    if 0 <= dy - half <= 2:
                        wb[rows, half] = w1[:, c, dy - half, kx]
    o["w1band"] = wb.reshape(KC, 128)
    i = (np.arange(128) % CH) // 2
    o["grp"] = ((i[:, None] == i[None, :]) / 8.0).astype(np.float32)
    pw = np.zeros((2, CH, E, SL, P), tokp["proj_w"].dtype)
    w = tokp["proj_w"].transpose(1, 0, 2, 3)
    pw[0, :, :, 1:9], pw[1, :, :, 0:8] = w[:, :, 1::2], w[:, :, 0::2]
    o["proj"] = pw.reshape(128, E * DENSE)

    o["ident"] = np.eye(128, dtype=np.float32)
    o["hmask"] = ((np.arange(HC)[:, None] // HS == np.arange(HT)[None]) * HS ** -0.5).astype(np.float32)
    cm = np.zeros((2, 64, TI), np.float32)
    cm[:, :TI] = np.where(np.tril(np.ones((TI, TI), bool)), 0.0, LOWEST)
    o["causal"] = cm.reshape(128, TI)
    vocab = tokp["row_emb"].shape[0]
    at = []
    for k in range(HP):
        low = int(np.float32(k) / np.float32(HP) * np.float32(vocab))
        high = int(np.float32(k + 1) / np.float32(HP) * np.float32(vocab))
        at.append((low + high) // 2)
    pos = np.zeros((2, 64, 2, E), tokp["row_emb"].dtype)
    for r in range(HP):
        for c in range(HP):
            pos[:, r * HP + c, 0], pos[:, r * HP + c, 1] = tokp["row_emb"][at[r]], tokp["col_emb"][at[c]]
    o["pos"] = pos.reshape(128, 2, E)
    o["proj_b"] = tokp["proj_b"][None]
    o["wqkv1"], o["wproj1"] = inp["L0_attn_Wqkv"], inp["L0_attn_Wproj"]
    o["qkb"] = inp["L0_attn_bqkv"][:2 * E].reshape(4, HC).T
    o["vb"] = inp["L0_attn_bqkv"][2 * E:].reshape(2, HC).T
    f = {k[7:]: v for k, v in inp.items() if k.startswith("L0_ffn_")}
    o["wqkv2"], o["wproj2"] = f["w_qkv"], f["w_proj"]
    ln = [f[k] for k in ("n1l_g", "n1l_b", "n1s_g", "n1s_b", "n2l_g", "n2l_b", "n2s_g", "n2s_b")]
    o["lnp"] = np.stack(ln, 1).reshape(2, HC, 8).transpose(1, 0, 2)
    o["w1"], o["w2"] = f["w_fc1"], f["w_fc2"]
    o["b1"] = f["b_fc1"].reshape(6, 128).T
    o["b2"] = f["b_fc2"][None]
    o["gw"] = np.tile(f["gumbel_weights"], (128, 1))
    o["brow"] = np.stack([inp["L0_attn_bproj"], f["b_proj"]])[None]
    return o


def kernel(**inputs):
    import numpy as _np
    import concourse.bacc as _bacc
    from concourse.bass_utils import run_bass_kernel_spmd as _run

    arr = layout({k: _np.asarray(v) for k, v in inputs.items()})
    nc = _bacc.Bacc("TRN2", target_bir_lowering=False, num_devices=1)
    arrays, a = {}, {}
    for name, v in arr.items():
        v = _np.ascontiguousarray(v)
        arrays[f"in_{name}"] = v
        a[name] = nc.dram_tensor(f"in_{name}", v.shape, mybir.dt.from_np(v.dtype), kind="ExternalInput").ap()
    out = nc.dram_tensor("out_tokens", (B, TI, E), F32, kind="ExternalOutput").ap()
    build_program(nc, a, out)
    r = _run(nc, [arrays], core_ids=[0])
    return r.results[0]["out_tokens"]
```
